# Optimizing a Trainium2 kernel written in Bass

```python
import numpy as np
import jax
import jax.numpy as jnp

def _softmax(x, axis=-1):
    return jax.nn.softmax(x, axis=axis)

def _gelu(x):
    return jax.nn.gelu(x, approximate=True)

def _silu(x):
    return jax.nn.silu(x)

def _sigmoid(x):
    return jax.nn.sigmoid(x)

def _layernorm(x, axis=-1, eps=1e-05):
    m = jnp.mean(x, axis=axis, keepdims=True)
    v = jnp.var(x, axis=axis, keepdims=True)
    return (x - m) / jnp.sqrt(v + eps)

def _scatter_add(tgt, idx, src, axis=0):
    return tgt.at[idx].add(src)

def _segment_sum(src, seg, n):
    return jax.ops.segment_sum(src, seg, n)
kernel_name = 'mk_decoder_postln_d2_seqx_r4_a28262'

def setup_inputs(seed: int=0):
    np.random.seed(seed)
    _w = jnp.asarray

    def _rec_inputs():
        import jax
        import jax.numpy as jnp
        _rk = jax.random.key(seed)
        x = -0.0002928 + 1 * jax.random.normal(jax.random.fold_in(_rk, 1), (16, 256, 256), jnp.float32)
        _lenS = 256 - jax.random.randint(jax.random.fold_in(_rk, 7), (16,), 0, max(1, 256 // 4) + 1, jnp.int32)
        _lenS2 = 256 - jax.random.randint(jax.random.fold_in(_rk, 8), (16,), 0, max(1, 256 // 4) + 1, jnp.int32)
        _ctx_1024P = jax.random.normal(jax.random.fold_in(_rk, 11), (16, 16, 256), jnp.float32)
        _ctx_1024c = jax.random.dirichlet(jax.random.fold_in(_rk, 511), 0.3 * jnp.ones((16,), jnp.float32), (16, 256))
        _ctx_1024t = jnp.einsum('bsk,bkd->bsd', _ctx_1024c, _ctx_1024P)
        _ctx_1024t = _ctx_1024t * jax.lax.rsqrt(jnp.mean(jnp.square(_ctx_1024t)) + 1e-12) * 0.953939
        ctx_1024 = -1.39393e-06 + 0.999914 * (_ctx_1024t + 0.3 * jax.random.normal(jax.random.fold_in(_rk, 611), (16, 256, 256), jnp.float32))
        _validS = jnp.arange(256)[None, :] < _lenS[:, None]
        _validS2 = jnp.arange(256)[None, :] < _lenS2[:, None]
        _causal = jnp.tril(jnp.ones((256, 256), dtype=bool))
        mask_BxSxS2_if1 = jnp.where(jnp.ones((16, 256, 256), dtype=bool), 1, 0).astype(jnp.int32)
        return (x, ctx_1024, mask_BxSxS2_if1)
    x, ctx_1024, mask_BxSxS2_if1 = _rec_inputs()

    def _L0_attn_setup():
        import jax, jax.numpy as jnp
        import numpy as np
        DIM = 256
        D_STATE = 16
        EXPAND = 2
        D_CONV = 4
        D_INNER = DIM * EXPAND
        DT_RANK = (DIM + 15) // 16
        BATCH = 2
        SEQ = 256

        def _selective_scan(u, delta, A, B, C, D):
            dA = jnp.exp(jnp.einsum('bld,dn->lbdn', delta, A))
            dBu = jnp.einsum('bld,bln,bdl->lbdn', delta, B, u)
            Ct = jnp.transpose(C, (1, 0, 2))

            def step(carry, inp):
                a, bu, c = inp
                carry = a * carry + bu
                y = jnp.einsum('bdn,bn->bd', carry, c)
                return (carry, y)
            x0 = jnp.zeros(dA.shape[1:], dA.dtype)
            _, ys = jax.lax.scan(step, x0, (dA, dBu, Ct))
            y = jnp.transpose(ys, (1, 2, 0))
            return y + u * D[:, None]
        key = jax.random.key(seed)
        ks = jax.random.split(key, 8)
        s = 0.02
        A = jnp.broadcast_to(jnp.arange(1, D_STATE + 1, dtype=jnp.float32), (D_INNER, D_STATE))
        return {'x': jax.random.normal(ks[0], (BATCH, SEQ, DIM), jnp.float32), 'in_w': jax.random.normal(ks[1], (2 * D_INNER, DIM), jnp.float32) * s, 'conv_w': jax.random.normal(ks[2], (D_INNER, 1, D_CONV), jnp.float32) * s, 'conv_b': jnp.zeros((D_INNER,), jnp.float32), 'xproj_w': jax.random.normal(ks[3], (DT_RANK + 2 * D_STATE, D_INNER), jnp.float32) * s, 'dt_w': jax.random.normal(ks[4], (D_INNER, DT_RANK), jnp.float32) * s, 'dt_b': jax.random.normal(ks[5], (D_INNER,), jnp.float32) * s, 'A_log': jnp.log(A), 'D': jnp.ones((D_INNER,), jnp.float32), 'out_w': jax.random.normal(ks[6], (DIM, D_INNER), jnp.float32) * s}
    _L0_attn_all = _L0_attn_setup()
    _L0_attn_in = {k: v for k, v in _L0_attn_all.items() if k in ('in_w', 'conv_w', 'conv_b', 'xproj_w', 'dt_w', 'dt_b', 'A_log', 'D', 'out_w')}
    del _L0_attn_all

    def _L0_xattn_setup():
        import jax, jax.numpy as jnp
        import numpy as np
        H = 16
        D_MODEL = 256
        D_K = D_MODEL // H
        NEG = -1000000000.0

        def _split_heads(x):
            B, S, _ = x.shape
            return x.reshape(B, S, H, D_K).transpose(0, 2, 1, 3)
        key = jax.random.key(seed)
        ks = jax.random.split(key, 12)
        B, S = (2, 512)
        s = 1.0 / np.sqrt(D_MODEL)
        inp = {'query': jax.random.normal(ks[0], (B, S, D_MODEL), jnp.float32), 'key': jax.random.normal(ks[1], (B, S, D_MODEL), jnp.float32), 'value': jax.random.normal(ks[2], (B, S, D_MODEL), jnp.float32), 'mask': jnp.ones((B, S, S), jnp.int32), 'Wq': jax.random.normal(ks[3], (D_MODEL, D_MODEL), jnp.float32) * s, 'bq': jnp.zeros((D_MODEL,), jnp.float32), 'Wk': jax.random.normal(ks[4], (D_MODEL, D_MODEL), jnp.float32) * s, 'bk': jnp.zeros((D_MODEL,), jnp.float32), 'Wv': jax.random.normal(ks[5], (D_MODEL, D_MODEL), jnp.float32) * s, 'bv': jnp.zeros((D_MODEL,), jnp.float32), 'Wo': jax.random.normal(ks[6], (D_MODEL, D_MODEL), jnp.float32) * s, 'bo': jnp.zeros((D_MODEL,), jnp.float32)}
        return inp
    _L0_xattn_all = _L0_xattn_setup()
    _L0_xattn_in = {k: v for k, v in _L0_xattn_all.items() if k in ('Wq', 'bq', 'Wk', 'bk', 'Wv', 'bv', 'Wo', 'bo')}
    del _L0_xattn_all

    def _L0_ffn_setup():
        import jax, jax.numpy as jnp
        import numpy as np
        DIM = 256
        HID = 256
        N_ROUTED = 7
        N_SHARED = 1
        TOP_K = 2
        B, S = (4, 512)
        key = jax.random.key(seed)
        ks = jax.random.split(key, 8)
        sc = 0.02
        return {'x': jax.random.normal(ks[0], (B, S, DIM), jnp.float32), 'gate_w': jax.random.normal(ks[1], (N_ROUTED, DIM), jnp.float32) * sc, 'expert_bias': jnp.zeros((N_ROUTED,), jnp.float32), 'sw1': jax.random.normal(ks[2], (DIM, HID), jnp.float32) * sc, 'sb1': jnp.zeros((HID,), jnp.float32), 'sw2': jax.random.normal(ks[3], (HID, DIM), jnp.float32) * sc, 'sb2': jnp.zeros((DIM,), jnp.float32), 'rw1': jax.random.normal(ks[4], (N_ROUTED, DIM, HID), jnp.float32) * sc, 'rb1': jnp.zeros((N_ROUTED, HID), jnp.float32), 'rw2': jax.random.normal(ks[5], (N_ROUTED, HID, DIM), jnp.float32) * sc, 'rb2': jnp.zeros((N_ROUTED, DIM), jnp.float32)}
    _L0_ffn_all = _L0_ffn_setup()
    _L0_ffn_in = {k: v for k, v in _L0_ffn_all.items() if k in ('gate_w', 'expert_bias', 'sw1', 'sb1', 'sw2', 'sb2', 'rw1', 'rb1', 'rw2', 'rb2')}
    del _L0_ffn_all

    def _L1_attn_setup():
        import jax, jax.numpy as jnp
        import numpy as np
        D_MODEL, N_HEADS, N_KV, HEAD_DIM, D_LAT = (256, 8, 2, 128, 32)
        N_REP = N_HEADS // N_KV
        B, T = (2, 512)
        key = jax.random.key(seed)
        ks = jax.random.split(key, 8)
        s = lambda fan_in: 1.0 / np.sqrt(fan_in)
        return {'x': jax.random.normal(ks[0], (B, T, D_MODEL), jnp.float32), 'wq': jax.random.normal(ks[1], (D_MODEL, N_HEADS * HEAD_DIM), jnp.float32) * s(D_MODEL), 'wk_down': jax.random.normal(ks[2], (D_MODEL, N_KV * D_LAT), jnp.float32) * s(D_MODEL), 'wv_down': jax.random.normal(ks[3], (D_MODEL, N_KV * D_LAT), jnp.float32) * s(D_MODEL), 'wk_up': jax.random.normal(ks[4], (D_LAT, HEAD_DIM), jnp.float32) * s(D_LAT), 'wv_up': jax.random.normal(ks[5], (D_LAT, HEAD_DIM), jnp.float32) * s(D_LAT), 'wo': jax.random.normal(ks[6], (N_HEADS * HEAD_DIM, D_MODEL), jnp.float32) * s(N_HEADS * HEAD_DIM)}
    _L1_attn_all = _L1_attn_setup()
    _L1_attn_in = {k: v for k, v in _L1_attn_all.items() if k in ('wq', 'wk_down', 'wv_down', 'wk_up', 'wv_up', 'wo')}
    del _L1_attn_all

    def _L1_xattn_setup():
        import jax, jax.numpy as jnp
        import numpy as np
        N_HEADS = 16
        EMBED = 256
        HEAD_DIM = EMBED // N_HEADS
        key = jax.random.key(seed)
        ks = jax.random.split(key, 11)
        B, S, E = (2, 512, EMBED)
        s = 1.0 / np.sqrt(E)
        return {'q': jax.random.normal(ks[0], (B, S, E), jnp.float32), 'k': jax.random.normal(ks[1], (B, S, E), jnp.float32), 'v': jax.random.normal(ks[2], (B, S, E), jnp.float32), 'Wq': jax.random.normal(ks[3], (E, E), jnp.float32) * s, 'bq': jax.random.normal(ks[4], (E,), jnp.float32) * s, 'Wk': jax.random.normal(ks[5], (E, E), jnp.float32) * s, 'bk': jax.random.normal(ks[6], (E,), jnp.float32) * s, 'Wv': jax.random.normal(ks[7], (E, E), jnp.float32) * s, 'bv': jax.random.normal(ks[8], (E,), jnp.float32) * s, 'Wp': jax.random.normal(ks[9], (E, E), jnp.float32) * s, 'bp': jax.random.normal(ks[10], (E,), jnp.float32) * s}
    _L1_xattn_all = _L1_xattn_setup()
    _L1_xattn_in = {k: v for k, v in _L1_xattn_all.items() if k in ('Wq', 'bq', 'Wk', 'bk', 'Wv', 'bv', 'Wp', 'bp')}
    del _L1_xattn_all

    def _L1_ffn_setup():
        import jax, jax.numpy as jnp
        import numpy as np
        TOP_K = 2
        key = jax.random.key(seed)
        k1, k2, k3, k4 = jax.random.split(key, 4)
        B, T, D, F, E = (2, 256, 256, 512, 8)
        x = jax.random.normal(k1, (B, T, D), dtype=jnp.float32)
        Wg = jax.random.normal(k2, (D, E), dtype=jnp.float32) * 0.02
        W1 = jax.random.normal(k3, (E, D, F), dtype=jnp.float32) * 0.02
        W2 = jax.random.normal(k4, (E, F, D), dtype=jnp.float32) * 0.02
        return {'x': x, 'Wg': Wg, 'W1': W1, 'W2': W2}
    _L1_ffn_all = _L1_ffn_setup()
    _L1_ffn_in = {k: v for k, v in _L1_ffn_all.items() if k in ('Wg', 'W1', 'W2')}
    del _L1_ffn_all
    return {'x': x, 'ctx_1024': ctx_1024, 'mask_BxSxS2_if1': mask_BxSxS2_if1, 'L0_attn_in_w': _L0_attn_in['in_w'], 'L0_attn_conv_w': _L0_attn_in['conv_w'], 'L0_attn_conv_b': _L0_attn_in['conv_b'], 'L0_attn_xproj_w': _L0_attn_in['xproj_w'], 'L0_attn_dt_w': _L0_attn_in['dt_w'], 'L0_attn_dt_b': _L0_attn_in['dt_b'], 'L0_attn_A_log': _L0_attn_in['A_log'], 'L0_attn_D': _L0_attn_in['D'], 'L0_attn_out_w': _L0_attn_in['out_w'], 'L0_xattn_Wq': _L0_xattn_in['Wq'], 'L0_xattn_bq': _L0_xattn_in['bq'], 'L0_xattn_Wk': _L0_xattn_in['Wk'], 'L0_xattn_bk': _L0_xattn_in['bk'], 'L0_xattn_Wv': _L0_xattn_in['Wv'], 'L0_xattn_bv': _L0_xattn_in['bv'], 'L0_xattn_Wo': _L0_xattn_in['Wo'], 'L0_xattn_bo': _L0_xattn_in['bo'], 'L0_ffn_gate_w': _L0_ffn_in['gate_w'], 'L0_ffn_expert_bias': _L0_ffn_in['expert_bias'], 'L0_ffn_sw1': _L0_ffn_in['sw1'], 'L0_ffn_sb1': _L0_ffn_in['sb1'], 'L0_ffn_sw2': _L0_ffn_in['sw2'], 'L0_ffn_sb2': _L0_ffn_in['sb2'], 'L0_ffn_rw1': _L0_ffn_in['rw1'], 'L0_ffn_rb1': _L0_ffn_in['rb1'], 'L0_ffn_rw2': _L0_ffn_in['rw2'], 'L0_ffn_rb2': _L0_ffn_in['rb2'], 'L1_attn_wq': _L1_attn_in['wq'], 'L1_attn_wk_down': _L1_attn_in['wk_down'], 'L1_attn_wv_down': _L1_attn_in['wv_down'], 'L1_attn_wk_up': _L1_attn_in['wk_up'], 'L1_attn_wv_up': _L1_attn_in['wv_up'], 'L1_attn_wo': _L1_attn_in['wo'], 'L1_xattn_Wq': _L1_xattn_in['Wq'], 'L1_xattn_bq': _L1_xattn_in['bq'], 'L1_xattn_Wk': _L1_xattn_in['Wk'], 'L1_xattn_bk': _L1_xattn_in['bk'], 'L1_xattn_Wv': _L1_xattn_in['Wv'], 'L1_xattn_bv': _L1_xattn_in['bv'], 'L1_xattn_Wp': _L1_xattn_in['Wp'], 'L1_xattn_bp': _L1_xattn_in['bp'], 'L1_ffn_Wg': _L1_ffn_in['Wg'], 'L1_ffn_W1': _L1_ffn_in['W1'], 'L1_ffn_W2': _L1_ffn_in['W2']}

def reference(x, ctx_1024, mask_BxSxS2_if1, L0_attn_in_w, L0_attn_conv_w, L0_attn_conv_b, L0_attn_xproj_w, L0_attn_dt_w, L0_attn_dt_b, L0_attn_A_log, L0_attn_D, L0_attn_out_w, L0_xattn_Wq, L0_xattn_bq, L0_xattn_Wk, L0_xattn_bk, L0_xattn_Wv, L0_xattn_bv, L0_xattn_Wo, L0_xattn_bo, L0_ffn_gate_w, L0_ffn_expert_bias, L0_ffn_sw1, L0_ffn_sb1, L0_ffn_sw2, L0_ffn_sb2, L0_ffn_rw1, L0_ffn_rb1, L0_ffn_rw2, L0_ffn_rb2, L1_attn_wq, L1_attn_wk_down, L1_attn_wv_down, L1_attn_wk_up, L1_attn_wv_up, L1_attn_wo, L1_xattn_Wq, L1_xattn_bq, L1_xattn_Wk, L1_xattn_bk, L1_xattn_Wv, L1_xattn_bv, L1_xattn_Wp, L1_xattn_bp, L1_ffn_Wg, L1_ffn_W1, L1_ffn_W2):
    import jax
    import jax.numpy as jnp

    def _L0_attn_ref(x, in_w, conv_w, conv_b, xproj_w, dt_w, dt_b, A_log, D, out_w):
        import jax, jax.numpy as jnp
        import numpy as np
        DIM = 256
        D_STATE = 16
        EXPAND = 2
        D_CONV = 4
        D_INNER = DIM * EXPAND
        DT_RANK = (DIM + 15) // 16
        BATCH = 2
        SEQ = 256

        def _selective_scan(u, delta, A, B, C, D):
            dA = jnp.exp(jnp.einsum('bld,dn->lbdn', delta, A))
            dBu = jnp.einsum('bld,bln,bdl->lbdn', delta, B, u)
            Ct = jnp.transpose(C, (1, 0, 2))

            def step(carry, inp):
                a, bu, c = inp
                carry = a * carry + bu
                y = jnp.einsum('bdn,bn->bd', carry, c)
                return (carry, y)
            x0 = jnp.zeros(dA.shape[1:], dA.dtype)
            _, ys = jax.lax.scan(step, x0, (dA, dBu, Ct))
            y = jnp.transpose(ys, (1, 2, 0))
            return y + u * D[:, None]
        b, l, d = x.shape
        xr = x @ in_w.T
        xx, res = jnp.split(xr, 2, axis=-1)
        xx = jnp.transpose(xx, (0, 2, 1))
        xx = jax.lax.conv_general_dilated(xx, conv_w, window_strides=(1,), padding=[(D_CONV - 1, 0)], dimension_numbers=('NCH', 'OIH', 'NCH'), feature_group_count=D_INNER) + conv_b[None, :, None]
        xx = jax.nn.silu(xx)
        A = -jnp.exp(A_log)
        x_dbl = jnp.einsum('bdl,kd->blk', xx, xproj_w)
        delta, B, C = jnp.split(x_dbl, [DT_RANK, DT_RANK + D_STATE], axis=-1)
        delta = jax.nn.softplus(delta @ dt_w.T + dt_b)
        y = _selective_scan(xx, delta, A, B, C, D)
        y = y * jax.nn.silu(jnp.transpose(res, (0, 2, 1)))
        return jnp.transpose(y, (0, 2, 1)) @ out_w.T

    def _L0_xattn_ref(query, key, value, mask, Wq, bq, Wk, bk, Wv, bv, Wo, bo):
        import jax, jax.numpy as jnp
        import numpy as np
        H = 16
        D_MODEL = 256
        D_K = D_MODEL // H
        NEG = -1000000000.0

        def _split_heads(x):
            B, S, _ = x.shape
            return x.reshape(B, S, H, D_K).transpose(0, 2, 1, 3)
        q = _split_heads(query @ Wq.T + bq)
        k = _split_heads(key @ Wk.T + bk)
        v = _split_heads(value @ Wv.T + bv)
        scores = jnp.einsum('bhqd,bhkd->bhqk', q, k) / np.sqrt(D_K)
        scores = jnp.where(mask[:, None, :, :] == 0, NEG, scores)
        p_attn = jax.nn.log_softmax(scores, axis=-1)
        x = jnp.einsum('bhqk,bhkd->bhqd', p_attn, v)
        B, _, S, _ = x.shape
        x = x.transpose(0, 2, 1, 3).reshape(B, S, H * D_K)
        return x @ Wo.T + bo

    def _L0_ffn_ref(x, gate_w, expert_bias, sw1, sb1, sw2, sb2, rw1, rb1, rw2, rb2):
        import jax, jax.numpy as jnp
        import numpy as np
        DIM = 256
        HID = 256
        N_ROUTED = 7
        N_SHARED = 1
        TOP_K = 2
        B, S = (4, 512)
        b, s, d = x.shape
        xf = x.reshape(-1, d)
        sh = jax.nn.gelu(xf @ sw1 + sb1, approximate=False) @ sw2 + sb2
        sh = sh / N_SHARED
        logits = xf @ gate_w.T + jax.lax.stop_gradient(expert_bias)
        topv, topi = jax.lax.top_k(logits, TOP_K)
        w = jax.nn.softmax(topv, axis=-1)
        combine = jnp.sum(jax.nn.one_hot(topi, N_ROUTED, dtype=xf.dtype) * w[..., None], axis=1)
        h = jax.nn.gelu(jnp.einsum('td,edh->eth', xf, rw1) + rb1[:, None, :], approximate=False)
        out_e = jnp.einsum('eth,ehd->etd', h, rw2) + rb2[:, None, :]
        routed = jnp.einsum('te,etd->td', combine, out_e)
        return (sh + routed).reshape(b, s, d)

    def _L1_attn_ref(x, wq, wk_down, wv_down, wk_up, wv_up, wo):
        import jax, jax.numpy as jnp
        import numpy as np
        D_MODEL, N_HEADS, N_KV, HEAD_DIM, D_LAT = (256, 8, 2, 128, 32)
        N_REP = N_HEADS // N_KV
        B, T = (2, 512)
        Bq, Tq, _ = x.shape
        scale = HEAD_DIM ** (-0.5)
        q = (x @ wq).reshape(Bq, Tq, N_KV, N_REP, HEAD_DIM)
        k_lat = (x @ wk_down).reshape(Bq, Tq, N_KV, D_LAT)
        v_lat = (x @ wv_down).reshape(Bq, Tq, N_KV, D_LAT)
        k = jnp.einsum('bkhl,ld->bkhd', k_lat, wk_up)
        v = jnp.einsum('bkhl,ld->bkhd', v_lat, wv_up)
        scores = jnp.einsum('bqhrd,bkhd->bhrqk', q, k) * scale
        causal = jnp.tril(jnp.ones((Tq, Tq), dtype=bool))
        scores = jnp.where(causal, scores, jnp.finfo(scores.dtype).min)
        probs = jax.nn.softmax(scores, axis=-1)
        y = jnp.einsum('bhrqk,bkhd->bqhrd', probs, v)
        y = y.reshape(Bq, Tq, N_HEADS * HEAD_DIM)
        return y @ wo

    def _L1_xattn_ref(q, k, v, Wq, bq, Wk, bk, Wv, bv, Wp, bp):
        import jax, jax.numpy as jnp
        import numpy as np
        N_HEADS = 16
        EMBED = 256
        HEAD_DIM = EMBED // N_HEADS
        B, Sq, E = q.shape
        Skv = k.shape[1]
        qh = q @ Wq.T + bq
        kh = k @ Wk.T + bk
        vh = v @ Wv.T + bv
        qh = qh.reshape(B, N_HEADS, Sq, HEAD_DIM)
        kh = kh.reshape(B, N_HEADS, Skv, HEAD_DIM)
        vh = vh.reshape(B, N_HEADS, Skv, HEAD_DIM)
        scale = 1.0 / jnp.sqrt(jnp.float32(HEAD_DIM))
        scores = jnp.einsum('bhqd,bhkd->bhqk', qh, kh) * scale
        causal = jnp.triu(jnp.ones((Sq, Sq), bool), k=1)
        scores = jnp.where(causal, -jnp.inf, scores)
        attn = jax.nn.softmax(scores, axis=-1)
        out = jnp.einsum('bhqk,bhkd->bhqd', attn, vh)
        out = out.reshape(B, Sq, E)
        return out @ Wp.T + bp

    def _L1_ffn_ref(x, Wg, W1, W2):
        import jax, jax.numpy as jnp
        import numpy as np
        TOP_K = 2
        B, T, D = x.shape
        E = Wg.shape[-1]
        xt = x.reshape(B * T, D)
        logits = xt @ Wg
        probs = jax.nn.softmax(logits, axis=-1)
        topw, topi = jax.lax.top_k(probs, TOP_K)
        topw = topw / jnp.sum(topw, axis=-1, keepdims=True)
        combine = jnp.sum(jax.nn.one_hot(topi, E, dtype=xt.dtype) * topw[..., None], axis=1)
        h = jax.nn.relu(jnp.einsum('nd,edf->enf', xt, W1))
        y = jnp.einsum('enf,efd->end', h, W2)
        out = jnp.einsum('ne,end->nd', combine, y)
        return out.reshape(B, T, D)
    x = _layernorm(x + _L0_attn_ref(x, L0_attn_in_w, L0_attn_conv_w, L0_attn_conv_b, L0_attn_xproj_w, L0_attn_dt_w, L0_attn_dt_b, L0_attn_A_log, L0_attn_D, L0_attn_out_w), axis=-1)
    x = _layernorm(x + _L0_xattn_ref(x, ctx_1024, ctx_1024, mask_BxSxS2_if1, L0_xattn_Wq, L0_xattn_bq, L0_xattn_Wk, L0_xattn_bk, L0_xattn_Wv, L0_xattn_bv, L0_xattn_Wo, L0_xattn_bo), axis=-1)
    x = _layernorm(x + _L0_ffn_ref(x, L0_ffn_gate_w, L0_ffn_expert_bias, L0_ffn_sw1, L0_ffn_sb1, L0_ffn_sw2, L0_ffn_sb2, L0_ffn_rw1, L0_ffn_rb1, L0_ffn_rw2, L0_ffn_rb2), axis=-1)
    x = _layernorm(x + _L1_attn_ref(x, L1_attn_wq, L1_attn_wk_down, L1_attn_wv_down, L1_attn_wk_up, L1_attn_wv_up, L1_attn_wo), axis=-1)
    x = _layernorm(x + _L1_xattn_ref(x, ctx_1024, ctx_1024, L1_xattn_Wq, L1_xattn_bq, L1_xattn_Wk, L1_xattn_bk, L1_xattn_Wv, L1_xattn_bv, L1_xattn_Wp, L1_xattn_bp), axis=-1)
    x = _layernorm(x + _L1_ffn_ref(x, L1_ffn_Wg, L1_ffn_W1, L1_ffn_W2), axis=-1)
    return x

_drawn_inputs = setup_inputs


def setup_inputs(seed=0):
    import zlib

    import numpy as np

    out = dict(_drawn_inputs(seed))
    spreads = {'L0_attn_conv_b': (0.0, 0.8),
     'L0_attn_D': (1.0, 0.6),
     'L0_xattn_bq': (0.0, 0.757),
     'L0_xattn_bk': (0.0, 2.0),
     'L0_xattn_bv': (0.0, 0.1),
     'L0_xattn_bo': (0.0, 2.0),
     'L0_ffn_expert_bias': (0.0, 0.1),
     'L0_ffn_sb1': (0.0, 0.48),
     'L0_ffn_sb2': (0.0, 0.1),
     'L0_ffn_rb1': (0.0, 0.567),
     'L0_ffn_rb2': (0.0, 0.1)}
    factors = {'L0_attn_in_w': 8.0,
     'L0_attn_conv_w': 8.0,
     'L0_attn_xproj_w': 8.0,
     'L0_attn_dt_w': 8.0,
     'L0_attn_dt_b': 25.376,
     'L0_attn_A_log': 8.0,
     'L0_attn_out_w': 8.0,
     'L1_attn_wq': 8.0,
     'L1_attn_wk_down': 8.0,
     'L1_attn_wk_up': 8.0,
     'L1_xattn_bq': 3.751,
     'L1_xattn_bk': 3.606}
    for name, (base, spread) in spreads.items():
        noise = np.random.default_rng([zlib.crc32(name.encode()), seed]).standard_normal(out[name].shape)
        drawn = base * np.exp(spread * noise) if base else spread * noise
        out[name] = jnp.asarray(drawn.astype(out[name].dtype))
    for name, factor in factors.items():
        out[name] = (out[name] * factor).astype(out[name].dtype)
    return out
```

```python
from contextlib import ExitStack

import numpy as np
import concourse.bass as bass
from concourse import mybir

FP32 = mybir.dt.float32
BF16 = mybir.dt.bfloat16
I32 = mybir.dt.int32
U32 = mybir.dt.uint32
ALU = mybir.AluOpType
ACT = mybir.ActivationFunctionType
AX = mybir.AxisListType

P = 128
BATCH, T, D = 16, 256, 256
TT = T // P
FT = D // P
DI = 512
DT = DI // P
NS = 16
RANK = 16
TAPS = 4
H, HD = 16, 16
GH, GKV, LAT, GHD = 8, 2, 32, 128
E0, E1, HID1 = 7, 8, 512
EPS = 1e-5
NEG = -1e9
HIDE = -1e30
LOWEST = -3e38
PARTS_Q = (0, 0, 1, 1, 0, 2)
PARTS_K = (0, 1, 0, 1, 2, 0)


class Engine:

    def __init__(self, eng, name, new_sem):
        self.eng, self.name, self.new_sem = eng, name, new_sem
        self.sems, self.count, self.seen = {}, {}, {}

    def wait(self, after):
        for t in after:
            if t is None:
                continue
            sem, value, key = t
            if self.seen.get(key, 0) < value:
                self.eng.wait_ge(sem, value)
                self.seen[key] = value

    def step(self, stage, issue, after=()):
        self.wait(after)
        key = f"{self.name}_{stage}"
        if key not in self.sems:
            self.sems[key] = self.new_sem(key)
            self.count[key] = 0
        issue(self.eng).then_inc(self.sems[key], 1)
        self.count[key] += 1
        return self.sems[key], self.count[key], key

    def all_steps(self):
        return [(self.sems[k], self.count[k], k) for k in self.sems]


class Dma:

    def __init__(self, engine, name, new_sem, turns):
        self.engine, self.name = engine, name
        self.sems = [new_sem(f"dma_{name}{i}") for i in range(turns)]
        self.count = [0] * turns
        self.at = 0

    def send(self, pairs, after=()):
        self.engine.wait(after)
        i = self.at % len(self.sems)
        self.at += 1
        for out, in_ in pairs:
            self.engine.eng.dma_start(out, in_).then_inc(self.sems[i], 16)
            self.count[i] += 16
        return self.sems[i], self.count[i], f"{self.name}{i}"


class Bank:

    def __init__(self, tensor):
        self.t, self.free = tensor, None


def program(nc, a, out, scratch_q, scratch_o, scratch_v, scratch_x, scratch_xT):
    ctx = ExitStack()
    phase = ExitStack()
    with ctx:
        def keep(name, shape, dt=FP32):
            return ctx.enter_context(nc.sbuf_tensor(name, shape, dt))

        def sb(name, shape, dt=FP32):
            return phase.enter_context(nc.sbuf_tensor(name, shape, dt))

        def new_sem(name):
            return ctx.enter_context(nc.semaphore(name))

        pe = Engine(nc.tensor, "pe", new_sem)
        dve = Engine(nc.vector, "dve", new_sem)
        act = Engine(nc.scalar, "act", new_sem)
        pool = Engine(nc.gpsimd, "pool", new_sem)
        sp = Engine(nc.sync, "sp", new_sem)

        banks = [Bank(ctx.enter_context(nc.psum_tensor(f"bank{i}", [P, 512], FP32))) for i in range(8)]
        mamba_banks, rest_banks = banks[:4], banks[4:]

        stats = {s: (keep("stats" + s, [P, TT, 6]), keep("mv" + s, [P, TT, 2]), keep("rstd" + s, [P, TT]))
                 for s in ("m", "r")}
        eps = keep("eps", [P, 1])
        logits = keep("logits", [P, TT, 8])
        top = keep("top", [P, TT, 8])
        top_i = keep("top_i", [P, TT, 8], U32)
        top_f = keep("top_f", [P, TT, 2])
        wts = keep("wts", [P, TT, 4])
        comb = keep("comb", [P, TT, 8])
        comb2 = keep("comb2", [P, TT, 8])
        x_sum = keep("x_sum", [P, TT, D])
        iota = keep("iota", [P, 8])

        def weight(name, shape, view, dt=FP32, alloc=sb):
            t = alloc("w_" + name, shape, dt)
            return t, (t[tuple(slice(None) for _ in shape)], view)

        k_rows = lambda ap, k: ap.rearrange("(k p) n -> p k n", k=k)
        in_w, l1 = weight("in_w", [P, FT, 2 * DI], k_rows(a["in_wT"], FT))
        conv_w, l2 = weight("conv_w", [P, DT, TAPS], a["conv_w"].rearrange("(k p) n -> p k n", k=DT))
        vec = lambda name, k: a[name]
        conv_b, l3 = weight("conv_b", [P, DT], vec("conv_b", DT))
        xproj, l4 = weight("xproj", [P, DT, 2 * NS + RANK], k_rows(a["xprojT"], DT))
        dt_w, l5 = weight("dt_w", [RANK, DI], a["dt_wT"])
        dt_b, l6 = weight("dt_b", [P, DT], vec("dt_b", DT))
        A, l7 = weight("A_log", [P, DT, NS], k_rows(a["A_log"], DT))
        skip_w, l8 = weight("D", [P, DT], vec("D", DT))
        out_w, l9 = weight("out_w", [P, DT, D], k_rows(a["out_wT"], DT))
        ident, l10 = weight("ident", [P, P], a["ident"])
        
        consts = sb("consts", [P, 5 * P + 32], BF16)
        identb, causal, causalT, bcausal, bcausalT = (consts[:, i * P:(i + 1) * P] for i in range(5))
        sel1 = consts[0:96, 5 * P:]

        def sel(row):
            return sel1[:, row:row + 1].broadcast_to([96, P])


        xw, xloads = {}, []
        for layer in "01":
            for m in "qkvo":
                xw[layer + m], l = weight(f"x{layer}{m}", [P, FT, D], k_rows(a[f"W{m}{layer}T"], FT))
                xloads.append(l)
                if m in "qk":
                    xw[layer + "b" + m], l = weight(f"x{layer}b{m}", [P, FT], vec(f"b{m}{layer}", FT))
                else:
                    xw[layer + "b" + m], l = weight(f"x{layer}b{m}", [P, D],
                                                    a[f"b{m}{layer}"].partition_broadcast(P))
                xloads.append(l)
        head_block, l = weight("head_block", [H, D], a["head_block"])
        xloads.append(l)
        ones16 = sb("ones16", [P, H])
        onesb = sb("onesb", [P, P], BF16)

        E0A = E0 + 1
        w1_0, f1 = weight("w1_0", [P, E0A, FT, D], a["w1_0"].rearrange("e (k p) n -> p e k n", k=FT))
        w2_0, f2 = weight("w2_0", [P, E0A, FT, D], a["w2_0"].rearrange("e (k p) n -> p e k n", k=FT))
        b1_0, f3 = weight("b1_0", [P, E0A, FT], a["b1_0"])
        b2_0, f4 = weight("b2_0", [E0A, D], a["b2_0"])
        gate0, f5 = weight("gate0", [P, FT, E0], k_rows(a["gate0T"], FT))
        gbias, f6 = weight("gbias", [P, E0], a["gbias"].partition_broadcast(P))
        f7 = (iota[:, :], a["iota"])

        kdown, g1 = weight("kdown", [P, FT, GKV * LAT], k_rows(a["wk_down"], FT))
        vdown, g2 = weight("vdown", [P, FT, GKV * LAT], k_rows(a["wv_down"], FT))
        kup, g3 = weight("kup", [P, LAT], a["wk_upT"])
        vup, g4 = weight("vup", [P, LAT], a["wv_upT"])
        kdown4 = sb("kdown4", [P, FT, GKV, 4, LAT])
        Wqk = sb("Wqk", [P, FT, GH * LAT])
        Wvo = sb("Wvo", [P, FT, D])

        dma_w = {n: Dma(sp, "w_" + n, new_sem, 1) for n in ("mamba", "xattn", "ffn0", "gqa", "fold")}

        x_in = sb("x_in", [P, TT, D])
        xT_in = sb("xT_in", [P, FT, T])
        ctxT = sb("ctxT", [P, FT, T])
        mask = sb("mask", [P, TT, T], I32)
        maskT = sb("maskT", [P, TT, T], I32)
        x1 = [sb(f"x1_{i}", [P, TT, D]) for i in range(2)]
        x1T = [sb(f"x1T_{i}", [P, FT, T]) for i in range(2)]
        xs = [sb(f"xs{i}", [P, TT, D]) for i in range(2)]
        xsT = [sb(f"xsT{i}", [P, FT, T]) for i in range(2)]
        dma_x = Dma(sp, "x", new_sem, 2)
        dma_ctx = Dma(sp, "ctx", new_sem, 2)
        dma_out = Dma(sp, "out", new_sem, 2)
        dma_scratch = {n: Dma(sp, n, new_sem, 2) for n in
                       ("q_store", "q_load", "k_store", "k_load", "v_store", "v_load", "o_store", "o_load")}

        xx_pad = sb("xx_pad", [P, DT, T + TAPS - 1])
        u = sb("u", [P, DT, T])
        gate = sb("gate", [P, DT, T])
        delta = sb("delta", [P, DT, T])
        du = u
        work = sb("work", [P, DT, T])
        dbc = sb("dbc", [RANK, T])
        bc3 = sb("bc3", [96, T], BF16)
        bc_rest = sb("bc_rest", [32, T])
        bc_mid = sb("bc_mid", [32, T], BF16)
        dA = [sb(f"dA{i}", [P, DT, T]) for i in range(2)]
        hs = [sb(f"hs{i}", [P, DT, T]) for i in range(2)]
        b_all = [sb(f"b_all{i}", [P, T]) for i in range(2)]
        prod = hs
        one = sb("one", [P, 1])

        proj = sb("proj", [P, FT, T])
        parts = sb("parts", [P, 3, FT, T], BF16)
        q_store = sb("q_store", [P, H * T // 2])
        q_packed = q_store[0:96, :].bitcast(BF16).rearrange("p (h t) -> p h t", t=T)
        k_packed = sb("k_packed", [96, H, T], BF16)
        V = sb("V", [P, TT, D])
        Vpad = sb("Vpad", [P, TT, H, P])
        Vb = sb("Vb", [P, 2 * H, HD])
        nmax = sb("nmax", [P, TT, H])
        sums = sb("sums", [P, TT, H])
        nlse = sb("nlse", [P, TT, H])
        flag = sb("flag", [P, TT, H])
        lseT = sb("lseT", [H, T])
        lse3 = sb("lse3", [96, T], BF16)
        lse_mid = sb("lse_mid", [H, T], BF16)
        v_cols = sb("v_cols", [H, D])
        hide = sb("hide", [P, TT, T], BF16)
        keepT = sb("keepT", [P, TT, T], BF16)
        negT = sb("negT", [P, TT, T])
        any_kept = sb("any_kept", [P, T])
        probs = [sb(f"probs{i}", [P, TT, T]) for i in range(3)]
        attT = proj
        raw = {w: Vpad[0:96, c, :, :].rearrange("p h n -> p (h n)").bitcast(BF16).rearrange("p (h t) -> p h t", t=T)
               for c, w in enumerate("qk")}
        blkT = Vpad[0:HD, :, :, :].rearrange("p c h n -> p (c h n)").rearrange("p (h t) -> p h t", t=T)
        K4 = negT
        VL = sb("VL", [P, TT, GKV * LAT])
        combT = any_kept[0:8, :]
        hid = [q_store[:, i * FT * T:(i + 1) * FT * T].rearrange("p (k t) -> p k t", t=T) for i in range(2)]

        w_mamba = dma_w["mamba"].send([l1, l2, l3, l4, l5, l6, l7, l8, l9, l10])

        def load_batch(b, after):
            return dma_x.send([(x_in[:, :, :], a["x"][b].rearrange("(t p) d -> p t d", p=P)),
                               (xT_in[:, :, :], a["xT"][b].rearrange("(t p) d -> p t d", p=P))], after)

        def load_ctx(b, after):
            return dma_ctx.send([(ctxT[:, :, :], a["ctxT"][b].rearrange("(t p) d -> p t d", p=P)),
                                 (mask[:, :, :], a["mask"][b].rearrange("(t p) d -> p t d", p=P)),
                                 (maskT[:, :, :], a["maskT"][b].rearrange("(t p) d -> p t d", p=P))], after)

        x_loaded = load_batch(0, [])
        ctx_loaded = load_ctx(0, [])
        w_xattn = dma_w["xattn"].send(xloads)
        w_ffn0 = dma_w["ffn0"].send([f1, f2, f3, f4, f5, f6, f7])
        w_gqa = dma_w["gqa"].send([g1, g2, g3, g4])
        wqT = hid[0][:, :, :].rearrange("p k n -> p (k n)")

        consts_raw = q_store[:, 0:5 * P + 32]
        consts_loaded = dma_w["fold"].send([(consts_raw, a["consts"])])
        consts_ready = dve.step("const", lambda e: e.tensor_copy(consts[:, :], consts_raw), [consts_loaded])
        for t, value in ((eps, EPS), (one, 1.0), (ones16, 1.0), (onesb, 1.0)):
            const = pool.step("const", lambda e: e.memset(t[:, :], value))
        for t in (xx_pad, dA[0], dA[1]):
            edge = pool.step("const", lambda e: e.memset(t[:, :, 0:TAPS - 1], 0.0))
        const = pool.step("const", lambda e: e.memset(lse3[:, :], 0.0))
        const = pool.step("const", lambda e: e.memset(logits[:, :, :], LOWEST))
        A_exp = act.step("const", lambda e: e.activation(A[:, :, :], A[:, :, :], ACT.Exp), [w_mamba])
        A_neg = pool.step("const", lambda e: e.tensor_scalar(A[:, :, :], A[:, :, :], -1.0, None, ALU.mult), [A_exp])
        for g in range(GKV):
            for r in range(4):
                kdown4_done = pool.step("const", lambda e: e.tensor_copy(
                    kdown4[:, :, g, r, :], kdown[:, :, g * LAT:(g + 1) * LAT]), [w_gqa])
        folded = [w_gqa, consts_ready]
        for h in range(GH):
            loaded = dma_w["fold"].send([(wqT[:, 0:D], a["wqT"][h * GHD:(h + 1) * GHD, :]),
                                         (wqT[:, D:2 * D], a["wo"][h * GHD:(h + 1) * GHD, :])], folded)
            k = rest_banks[h % 2]
            for c in range(FT):
                t = pe.step("fold", lambda e: e.matmul(k.t[:, c * LAT:(c + 1) * LAT], wqT[:, c * P:(c + 1) * P],
                                                       kup[:, :], start=True, stop=True), [loaded, k.free, w_gqa])
            r = 32 * (h % 4)
            t = pe.step("fold", lambda e: e.matmul(k.t[r:r + LAT, D:2 * D], vup[:, :], wqT[:, D:2 * D],
                                                   start=True, stop=True))
            dve.step("fold", lambda e: e.tensor_copy(
                Wqk[:, :, h * LAT:(h + 1) * LAT], k.t[:, 0:FT * LAT].rearrange("p (c l) -> p c l", c=FT)), [t])
            k.free = dve.step("fold", lambda e: e.tensor_copy(Wvo[r:r + LAT, h // 4, :], k.t[r:r + LAT, D:2 * D]))
            folded = [t]
        fold_done = k.free

        def halves(bank):
            return bank.t[:, :].rearrange("p (k n) -> p k n", k=2)

        def layer_norm(s, ring, bank, x_old, ready, y, yT, y_free, store=None):
            st, mv, rstd = stats[s]
            summed = dve.step(s + "_ln", lambda e: e.tensor_tensor(y[:, :, :], halves(bank), x_old, ALU.add), ready + y_free)
            bank.free = summed
            ring.append(bank)
            for t in range(TT):
                k = dve.step(s + "_ln", lambda e: e.bn_stats(st[:, t, :], y[:, t, :]), [summed])
            for t in range(TT):
                k = dve.step(s + "_ln", lambda e: e.bn_aggr(mv[:, t, :], st[:, t, :]), [k])
            k2 = act.step(s + "_ln", lambda e: e.activation(rstd[:, :], mv[:, :, 1], ACT.Ln, bias=eps[:, 0:1]), [k, const])
            k2 = act.step(s + "_ln", lambda e: e.activation(rstd[:, :], rstd[:, :], ACT.Exp, scale=-0.5), [k2])
            for t in range(TT):
                normed = dve.step(s + "_ln", lambda e: e.tensor_scalar(
                    y[:, t, :], y[:, t, :], mv[:, t, 0:1], rstd[:, t:t + 1], ALU.subtract, ALU.mult), [k2, k])
            yield
            if yT is None:
                return
            turned = ring.pop(0)
            for c in range(FT):
                for t in range(TT):
                    k = pe.step(s + "_ln", lambda e: e.transpose(
                        turned.t[:, c * T + t * P:c * T + (t + 1) * P], y[:, t, c * P:(c + 1) * P], ident[:, :]),
                        [normed, turned.free, w_mamba])
            turned.free = act.step(s + "_ln", lambda e: e.activation(yT[:, :, :], halves(turned), ACT.Copy), [k] + y_free)
            ring.append(turned)
            result[s] = (normed, turned.free)

        result = {}

        def mamba(b, loaded, y_free):
            ring = mamba_banks
            x, xT = x_in, xT_in
            G = "mamba"

            filled = []
            for m in range(DT):
                k = ring.pop(0)
                for j in range(2):
                    for c in range(FT):
                        n0 = (2 * m + j) * P
                        t = pe.step(G, lambda e: e.matmul(k.t[:, j * T:(j + 1) * T], in_w[:, c, n0:n0 + P], xT[:, c, :],
                                                          start=c == 0, stop=c == FT - 1), [loaded, w_mamba, k.free])
                filled.append((k, t))
            for m in range(2):
                k, t = filled[m]
                in_pad = act.step(G, lambda e: e.activation(
                    xx_pad[:, 2 * m:2 * m + 2, TAPS - 1:], halves(k), ACT.Copy), [t, edge] + conv_read)
                k.free = in_pad
                ring.append(k)
            for m in range(2):
                k, t = filled[2 + m]
                res_in = act.step(G, lambda e: e.activation(gate[:, 2 * m:2 * m + 2, :], halves(k), ACT.Copy), [t])
                k.free = res_in
                ring.append(k)
            yield
            for d in range(DT):
                t = dve.step(G, lambda e: e.tensor_scalar(work[:, d, :], xx_pad[:, d, 0:T], conv_w[:, d, 0:1],
                                                          conv_b[:, d:d + 1], ALU.mult, ALU.add), [in_pad])
            for tap in range(1, TAPS):
                for d in range(DT):
                    t = dve.step(G, lambda e: e.scalar_tensor_tensor(
                        work[:, d, :], xx_pad[:, d, tap:tap + T], conv_w[:, d, tap:tap + 1], work[:, d, :],
                        ALU.mult, ALU.add), [t])
                yield
            conv_read[:] = [t]
            t2 = act.step(G, lambda e: e.activation(u[:, :, :], work[:, :, :], ACT.Exp, scale=-1.0), [t])
            t2 = pool.step(G, lambda e: e.tensor_scalar(u[:, :, :], u[:, :, :], 1.0, None, ALU.add), [t2])
            t2 = dve.step(G, lambda e: e.reciprocal(u[:, :, :], u[:, :, :]), [t2])
            u_ready = pool.step(G, lambda e: e.tensor_tensor(u[:, :, :], u[:, :, :], work[:, :, :], ALU.mult), [t2])
            yield
            t2 = act.step(G, lambda e: e.activation(work[:, :, :], gate[:, :, :], ACT.Exp, scale=-1.0), [res_in, u_ready])
            t2 = pool.step(G, lambda e: e.tensor_scalar(work[:, :, :], work[:, :, :], 1.0, None, ALU.add), [t2])
            t2 = dve.step(G, lambda e: e.reciprocal(work[:, :, :], work[:, :, :]), [t2])
            gate_ready = pool.step(G, lambda e: e.tensor_tensor(gate[:, :, :], gate[:, :, :], work[:, :, :], ALU.mult), [t2])
            yield
            k = ring.pop(0)
            for d in range(DT):
                t = pe.step(G, lambda e: e.matmul(k.t[0:2 * NS + RANK, 0:T], xproj[:, d, :], u[:, d, :],
                                                  start=d == 0, stop=d == DT - 1), [u_ready, k.free])
            low = act.step(G, lambda e: e.activation(dbc[:, :], k.t[2 * NS:, 0:T][0:RANK], ACT.Copy), [t])
            t = dve.step(G, lambda e: e.tensor_copy(bc3[0:32, :], k.t[0:32, 0:T]), [low])
            t = dve.step(G, lambda e: e.tensor_tensor(bc_rest[:, :], k.t[0:32, 0:T], bc3[0:32, :], ALU.subtract), [t])
            k.free = t
            t = dve.step(G, lambda e: e.tensor_copy(bc_mid[:, :], bc_rest[:, :]), [t])
            dve.step(G, lambda e: e.tensor_copy(bc3[32:64, :], bc_mid[:, :]), [t])
            bc_ready = dve.step(G, lambda e: e.tensor_tensor(bc3[64:96, :], bc_rest[:, :], bc_mid[:, :], ALU.subtract))
            k2 = k
            yield
            for m in range(2):
                k = ring.pop(0)
                for j in range(2):
                    d = 2 * m + j
                    t = pe.step(G, lambda e: e.matmul(k.t[:, j * T:(j + 1) * T], dt_w[:, d * P:(d + 1) * P], dbc[:, :],
                                                      start=True, stop=True), [low, k.free])
                for j in range(2):
                    d = 2 * m + j
                    ta = act.step(G, lambda e: e.activation(delta[:, d, :], k.t[:, j * T:(j + 1) * T], ACT.Abs,
                                                            bias=dt_b[:, d:d + 1]), [t])
                for j in range(2):
                    d = 2 * m + j
                    tv = dve.step(G, lambda e: e.tensor_scalar(work[:, d, :], k.t[:, j * T:(j + 1) * T],
                                                               dt_b[:, d:d + 1], 0.0, ALU.add, ALU.max), [t, ta, gate_ready])
                k.free = tv
                ring.append(k)
            ring.append(k2)
            t = act.step(G, lambda e: e.activation(delta[:, :, :], delta[:, :, :], ACT.Exp, scale=-1.0), [ta])
            t = act.step(G, lambda e: e.activation(delta[:, :, :], delta[:, :, :], ACT.Ln, bias=one[:, 0:1]), [t, const])
            delta_ready = pool.step(G, lambda e: e.tensor_tensor(delta[:, :, :], delta[:, :, :], work[:, :, :], ALU.add), [t, tv])
            for d in range(DT):
                t = dve.step(G, lambda e: e.tensor_scalar(work[:, d, :], u[:, d, :], skip_w[:, d:d + 1], None, ALU.mult),
                             [delta_ready])
            du_ready = pool.step(G, lambda e: e.tensor_tensor(du[:, :, :], delta[:, :, :], u[:, :, :], ALU.mult), [delta_ready, t])
            yield

            y_banks = [ring.pop(0), ring.pop(0)]
            multiplied, summed_y, copied = {}, {}, {}
            for n in range(NS):
                i = n % 2
                k = ring.pop(0)
                for half, row in ((0, n), (1, NS + n)):
                    t = pe.step(G, lambda e: e.matmul(k.t[:, half * T:(half + 1) * T], sel(row), bc3[:, :],
                                                      start=True, stop=True), [bc_ready, consts_ready, k.free])
                for d in range(DT):
                    decay = act.step(G, lambda e: e.activation(dA[i][:, d, 1:], delta[:, d, 1:], ACT.Exp,
                                                               scale=A[:, d, n:n + 1]),
                                     [delta_ready, A_neg, edge, multiplied.get(n - 2, last_scan[0])])
                b_copied = act.step(G, lambda e: e.activation(b_all[i][:, :], k.t[:, 0:T], ACT.Copy), [t, copied.get(n - 2)])
                dbu = pool.step(G, lambda e: e.tensor_tensor(
                    hs[i][:, :, :], du[:, :, :], b_all[i][:, :].unsqueeze(1).broadcast_to([P, DT, T]), ALU.mult),
                    [b_copied, du_ready, summed_y.get(n - 2, last_y[0])])
                copied[n] = dbu
                flat = lambda x: x[:, :, :].rearrange("p d t -> p (d t)")
                scanned = dve.step(G, lambda e: e.tensor_tensor_scan(flat(hs[i]), flat(dA[i]), flat(hs[i]), 0.0,
                                                                     ALU.mult, ALU.add), [decay, dbu])
                multiplied[n] = dve.step(G, lambda e: e.tensor_tensor(
                    prod[i][:, :, :], hs[i][:, :, :], k.t[:, T:2 * T].unsqueeze(1).broadcast_to([P, DT, T]), ALU.mult),
                    [scanned])
                k.free = multiplied[n]
                ring.append(k)
                for m in range(2):
                    summed_y[n] = pe.step(G, lambda e: e.matmul(
                        y_banks[m].t[:, :], ident[:, :], prod[i][:, 2 * m:2 * m + 2, :].rearrange("p d t -> p (d t)"),
                        start=n == 0, stop=n == NS - 1), [multiplied[n], y_banks[m].free])
                yield
            last_scan[0], last_y[0] = multiplied[NS - 1], summed_y[NS - 1]
            for m in range(2):
                t = dve.step(G, lambda e: e.tensor_tensor(work[:, 2 * m:2 * m + 2, :], work[:, 2 * m:2 * m + 2, :],
                                                          halves(y_banks[m]), ALU.add), [summed_y[NS - 1]])
            for k in y_banks:
                k.free = t
                ring.append(k)
            t = pool.step(G, lambda e: e.tensor_tensor(work[:, :, :], work[:, :, :], gate[:, :, :], ALU.mult), [t])
            k = ring.pop(0)
            for tt in range(TT):
                for d in range(DT):
                    t2 = pe.step(G, lambda e: e.matmul(k.t[:, tt * D:(tt + 1) * D], work[:, d, tt * P:(tt + 1) * P],
                                                       out_w[:, d, :], start=d == 0, stop=d == DT - 1), [t, k.free])
            yield
            yield from layer_norm("m", ring, k, x[:, :, :], [t2, loaded], x1[b % 2], x1T[b % 2], y_free)

        conv_read, last_scan, last_y = [], [None], [None]

        def project(G, w, src, ready, free=()):
            k = rest_banks.pop(0)
            for f in range(FT):
                for c in range(FT):
                    t = pe.step(G, lambda e: e.matmul(k.t[:, f * T:(f + 1) * T], w[:, c, f * P:(f + 1) * P], src[:, c, :],
                                                      start=c == 0, stop=c == FT - 1), ready + [k.free])
            return k, t

        def project_tokens(G, w, src, ready):
            k = rest_banks.pop(0)
            for tt in range(TT):
                for c in range(FT):
                    t = pe.step(G, lambda e: e.matmul(k.t[:, tt * D:(tt + 1) * D], src[:, c, tt * P:(tt + 1) * P],
                                                      w[:, c, :], start=c == 0, stop=c == FT - 1), ready + [k.free])
            return k, t

        def pack(G, what, b, w, bias, scale, src, ready, order, packed, packed_free, slot):
            k, t = project(G, w, src, ready)
            for f in range(FT):
                t = dve.step(G, lambda e: e.tensor_scalar(proj[:, f, :], k.t[:, f * T:(f + 1) * T], bias[:, f:f + 1],
                                                          scale, ALU.add, ALU.mult), [t, w_xattn] + parts_read)
            k.free = t
            rest_banks.append(k)
            t = pool.step(G, lambda e: e.tensor_copy(parts[:, 0, :, :], proj[:, :, :]), [t] + parts_read)
            t = pool.step(G, lambda e: e.tensor_tensor(proj[:, :, :], proj[:, :, :], parts[:, 0, :, :], ALU.subtract), [t])
            t = pool.step(G, lambda e: e.tensor_copy(parts[:, 1, :, :], proj[:, :, :]), [t])
            t = pool.step(G, lambda e: e.tensor_tensor(parts[:, 2, :, :], proj[:, :, :], parts[:, 1, :, :], ALU.subtract), [t])
            yield
            stored = dma_scratch[what + "_store"].send(
                [(scratch_q[b, slot, s].rearrange("(k p) t -> p k t", k=FT), parts[:, s, :, :]) for s in range(3)], [t])
            parts_read[:] = [stored]
            loaded = dma_scratch[what + "_load"].send(
                [(packed[r * HD:(r + 1) * HD, :, :], scratch_q[b, slot, s].rearrange("(c e) t -> e c t", e=HD))
                 for r, s in enumerate(order)], [stored] + packed_free)
            packed_ready[what] = loaded
            yield

        parts_read, packed_ready = [], {}
        softmaxed = [None]

        def turn_lse(G, heads, t):
            k = rest_banks.pop(0)
            for q in range(TT):
                t2 = pe.step(G, lambda e: e.transpose(k.t[0:heads, q * P:(q + 1) * P], nlse[:, q, 0:heads], ident[:, :]),
                             [t, k.free])
            t2 = dve.step(G, lambda e: e.tensor_copy(lseT[0:heads, :], k.t[0:heads, 0:T]), [t2])
            k.free = t2
            rest_banks.append(k)
            return t2

        def split_lse(G, heads, t):
            t = dve.step(G, lambda e: e.tensor_copy(lse3[0:heads, :], lseT[0:heads, :]), [t, const])
            t = dve.step(G, lambda e: e.tensor_tensor(lseT[0:heads, :], lseT[0:heads, :], lse3[0:heads, :], ALU.subtract), [t])
            t = dve.step(G, lambda e: e.tensor_copy(lse_mid[0:heads, :], lseT[0:heads, :]), [t])
            dve.step(G, lambda e: e.tensor_copy(lse3[32:32 + heads, :], lse_mid[0:heads, :]), [t])
            return dve.step(G, lambda e: e.tensor_tensor(lse3[64:64 + heads, :], lseT[0:heads, :], lse_mid[0:heads, :],
                                                         ALU.subtract))

        def tokens_of(G, w, bias_row, src, ready, x_old, t_x):
            s = pool.step(G, lambda e: e.tensor_tensor(
                x_sum[:, :, :], x_old[:, :, :], bias_row[:, :].unsqueeze(1).broadcast_to([P, TT, D]), ALU.add),
                [t_x, w_xattn] + x_sum_read)
            k, t = project_tokens(G, w, src, ready)
            return k, t, s

        x_sum_read = []

        def xattn0(b, ctx_ready, x_ready, xT_ready, y, yT):
            G = "x0"
            x, xT = x1[b % 2], x1T[b % 2]
            t = dve.step(G, lambda e: e.tensor_scalar(hide[:, :, :], mask[:, :, :], 0.0, HIDE, ALU.is_equal, ALU.mult), [ctx_ready])
            hide_ready = t
            keep_ready = dve.step(G, lambda e: e.tensor_scalar(keepT[:, :, :], maskT[:, :, :], 0.0, None, ALU.not_equal), [ctx_ready])
            k = rest_banks.pop(0)
            for c in range(TT):
                t = pe.step(G, lambda e: e.matmul(k.t[:, 0:T], onesb[:, :], keepT[:, c, :], start=c == 0, stop=c == TT - 1),
                            [keep_ready, const, k.free])
            t = dve.step(G, lambda e: e.tensor_scalar(any_kept[:, :], k.t[:, 0:T], 0.0, NEG, ALU.is_gt, ALU.mult), [t])
            k.free = t
            rest_banks.append(k)
            for c in range(TT):
                neg_ready = dve.step(G, lambda e: e.scalar_tensor_tensor(
                    negT[:, c, :], maskT[:, c, :], 0.0, any_kept[:, :], ALU.is_equal, ALU.mult), [t])
            masks_read[0] = neg_ready
            yield
            yield from pack(G, "k", b, xw["0k"], xw["0bk"], 1.0, ctxT, [ctx_ready, w_xattn], PARTS_K, k_packed,
                            [softmaxed[0]], 0)
            yield from pack(G, "q", b, xw["0q"], xw["0bq"], HD ** -0.5, xT, [xT_ready, w_xattn], PARTS_Q, q_packed,
                            [softmaxed[0]], 1)
            k, t = project_tokens(G, xw["0v"], ctxT, [ctx_ready, w_xattn])
            t = dve.step(G, lambda e: e.tensor_tensor(V[:, :, :], halves(k), xw["0bv"][:, :].unsqueeze(1).broadcast_to([P, TT, D]),
                                                      ALU.add), [t, w_xattn])
            k.free = v_ready = t
            rest_banks.append(k)
            zeroed = pool.step(G, lambda e: e.memset(Vpad[:, :, :, :], 0.0), blk_read)
            for c in range(TT):
                for f in range(FT):
                    half = Vpad[:, c, 8 * f:8 * f + 8, :].rearrange("p h n -> p (h n)")
                    for j in range(8):
                        pad_ready = pool.step(G, lambda e: e.tensor_copy(
                            Vpad[:, c, 8 * f + j, j * HD:(j + 1) * HD], V[:, c, f * P + j * HD:f * P + (j + 1) * HD]),
                            [v_ready, zeroed])
            k = rest_banks.pop(0)
            for c in range(TT):
                t = pe.step(G, lambda e: e.matmul(k.t[0:H, 0:D], ones16[:, :], V[:, c, :], start=c == 0, stop=c == TT - 1),
                            [v_ready, k.free, const])
            cols_ready = dve.step(G, lambda e: e.tensor_tensor(v_cols[:, :], k.t[0:H, 0:D], head_block[:, :], ALU.mult), [t])
            k.free = cols_ready
            rest_banks.append(k)
            yield
            for h in range(H):
                k = rest_banks.pop(0)
                for q in range(TT):
                    dst = k.t[:, q * T:(q + 1) * T]
                    pe.step(G, lambda e: e.matmul(dst, q_packed[:, h, q * P:(q + 1) * P], k_packed[:, h, :], start=True, stop=False),
                            [packed_ready["q"], packed_ready["k"], k.free])
                    t = pe.step(G, lambda e: e.matmul(dst, identb[:, :], hide[:, q, :], start=False, stop=True), [hide_ready])
                t = dve.step(G, lambda e: e.tensor_reduce(nmax[:, :, h], halves(k), AX.X, ALU.max, negate=True), [t])
                for q in range(TT):
                    t2 = act.step(G, lambda e: e.activation(k.t[:, q * T:(q + 1) * T], k.t[:, q * T:(q + 1) * T], ACT.Exp,
                                                            bias=nmax[:, q, h:h + 1], accum_out=sums[:, q, h:h + 1]), [t])
                k.free = t2
                rest_banks.append(k)
                yield
            ln = act.step(G, lambda e: e.activation(sums[:, :, :], sums[:, :, :], ACT.Ln), [t2])
            t = dve.step(G, lambda e: e.scalar_tensor_tensor(flag[:, :, :], nmax[:, :, :], -HIDE / 2, nmax[:, :, :],
                                                             ALU.is_lt, ALU.mult), [t2])
            t = dve.step(G, lambda e: e.tensor_tensor(nlse[:, :, :], flag[:, :, :], sums[:, :, :], ALU.subtract), [ln, t])
            lse_ready = turn_lse(G, H, t)
            yield
            acc = rest_banks.pop(0)
            scored = {}

            def score(h):
                k = rest_banks.pop(0)
                for c in range(TT):
                    t = pe.step(G, lambda e: e.matmul(k.t[:, c * T:(c + 1) * T], k_packed[:, h, c * P:(c + 1) * P],
                                                      q_packed[:, h, :], start=True, stop=True), [k.free])
                softmaxed[0] = t
                scored[h] = dve.step(G, lambda e: e.tensor_tensor(probs[h % 3][:, :, :], halves(k), keepT[:, :, :], ALU.mult),
                                     [t, probs_read.get(h % 3)])
                k.free = scored[h]
                rest_banks.append(k)

            score(0)
            for f in range(FT):
                dst = acc.t[:, f * T:(f + 1) * T]
                for c in range(TT):
                    pe.step(G, lambda e: e.matmul(dst, V[:, c, f * P:(f + 1) * P], negT[:, c, :], start=c == 0, stop=False),
                            [acc.free, neg_ready, v_ready])
                pe.step(G, lambda e: e.matmul(dst, v_cols[:, f * P:(f + 1) * P], lseT[:, :], start=False, stop=False),
                        [lse_ready, cols_ready])
                for h in range(8 * f, 8 * f + 8):
                    if h + 1 < H:
                        score(h + 1)
                    for c in range(TT):
                        t = pe.step(G, lambda e: e.matmul(dst, Vpad[:, c, h, :], probs[h % 3][:, c, :], start=False,
                                                          stop=h == 8 * f + 7 and c == TT - 1), [scored[h], pad_ready])
                    probs_read[h % 3] = t
                    yield
            pad_read[0] = t
            t = act.step(G, lambda e: e.activation(attT[:, :, :], halves(acc), ACT.Copy), [t])
            acc.free = t
            rest_banks.append(acc)
            k, t, s = tokens_of(G, xw["0o"], xw["0bo"], attT, [t, w_xattn], x, x_ready)
            x1_read[b % 2] = s
            yield from layer_norm("r", rest_banks, k, x_sum[:, :, :], [t, s], y, yT, [])
            x_sum_read[:] = [result["r"][0]]

        probs_read, pad_read, masks_read, vb_read, x1_read = {}, [None], [None], [None], {}

        def route(G, n, xT, gate_w, bias, ready):
            k = rest_banks.pop(0)
            for tt in range(TT):
                for c in range(FT):
                    t = pe.step(G, lambda e: e.matmul(k.t[:, tt * 8:tt * 8 + n], xT[:, c, tt * P:(tt + 1) * P], gate_w[:, c, :],
                                                      start=c == 0, stop=c == FT - 1), ready + [k.free])
            src = k.t[:, 0:16].rearrange("p (t n) -> p t n", t=TT)[:, :, 0:n]
            if bias is None:
                t = dve.step(G, lambda e: e.tensor_copy(logits[:, :, 0:n], src), [t, const])
            else:
                t = dve.step(G, lambda e: e.tensor_tensor(
                    logits[:, :, 0:n], src, bias[:, :].unsqueeze(1).broadcast_to([P, TT, n]), ALU.add), [t, const])
            k.free = t
            rest_banks.append(k)
            for tt in range(TT):
                t = dve.step(G, lambda e: e.max(top[:, tt, :], logits[:, tt, :]), [t])
            for tt in range(TT):
                t = dve.step(G, lambda e: e.max_index(top_i[:, tt, :], top[:, tt, :], logits[:, tt, :]), [t])
            t = dve.step(G, lambda e: e.tensor_copy(top_f[:, :, :], top_i[:, :, 0:2]), [t])
            t2 = dve.step(G, lambda e: e.tensor_tensor(wts[:, :, 0:1], top[:, :, 1:2], top[:, :, 0:1], ALU.subtract))
            t2 = act.step(G, lambda e: e.activation(wts[:, :, 1:2], wts[:, :, 0:1], ACT.Exp), [t2])
            t2 = dve.step(G, lambda e: e.tensor_scalar(wts[:, :, 2:3], wts[:, :, 1:2], 1.0, None, ALU.add), [t2])
            t2 = dve.step(G, lambda e: e.reciprocal(wts[:, :, 2:3], wts[:, :, 2:3]), [t2])
            t2 = dve.step(G, lambda e: e.tensor_tensor(wts[:, :, 3:4], wts[:, :, 1:2], wts[:, :, 2:3], ALU.mult), [t2])
            for tt in range(TT):
                dve.step(G, lambda e: e.tensor_scalar(comb[:, tt, :], iota[:, :], top_f[:, tt, 0:1], wts[:, tt, 2:3],
                                                      ALU.is_equal, ALU.mult), [t, t2, w_ffn0])
                t3 = dve.step(G, lambda e: e.tensor_scalar(comb2[:, tt, :], iota[:, :], top_f[:, tt, 1:2], wts[:, tt, 3:4],
                                                           ALU.is_equal, ALU.mult), [])
            return dve.step(G, lambda e: e.tensor_tensor(comb[:, :, :], comb[:, :, :], comb2[:, :, :], ALU.add), [t3])

        def ffn0(b, x_ready, xT_ready, x, xT, y, yT, y_free):
            G = "f0"
            E = E0 + 1
            routed = route(G, E0, xT, gate0, gbias, [xT_ready, w_ffn0])
            routed = dve.step(G, lambda e: e.memset(comb[:, :, E0:E], 1.0), [routed])
            yield
            k = rest_banks.pop(0)
            for tt in range(TT):
                t = pe.step(G, lambda e: e.transpose(k.t[0:E, tt * P:(tt + 1) * P], comb[:, tt, :], ident[:, :]),
                            [routed, k.free])
            turned = dve.step(G, lambda e: e.tensor_copy(combT[:, :], k.t[0:E, 0:T]), [t])
            k.free = turned
            rest_banks.append(k)
            hidden = {}

            def up(j):
                k = rest_banks.pop(0)
                for f in range(FT):
                    for c in range(FT):
                        t = pe.step(G, lambda e: e.matmul(k.t[:, f * T:(f + 1) * T], w1_0[:, j, c, f * P:(f + 1) * P],
                                                          xT[:, c, :], start=c == 0, stop=c == FT - 1),
                                    [xT_ready, w_ffn0, k.free])
                for f in range(FT):
                    hidden[j] = act.step(G, lambda e: e.activation(hid[j % 2][:, f, :], k.t[:, f * T:(f + 1) * T], ACT.Gelu,
                                                                   bias=b1_0[:, j, f:f + 1]),
                                         [t, hid_read.get(j % 2), fold_done])
                k.free = hidden[j]
                rest_banks.append(k)

            up(0)
            k = rest_banks.pop(0)
            for tt in range(TT):
                t = pe.step(G, lambda e: e.matmul(k.t[:, tt * D:(tt + 1) * D], combT[:, tt * P:(tt + 1) * P], b2_0[:, :],
                                                  start=True, stop=True), [turned, k.free])
            t = dve.step(G, lambda e: e.tensor_tensor(x_sum[:, :, :], halves(k), x[:, :, :], ALU.add), [t, x_ready] + x_sum_read)
            k.free = t
            rest_banks.append(k)
            yield
            for j in range(E):
                if j + 1 < E:
                    up(j + 1)
                k = rest_banks.pop(0)
                for tt in range(TT):
                    for f in range(FT):
                        t2 = pe.step(G, lambda e: e.matmul(k.t[:, tt * D:(tt + 1) * D], hid[j % 2][:, f, tt * P:(tt + 1) * P],
                                                           w2_0[:, j, f, :], start=f == 0, stop=f == FT - 1),
                                     [hidden[j], k.free])
                hid_read[j % 2] = t2
                if j < E - 1:
                    for tt in range(TT):
                        t = dve.step(G, lambda e: e.scalar_tensor_tensor(
                            x_sum[:, tt, :], k.t[:, tt * D:(tt + 1) * D], comb[:, tt, j:j + 1], x_sum[:, tt, :],
                            ALU.mult, ALU.add), [t2, t])
                    k.free = t
                    rest_banks.append(k)
                yield
            yield from layer_norm("r", rest_banks, k, x_sum[:, :, :], [t2, t], y, yT, y_free)
            x_sum_read[:] = [result["r"][0]]

        hid_read = {}

        def gqa(b, x_ready, xT_ready, x, xT, y, yT):
            G = "g1"
            k, t = project(G, Wqk, xT, [xT_ready, fold_done])
            q_ready = act.step(G, lambda e: e.activation(proj[:, :, :], halves(k), ACT.Copy, scale=GHD ** -0.5), [t] + parts_read)
            k.free = q_ready
            rest_banks.append(k)
            k = rest_banks.pop(0)
            for g in range(GKV):
                for c in range(FT):
                    t = pe.step(G, lambda e: e.matmul(k.t[:, g * T:(g + 1) * T],
                                                      kdown4[:, c, g, :, :].rearrange("p r l -> p (r l)"), xT[:, c, :],
                                                      start=c == 0, stop=c == FT - 1), [xT_ready, kdown4_done, k.free])
            k_ready = act.step(G, lambda e: e.activation(K4[:, :, :], halves(k), ACT.Copy), [t])
            k.free = k_ready
            rest_banks.append(k)
            k = rest_banks.pop(0)
            W = GKV * LAT
            for tt in range(TT):
                for c in range(FT):
                    t = pe.step(G, lambda e: e.matmul(k.t[:, tt * W:(tt + 1) * W], xT[:, c, tt * P:(tt + 1) * P], vdown[:, c, :],
                                                      start=c == 0, stop=c == FT - 1), [k.free])
            v_ready = act.step(G, lambda e: e.activation(
                VL[:, :, :], k.t[:, 0:TT * W].rearrange("p (t n) -> p t n", t=TT), ACT.Copy), [t])
            k.free = v_ready
            rest_banks.append(k)
            yield
            for h in range(GH):
                r, g = 32 * (h % 4), h // 4
                k = rest_banks.pop(0)
                for q, at, n in ((0, 0, P), (1, P, T)):
                    pe.step(G, lambda e: e.matmul(k.t[:, at:at + n], proj[r:r + LAT, g, q * P:(q + 1) * P], K4[r:r + LAT, g, 0:n],
                                                  start=True, stop=False), [q_ready, k_ready, k.free])
                    t = pe.step(G, lambda e: e.matmul(k.t[:, at + n - P:at + n], identb[:, :], causal[:, :], start=False, stop=True))
                for q, at, n in ((0, 0, P), (1, P, T)):
                    t2 = dve.step(G, lambda e: e.tensor_reduce(nmax[:, q, h:h + 1], k.t[:, at:at + n], AX.X, ALU.max, negate=True), [t])
                for q, at, n in ((0, 0, P), (1, P, T)):
                    t3 = act.step(G, lambda e: e.activation(k.t[:, at:at + n], k.t[:, at:at + n], ACT.Exp, bias=nmax[:, q, h:h + 1],
                                                            accum_out=sums[:, q, h:h + 1]), [t2])
                k.free = t3
                rest_banks.append(k)
                if h % 2:
                    yield
            ln = act.step(G, lambda e: e.activation(sums[:, :, 0:GH], sums[:, :, 0:GH], ACT.Ln), [t3])
            t = dve.step(G, lambda e: e.tensor_tensor(nlse[:, :, 0:GH], nmax[:, :, 0:GH], sums[:, :, 0:GH], ALU.subtract), [ln])
            t = turn_lse(G, GH, t)
            lse_ready = split_lse(G, GH, t)
            yield
            acc = rest_banks.pop(0)
            ready = {}

            def score(h):
                r, g = 32 * (h % 4), h // 4
                k = rest_banks.pop(0)
                for c, at, q0 in ((0, 0, 0), (1, T, P)):
                    n = T - q0
                    pe.step(G, lambda e: e.matmul(k.t[:, at:at + n], K4[r:r + LAT, g, c * P:(c + 1) * P], proj[r:r + LAT, g, q0:T],
                                                  start=True, stop=False), [k.free])
                    pe.step(G, lambda e: e.matmul(k.t[:, at:at + P], identb[:, :], causalT[:, :], start=False, stop=False))
                    t = pe.step(G, lambda e: e.matmul(k.t[:, at:at + n], sel(h), lse3[:, q0:T], start=False, stop=True), [lse_ready])
                flat = probs[h % 3][:, :, :].rearrange("p c t -> p (c t)")
                ready[h] = act.step(G, lambda e: e.activation(flat[:, 0:T + P], k.t[:, 0:T + P], ACT.Exp), [t, probs_read.get(h % 3)])
                k.free = ready[h]
                rest_banks.append(k)

            score(0)
            score(1)
            for h in range(GH):
                r, g = 32 * (h % 4), h // 4
                if h + 2 < GH:
                    score(h + 2)
                flat = probs[h % 3][:, :, :].rearrange("p c t -> p (c t)")
                pe.step(G, lambda e: e.matmul(acc.t[r:r + LAT, g * T:(g + 1) * T], VL[:, 0, g * LAT:(g + 1) * LAT], flat[:, 0:T],
                                              start=True, stop=False), [ready[h], v_ready, acc.free])
                t = pe.step(G, lambda e: e.matmul(acc.t[r:r + LAT, g * T + P:(g + 1) * T], VL[:, 1, g * LAT:(g + 1) * LAT],
                                                  flat[:, T:T + P], start=False, stop=True))
                probs_read[h % 3] = t
                yield
            t = act.step(G, lambda e: e.activation(attT[:, :, :], halves(acc), ACT.Copy), [t])
            acc.free = t
            rest_banks.append(acc)
            k, t = project_tokens(G, Wvo, attT, [t])
            yield from layer_norm("r", rest_banks, k, x[:, :, :], [t, x_ready], y, yT, [])

        def xattn1(b, x_ready, xT_ready, x, xT, y, yT):
            G = "x1"
            BT = T // H
            HT = BT // 2
            k, t = project_tokens(G, xw["1v"], ctxT, [w_xattn])
            t = dve.step(G, lambda e: e.tensor_tensor(V[:, :, :], halves(k), xw["1bv"][:, :].unsqueeze(1).broadcast_to([P, TT, D]),
                                                      ALU.add), [t, w_xattn])
            k.free = t
            rest_banks.append(k)
            stored = dma_scratch["v_store"].send([(scratch_v[b].rearrange("(t p) d -> p t d", p=P), V[:, :, :])], [t])
            v_ready = dma_scratch["v_load"].send(
                [(Vb[c * HT:(c + 1) * HT, :, :],
                  scratch_v[b].rearrange("(j t) (c e) -> c t j e", t=HT, e=HD)[c]) for c in range(H)], [stored, vb_read[0]])
            yield
            yield from pack(G, "k", b, xw["1k"], xw["1bk"], 1.0, ctxT, [w_xattn], PARTS_K, raw["k"], [pad_read[0]], 2)
            result["ctx"] = parts_read[0]
            yield from pack(G, "q", b, xw["1q"], xw["1bq"], HD ** -0.5, xT, [xT_ready, w_xattn], PARTS_Q, raw["q"],
                            [pad_read[0]], 3)
            for what, packed in (("k", k_packed), ("q", q_packed)):
                for tile in range(2):
                    ordered = dve.step(G, lambda e: e.tensor_copy(
                        packed[:, :, tile * P:(tile + 1) * P].rearrange("p h (c t) -> p h c t", t=HT),
                        raw[what][:, :, :].rearrange("p c (h i t) -> p h i c t", h=H, i=2)[:, :, tile]),
                        [packed_ready[what], softmaxed[0]])
            yield

            for h in range(H):
                k = rest_banks.pop(0)
                for q, at, n in ((0, 0, P), (1, P, T)):
                    pe.step(G, lambda e: e.matmul(k.t[:, at:at + n], q_packed[:, h, q * P:(q + 1) * P], k_packed[:, h, 0:n],
                                                  start=True, stop=False), [ordered, k.free])
                    t = pe.step(G, lambda e: e.matmul(k.t[:, at + n - P:at + n], identb[:, :], bcausal[:, :], start=False, stop=True))
                for q, at, n in ((0, 0, P), (1, P, T)):
                    t2 = dve.step(G, lambda e: e.tensor_reduce(nmax[:, q, h:h + 1], k.t[:, at:at + n], AX.X, ALU.max, negate=True), [t])
                for q, at, n in ((0, 0, P), (1, P, T)):
                    t3 = act.step(G, lambda e: e.activation(k.t[:, at:at + n], k.t[:, at:at + n], ACT.Exp, bias=nmax[:, q, h:h + 1],
                                                            accum_out=sums[:, q, h:h + 1]), [t2])
                k.free = t3
                rest_banks.append(k)
                yield
            ln = act.step(G, lambda e: e.activation(sums[:, :, :], sums[:, :, :], ACT.Ln), [t3])
            t = dve.step(G, lambda e: e.tensor_tensor(nlse[:, :, :], nmax[:, :, :], sums[:, :, :], ALU.subtract), [ln])
            t = turn_lse(G, H, t)
            lse_ready = split_lse(G, H, t)
            yield
            ready = {}

            def score(h):
                k = rest_banks.pop(0)
                for c, at, q0 in ((0, 0, 0), (1, T, P)):
                    n = T - q0
                    pe.step(G, lambda e: e.matmul(k.t[:, at:at + n], k_packed[:, h, c * P:(c + 1) * P], q_packed[:, h, q0:T],
                                                  start=True, stop=False), [k.free])
                    pe.step(G, lambda e: e.matmul(k.t[:, at:at + P], identb[:, :], bcausalT[:, :], start=False, stop=False))
                    t = pe.step(G, lambda e: e.matmul(k.t[:, at:at + n], sel(h), lse3[:, q0:T], start=False, stop=True), [lse_ready])
                softmaxed[0] = t
                flat = probs[h % 3][:, :, :].rearrange("p c t -> p (c t)")
                ready[h] = act.step(G, lambda e: e.activation(flat[:, 0:T + P], k.t[:, 0:T + P], ACT.Exp), [t, probs_read.get(h % 3)])
                k.free = ready[h]
                rest_banks.append(k)

            score(0)
            score(1)
            for h in range(H):
                if h + 2 < H:
                    score(h + 2)
                if h % 2 == 0:
                    acc = rest_banks.pop(0)
                at = (h % 2) * T
                flat = probs[h % 3][:, :, :].rearrange("p c t -> p (c t)")
                pe.step(G, lambda e: e.matmul(acc.t[0:HD, at:at + T], Vb[:, 2 * h, :], flat[:, 0:T], start=True, stop=False),
                        [ready[h], v_ready, acc.free])
                t = pe.step(G, lambda e: e.matmul(acc.t[0:HD, at + P:at + T], Vb[:, 2 * h + 1, :], flat[:, T:T + P],
                                                  start=False, stop=True))
                probs_read[h % 3] = t
                if h % 2:
                    t = act.step(G, lambda e: e.activation(
                        blkT[:, :, (h - 1) * BT:(h + 1) * BT].rearrange("p c (i t) -> p c i t", t=HT),
                        acc.t[0:HD, :].rearrange("p (i c t) -> p c i t", c=H, t=HT), ACT.Copy), [t, ordered])
                    acc.free = t
                    rest_banks.append(acc)
                yield
            vb_read[0] = probs_read[(H - 1) % 3]
            stored = dma_scratch["o_store"].send([(scratch_o[b].rearrange("(c e) t -> e c t", e=HD), blkT[:, :, :])], [t])
            blk_read[:] = [stored]
            t = dma_scratch["o_load"].send([(attT[:, :, :], scratch_o[b].rearrange("(k p) t -> p k t", k=FT))], [stored])
            yield
            k, t, s = tokens_of(G, xw["1o"], xw["1bo"], attT, [t, w_xattn], x, x_ready)
            yield from layer_norm("r", rest_banks, k, x_sum[:, :, :], [t, s], y, yT, [])
            x_sum_read[:] = [result["r"][0]]

        ctx_read, blk_read = [None], []

        def rest(b, ctx_ready, x1_ready, x1T_ready):
            yield from xattn0(b, ctx_ready, x1_ready, x1T_ready, xs[0], xsT[0])
            r = result["r"]
            yield from ffn0(b, r[0], r[1], xs[0], xsT[0], xs[1], xsT[1], [x5_stored[0]])
            r = result["r"]
            yield from gqa(b, r[0], r[1], xs[1], xsT[1], xs[0], xsT[0])
            r = result["r"]
            yield from xattn1(b, r[0], r[1], xs[0], xsT[0], xs[1], xsT[1])
            r = result["r"]
            x5_stored[0] = dma_out.send([(scratch_x[b].rearrange("(t p) d -> p t d", p=P), xs[1][:, :, :]),
                                         (scratch_xT[b].rearrange("(k p) t -> p k t", p=P), xsT[1][:, :, :])], [r[0], r[1]])

        x5_stored = [None]

        MAMBA_STEPS, REST_STEPS = 30, 100
        for _ in mamba(0, x_loaded, []):
            pass
        for b in range(BATCH):
            x1_ready, x1T_ready = result["m"]
            if b + 1 < BATCH:
                x_loaded = load_batch(b + 1, list(result["m"]))
                y_free = [x1_read.get((b + 1) % 2)]
                m = mamba(b + 1, x_loaded, y_free)
            else:
                m = iter(())
            if b:
                ctx_loaded = load_ctx(b, [result["ctx"], masks_read[0]])
            due = 0
            for _ in rest(b, ctx_loaded, x1_ready, x1T_ready):
                due += MAMBA_STEPS
                while due >= REST_STEPS:
                    due -= REST_STEPS
                    next(m, None)
            for _ in m:
                pass
        stages_done = [t for e in (pe, dve, act, pool) for t in e.all_steps()] + [x5_stored[0]]
        phase.close()
        for k in banks:
            k.free = None
        phase_b = ctx.enter_context(ExitStack())

        def sb2(name, shape, dt=FP32):
            return phase_b.enter_context(nc.sbuf_tensor(name, shape, dt))

        G = "f1"
        FH = HID1 // P
        x5 = [sb2(f"x5_{i}", [P, TT, D]) for i in range(2)]
        x5T = [sb2(f"x5T_{i}", [P, FT, T]) for i in range(2)]
        y6 = [sb2(f"y6_{i}", [P, TT, D]) for i in range(2)]
        hid1 = [sb2(f"hid1_{i}", [P, FH, T]) for i in range(2)]
        gate1, gate1_load = weight("gate1", [P, FT, E1], k_rows(a["Wg"], FT), alloc=sb2)
        w1_1 = sb2("w_w1_1", [P, E1, FT, HID1])
        w2_1 = sb2("w_w2_1", [P, E1, FH, D])
        dma_x5 = Dma(sp, "x5", new_sem, 2)

        def load_x5(b, after):
            return dma_x5.send([(x5[b % 2][:, :, :], scratch_x[b].rearrange("(t p) d -> p t d", p=P)),
                                (x5T[b % 2][:, :, :], scratch_xT[b].rearrange("(k p) t -> p k t", p=P))], after)

        x5_loaded = [load_x5(0, stages_done)]
        gate_loaded = Dma(sp, "gate1", new_sem, 1).send([gate1_load])
        w_loaded = [Dma(sp, f"expert{j}", new_sem, 1).send(
            [(w1_1[:, j, :, :], k_rows(a["W1"][j], FT)), (w2_1[:, j, :, :], k_rows(a["W2"][j], FH))]) for j in range(E1)]
        x5_loaded.append(load_x5(1, []))
        hidden, hid_free, y_sent, batch_done = {}, {}, {}, {}
        for b in range(BATCH):
            x, xT, y = x5[b % 2], x5T[b % 2], y6[b % 2]
            ready = x5_loaded[b]
            routed = route(G, E1, xT, gate1, None, [ready, gate_loaded])

            def up(j):
                for m in range(FH // 2):
                    k = rest_banks.pop(0)
                    for i in range(2):
                        f = 2 * m + i
                        for c in range(FT):
                            t = pe.step(G, lambda e: e.matmul(k.t[:, i * T:(i + 1) * T], w1_1[:, j, c, f * P:(f + 1) * P],
                                                              xT[:, c, :], start=c == 0, stop=c == FT - 1),
                                        [ready, w_loaded[j], k.free])
                    hidden[j] = act.step(G, lambda e: e.activation(hid1[j % 2][:, 2 * m:2 * m + 2, :], halves(k), ACT.Relu),
                                         [t, hid_free.get(j % 2)])
                    k.free = hidden[j]
                    rest_banks.append(k)

            up(0)
            t = None
            for j in range(E1):
                if j + 1 < E1:
                    up(j + 1)
                k = rest_banks.pop(0)
                for tt in range(TT):
                    for f in range(FH):
                        t2 = pe.step(G, lambda e: e.matmul(k.t[:, tt * D:(tt + 1) * D], hid1[j % 2][:, f, tt * P:(tt + 1) * P],
                                                           w2_1[:, j, f, :], start=f == 0, stop=f == FH - 1),
                                     [hidden[j], k.free])
                hid_free[j % 2] = t2
                src = x if j == 0 else x_sum
                for tt in range(TT):
                    t = dve.step(G, lambda e: e.scalar_tensor_tensor(
                        x_sum[:, tt, :], k.t[:, tt * D:(tt + 1) * D], comb[:, tt, j:j + 1], src[:, tt, :],
                        ALU.mult, ALU.add), [t2, t, routed, ready])
                k.free = t
                rest_banks.append(k)
            if b + 2 < BATCH:
                x5_loaded.append(load_x5(b + 2, [t, t2]))
            st, mv, rstd = stats["r"]
            for tt in range(TT):
                t = dve.step(G, lambda e: e.bn_stats(st[:, tt, :], x_sum[:, tt, :]), [t])
            for tt in range(TT):
                t = dve.step(G, lambda e: e.bn_aggr(mv[:, tt, :], st[:, tt, :]), [t])
            t2 = act.step(G, lambda e: e.activation(rstd[:, :], mv[:, :, 1], ACT.Ln, bias=eps[:, 0:1]), [t])
            t2 = act.step(G, lambda e: e.activation(rstd[:, :], rstd[:, :], ACT.Exp, scale=-0.5), [t2])
            for tt in range(TT):
                t = dve.step(G, lambda e: e.tensor_scalar(y[:, tt, :], x_sum[:, tt, :], mv[:, tt, 0:1], rstd[:, tt:tt + 1],
                                                          ALU.subtract, ALU.mult), [t2, t, y_sent.get(b % 2)])
            y_sent[b % 2] = dma_out.send([(out[b].rearrange("(t p) d -> p t d", p=P), y[:, :, :])], [t])
        for d in list(dma_scratch.values()) + [dma_out]:
            for i, s in enumerate(d.sems):
                sp.wait([(s, d.count[i], f"{d.name}{i}")])


def order_ct(n_tokens):
    return (16 * np.arange(n_tokens)[None, :] + np.arange(16)[:, None]).reshape(-1)


def constants():
    below = lambda rows, cols: np.where(cols[None, :] > rows[:, None], HIDE, 0.0).astype(np.float32)
    n = np.arange(P)
    block = order_ct(8)
    sel = np.zeros((P, 32), np.float32)
    sel[:96] = np.tile(np.eye(32), (3, 1))
    head_block = np.zeros((H, D), np.float32)
    for h in range(H):
        head_block[h, h * HD:(h + 1) * HD] = 1
    return {
        "ident": np.eye(P, dtype=np.float32), "head_block": head_block,
        "iota": np.tile(np.arange(8, dtype=np.float32), (P, 1)),
        "consts": np.concatenate([np.eye(P, dtype=np.float32), below(n, n), below(n, n).T,
                                  below(block, block), below(block, block).T, sel], 1),
    }


def kernel(**inputs):
    import numpy as _np
    import concourse.bacc as _bacc
    from concourse import mybir as _mybir
    from concourse.bass_utils import run_bass_kernel_spmd as _run

    i = {k: _np.asarray(v) for k, v in inputs.items()}
    m, c, e, r = "L0_attn_", "L0_xattn_", "L0_ffn_", "L1_attn_"
    xp = i[m + "xproj_w"].T
    host = {
        "x": i["x"], "xT": i["x"].transpose(0, 2, 1), "ctxT": i["ctx_1024"].transpose(0, 2, 1),
        "mask": i["mask_BxSxS2_if1"], "maskT": i["mask_BxSxS2_if1"].transpose(0, 2, 1),
        "in_wT": i[m + "in_w"].T, "conv_w": i[m + "conv_w"][:, 0, :], "conv_b": i[m + "conv_b"],
        "xprojT": _np.concatenate([xp[:, RANK:], xp[:, :RANK]], 1), "dt_wT": i[m + "dt_w"].T, "dt_b": i[m + "dt_b"],
        "A_log": i[m + "A_log"], "D": i[m + "D"], "out_wT": i[m + "out_w"].T,
        "w1_0": _np.concatenate([i[e + "rw1"], i[e + "sw1"][None]]), "b1_0": _np.concatenate([i[e + "rb1"], i[e + "sb1"][None]]),
        "w2_0": _np.concatenate([i[e + "rw2"], i[e + "sw2"][None]]), "b2_0": _np.concatenate([i[e + "rb2"], i[e + "sb2"][None]]),
        "gate0T": i[e + "gate_w"].T, "gbias": i[e + "expert_bias"],
        "wqT": i[r + "wq"].T, "wk_down": i[r + "wk_down"], "wv_down": i[r + "wv_down"],
        "wk_upT": i[r + "wk_up"].T, "wv_upT": i[r + "wv_up"].T, "wo": i[r + "wo"],
        "Wg": i["L1_ffn_Wg"], "W1": i["L1_ffn_W1"], "W2": i["L1_ffn_W2"],
    }
    for layer, last in (("0", "o"), ("1", "p")):
        for part in "qkvo":
            n = last if part == "o" else part
            host[f"W{part}{layer}T"] = i[f"L{layer}_xattn_W{n}"].T
            host[f"b{part}{layer}"] = i[f"L{layer}_xattn_b{n}"]
    cols = lambda v: v.reshape(*v.shape[:-1], -1, P)
    for name in ("conv_b", "dt_b", "D", "bq0", "bk0", "bq1", "bk1"):
        host[name] = cols(host[name]).T
    host["b1_0"] = cols(host["b1_0"]).transpose(2, 0, 1)
    host.update(constants())
    nc = _bacc.Bacc("TRN2", target_bir_lowering=False, num_devices=1)
    arrays, aps = {}, {}
    for name, v in host.items():
        v = _np.ascontiguousarray(v)
        arrays["in_" + name] = v
        aps[name] = nc.dram_tensor("in_" + name, v.shape, _mybir.dt.from_np(v.dtype), kind="ExternalInput").ap()
    out = nc.dram_tensor("out_0", (BATCH, T, D), FP32, kind="ExternalOutput").ap()
    scratch_q = nc.dram_tensor("scratch_q", (BATCH, 4, 3, D, T), BF16, kind="Internal").ap()
    scratch_o = nc.dram_tensor("scratch_o", (BATCH, D, T), FP32, kind="Internal").ap()
    scratch_v = nc.dram_tensor("scratch_v", (BATCH, T, D), FP32, kind="Internal").ap()
    scratch_x = nc.dram_tensor("scratch_x", (BATCH, T, D), FP32, kind="Internal").ap()
    scratch_xT = nc.dram_tensor("scratch_xT", (BATCH, D, T), FP32, kind="Internal").ap()
    program(nc, aps, out, scratch_q, scratch_o, scratch_v, scratch_x, scratch_xT)
    got = _run(nc, [arrays], core_ids=[0])
    return got.results[0]["out_0"]
```

```python
from contextlib import ExitStack

import numpy as np
import concourse.bass as bass
from concourse import mybir

FP32 = mybir.dt.float32
BF16 = mybir.dt.bfloat16
F32R = mybir.dt.float32r
I32 = mybir.dt.int32
U32 = mybir.dt.uint32
ALU = mybir.AluOpType
ACT = mybir.ActivationFunctionType
AX = mybir.AxisListType

P = 128
BATCH, T, D = 16, 256, 256
TT = T // P
FT = D // P
DI = 512
DT = DI // P
NS = 16
RANK = 16
TAPS = 4
H, HD = 16, 16
GH, GKV, LAT, GHD = 8, 2, 32, 128
E0, E1, HID1 = 7, 8, 512
EPS = 1e-5
NEG = -1e9
HIDE = -1e30
LOWEST = -3e38
MAMBA_LAG = 12
LATE_LAG = 40
PARTS_Q = (0, 0, 1, 1, 0, 2)
PARTS_K = (0, 1, 0, 1, 2, 0)


class Engine:

    def __init__(self, eng, name, new_sem):
        self.eng, self.name, self.new_sem = eng, name, new_sem
        self.sems, self.count, self.seen = {}, {}, {}

    def wait(self, after):
        for t in after:
            if t is None:
                continue
            sem, value, key = t
            if self.seen.get(key, 0) < value:
                self.eng.wait_ge(sem, value)
                self.seen[key] = value

    def step(self, stage, issue, after=()):
        self.wait(after)
        key = f"{self.name}_{stage}"
        if key not in self.sems:
            self.sems[key] = self.new_sem(key)
            self.count[key] = 0
        issue(self.eng).then_inc(self.sems[key], 1)
        self.count[key] += 1
        return self.sems[key], self.count[key], key

    def all_steps(self):
        return [(self.sems[k], self.count[k], k) for k in self.sems]


class Dma:

    def __init__(self, engine, name, new_sem, turns):
        self.engine, self.name = engine, name
        self.sems = [new_sem(f"dma_{name}{i}") for i in range(turns)]
        self.count = [0] * turns
        self.at = 0

    def send(self, pairs, after=()):
        self.engine.wait(after)
        i = self.at % len(self.sems)
        self.at += 1
        for out, in_ in pairs:
            self.engine.eng.dma_start(out, in_).then_inc(self.sems[i], 16)
            self.count[i] += 16
        return self.sems[i], self.count[i], f"{self.name}{i}"

    def all_sent(self):
        return [(s, self.count[i], f"{self.name}{i}") for i, s in enumerate(self.sems) if self.count[i]]


class Split:

    def __init__(self, alloc, name, shape):
        self.hi, self.lo = alloc(name + "_hi", shape, F32R), alloc(name + "_lo", shape, F32R)

    def divide(self, first, second, stage, at, x, ready):
        hi, lo = self.hi[at], self.lo[at]
        if first.name == "act":
            t = first.step(stage, lambda e: e.activation(hi, x, ACT.Copy), ready)
        else:
            t = first.step(stage, lambda e: e.tensor_copy(hi, x), ready)
        return second.step(stage, lambda e: e.tensor_tensor(lo, x, hi.bitcast(FP32), ALU.subtract), [t])


END = object()


def interleave(streams):
    waits = [w for _, w, _ in streams]
    alive = [True] * len(streams)
    while any(alive):
        for i, (g, _, n) in enumerate(streams):
            if waits[i] > 0:
                waits[i] -= 1
                continue
            for _ in range(n):
                if alive[i] and next(g, END) is END:
                    alive[i] = False


class Stream:

    def __init__(self, name):
        self.name = name
        self.normed = self.out = self.stored = None


class Bank:

    def __init__(self, tensor):
        self.t, self.free = tensor, None


def program(nc, a, out, scratch_q, scratch_o, scratch_v, scratch_x2, scratch_x2T, scratch_x, scratch_xT):
    ctx = ExitStack()
    phase = [ExitStack()]
    with ctx:
        def keep(name, shape, dt=FP32):
            return ctx.enter_context(nc.sbuf_tensor(name, shape, dt))

        def sb(name, shape, dt=FP32):
            return phase[0].enter_context(nc.sbuf_tensor(name, shape, dt))

        def new_sem(name):
            return ctx.enter_context(nc.semaphore(name))

        pe = Engine(nc.tensor, "pe", new_sem)
        dve = Engine(nc.vector, "dve", new_sem)
        act = Engine(nc.scalar, "act", new_sem)
        pool = Engine(nc.gpsimd, "pool", new_sem)
        sp = Engine(nc.sync, "sp", new_sem)
        ring = [Bank(ctx.enter_context(nc.psum_tensor(f"bank{i}", [P, 512], FP32))) for i in range(8)]

        def split_matmul(stage, out, w, w_at, x, x_at, start, stop, ready):
            parts = ((w.lo, x.hi), (w.hi, x.lo), (w.hi, x.hi))
            for i, (wp, xp) in enumerate(parts):
                t = pe.step(stage, lambda e: e.matmul(out, wp[w_at], xp[x_at],
                                                      start=start and i == 0, stop=stop and i == 2), ready)
            return t

        def next_phase(stores):
            done = [t for e in (pe, dve, act, pool) for t in e.all_steps()]
            done += [t for d in stores for t in d.all_sent()]
            phase[0].close()
            phase[0] = ExitStack()
            return done

        def weight(name, shape, view, dt=FP32, alloc=sb):
            t = alloc("w_" + name, shape, dt)
            return t, (t[tuple(slice(None) for _ in shape)], view)

        k_rows = lambda ap, k: ap.rearrange("(k p) n -> p k n", k=k)
        rows_of = lambda ap: ap.rearrange("(t p) d -> p t d", p=P)
        stats_of = lambda s: (sb("stats" + s, [P, TT, 6]), sb("mv" + s, [P, TT, 2]), sb("rstd" + s, [P, TT]))

        def routing_of(s):
            r = [sb(n + s, [P, TT, w], dt) for n, w, dt in (
                ("logits", 8, FP32), ("top", 8, FP32), ("top_i", 8, U32), ("top_f", 2, FP32), ("wts", 4, FP32),
                ("comb", 8, FP32), ("comb2", 8, FP32))]
            return r + [pool.step("const", lambda e: e.memset(r[0][:, :, :], LOWEST))]

        root = keep("root", [P, TT])
        iota = keep("iota", [P, 8])
        ident = keep("ident", [P, P])
        consts = keep("consts", [P, 5 * P + 32], BF16)
        identb, causal, causalT, bcausal, bcausalT = (consts[:, i * P:(i + 1) * P] for i in range(5))
        sel1 = consts[0:96, 5 * P:]

        def sel(row):
            return sel1[:, row:row + 1].broadcast_to([96, P])

        dma_w = {n: Dma(sp, "w_" + n, new_sem, 1) for n in ("const", "mamba", "x0", "route", "x1", "gqa", "fold")}
        ident_ready = dma_w["const"].send([(ident[:, :], a["ident"]), (iota[:, :], a["iota"])])
        const = pool.step("const", lambda e: e.memset(root[:, :], -0.5))

        in_w, l1 = weight("in_w", [P, FT, 2 * DI], k_rows(a["in_wT"], FT))
        conv_w, l2 = weight("conv_w", [P, DT, TAPS], k_rows(a["conv_w"], DT))
        conv_b, l3 = weight("conv_b", [P, DT], a["conv_b"])
        xproj, l4 = weight("xproj", [P, DT, 2 * NS + RANK], k_rows(a["xprojT"], DT))
        dt_w, l5 = weight("dt_w", [RANK, DI], a["dt_wT"])
        dt_b, l6 = weight("dt_b", [P, DT], a["dt_b"])
        A, l7 = weight("A_log", [P, DT, NS], k_rows(a["A_log"], DT))
        skip_w, l8 = weight("D", [P, DT], a["D"])
        out_w, l9 = weight("out_w", [P, DT, D], k_rows(a["out_wT"], DT))

        def attention_weights(layer):
            loads = []
            for m in "qkvo":
                xw[layer + m], l = weight(f"x{layer}{m}", [P, FT, D], k_rows(a[f"W{m}{layer}T"], FT))
                loads.append(l)
                if m in "qk":
                    xw[layer + "b" + m], l = weight(f"x{layer}b{m}", [P, FT], a[f"b{m}{layer}"])
                else:
                    xw[layer + "b" + m], l = weight(f"x{layer}b{m}", [P, D], a[f"b{m}{layer}"].partition_broadcast(P))
                loads.append(l)
            return loads

        xw = {}
        xloads = attention_weights("0")
        head_block, l = weight("head_block", [H, D], a["head_block"])
        xloads.append(l)
        ones16 = sb("ones16", [P, H])
        onesb = sb("onesb", [P, P], BF16)
        one = sb("one", [P, 1])

        def halves(bank):
            return bank.t[:, :].rearrange("p (k n) -> p k n", k=2)

        def layer_norm(s, bank, x_old, ready, y, yT, y_free):
            st, mv, rstd = s.stats
            G = "ln" + s.name
            yield
            summed = dve.step(G, lambda e: e.tensor_tensor(y[:, :, :], halves(bank), x_old, ALU.add), ready + y_free)
            bank.free = summed
            ring.append(bank)
            for t in range(TT):
                k = dve.step(G, lambda e: e.bn_stats(st[:, t, :], y[:, t, :]), [summed])
            for t in range(TT):
                k = dve.step(G, lambda e: e.bn_aggr(mv[:, t, :], st[:, t, :]), [k])
            k2 = dve.step(G, lambda e: e.tensor_scalar(rstd[:, :], mv[:, :, 1], EPS, None, ALU.add), [k])
            k2 = pool.step(G, lambda e: e.tensor_tensor(rstd[:, :], rstd[:, :], root[:, :], ALU.pow), [k2, const])
            for t in range(TT):
                normed = dve.step(G, lambda e: e.tensor_scalar(
                    y[:, t, :], y[:, t, :], mv[:, t, 0:1], rstd[:, t:t + 1], ALU.subtract, ALU.mult), [k2, k])
            yield
            yield
            yield
            turned = ring.pop(0)
            for c in range(FT):
                for t in range(TT):
                    k = pe.step(G, lambda e: e.transpose(
                        turned.t[:, c * T + t * P:c * T + (t + 1) * P], y[:, t, c * P:(c + 1) * P], ident[:, :]),
                        [normed, turned.free, ident_ready])
            turned.free = act.step(G, lambda e: e.activation(yT[:, :, :], halves(turned), ACT.Copy), [k] + y_free)
            ring.append(turned)
            s.normed = (normed, turned.free)
            yield

        scanning = []

        def mamba_stream(name):
            s = Stream(name)
            s.stats = stats_of(name)
            s.x_in = x_in = sb("x_in" + name, [P, TT, D])
            s.xT_in = xT_in = sb("xT_in" + name, [P, FT, T])
            s.x1 = x1 = sb("x1" + name, [P, TT, D])
            s.x1T = x1T = sb("x1T" + name, [P, FT, T])
            dma_x = Dma(sp, "x" + name, new_sem, 1)

            def load(b, after):
                return dma_x.send([(x_in[:, :, :], a["x"][b].rearrange("(t p) d -> p t d", p=P)),
                                   (xT_in[:, :, :], a["xT"][b].rearrange("(t p) d -> p t d", p=P))], after)

            xx_pad = sb("xx_pad" + name, [P, DT, T + TAPS - 1])
            u = sb("u" + name, [P, DT, T])
            gate = sb("gate" + name, [P, DT, T])
            delta = sb("delta" + name, [P, DT, T])
            du = u
            work = sb("work" + name, [P, DT, T])
            dbc = sb("dbc" + name, [RANK, T])
            bc3 = sb("bc3" + name, [96, T], BF16)
            bc_rest = sb("bc_rest" + name, [32, T])
            bc_mid = sb("bc_mid" + name, [32, T], BF16)
            dA = [sb(f"dA{name}{i}", [P, DT, T]) for i in range(2)]
            hs = [sb(f"hs{name}{i}", [P, DT, T]) for i in range(3)]
            b_all = [sb(f"b_all{name}{i}", [P, T]) for i in range(2)]
            for t in (xx_pad, dA[0], dA[1]):
                edge = pool.step("const", lambda e: e.memset(t[:, :, 0:TAPS - 1], 0.0))

            def mamba(b, loaded, y_free):
                x, xT, G = x_in, xT_in, "mamba" + s.name

                for m in range(DT):
                    k = ring.pop(0)
                    for j in range(2):
                        for c in range(FT):
                            n0 = (2 * m + j) * P
                            t = pe.step(G, lambda e: e.matmul(k.t[:, j * T:(j + 1) * T], in_w[:, c, n0:n0 + P], xT[:, c, :],
                                                              start=c == 0, stop=c == FT - 1), [loaded, w_mamba, k.free])
                    if m < 2:
                        t = in_pad = act.step(G, lambda e: e.activation(
                            xx_pad[:, 2 * m:2 * m + 2, TAPS - 1:], halves(k), ACT.Copy), [t, edge] + conv_read)
                    else:
                        t = res_in = act.step(G, lambda e: e.activation(
                            gate[:, 2 * m - 4:2 * m - 2, :], halves(k), ACT.Copy), [t])
                    k.free = t
                    ring.append(k)
                    yield
                for d in range(DT):
                    t = dve.step(G, lambda e: e.tensor_scalar(work[:, d, :], xx_pad[:, d, 0:T], conv_w[:, d, 0:1],
                                                              conv_b[:, d:d + 1], ALU.mult, ALU.add), [in_pad])
                for tap in range(1, TAPS):
                    for d in range(DT):
                        t = dve.step(G, lambda e: e.scalar_tensor_tensor(
                            work[:, d, :], xx_pad[:, d, tap:tap + T], conv_w[:, d, tap:tap + 1], work[:, d, :],
                            ALU.mult, ALU.add), [t])
                    yield
                conv_read[:] = [t]
                gate_ready = act.step(G, lambda e: e.activation(gate[:, :, :], gate[:, :, :], ACT.Silu), [res_in])
                u_ready = act.step(G, lambda e: e.activation(u[:, :, :], work[:, :, :], ACT.Silu), [t, last_scan[0]])
                yield
                k = ring.pop(0)
                for d in range(DT):
                    t = pe.step(G, lambda e: e.matmul(k.t[0:2 * NS + RANK, 0:T], xproj[:, d, :], u[:, d, :],
                                                      start=d == 0, stop=d == DT - 1), [u_ready, k.free])
                yield
                low = act.step(G, lambda e: e.activation(dbc[:, :], k.t[2 * NS:, 0:T][0:RANK], ACT.Copy), [t])
                t = dve.step(G, lambda e: e.tensor_copy(bc3[0:32, :], k.t[0:32, 0:T]), [low])
                t = dve.step(G, lambda e: e.tensor_tensor(bc_rest[:, :], k.t[0:32, 0:T], bc3[0:32, :], ALU.subtract), [t])
                k.free = t
                t = dve.step(G, lambda e: e.tensor_copy(bc_mid[:, :], bc_rest[:, :]), [t])
                dve.step(G, lambda e: e.tensor_copy(bc3[32:64, :], bc_mid[:, :]), [t])
                bc_ready = dve.step(G, lambda e: e.tensor_tensor(bc3[64:96, :], bc_rest[:, :], bc_mid[:, :], ALU.subtract))
                k2 = k
                yield
                yield
                for m in range(2):
                    k = ring.pop(0)
                    for j in range(2):
                        d = 2 * m + j
                        t = pe.step(G, lambda e: e.matmul(k.t[:, j * T:(j + 1) * T], dt_w[:, d * P:(d + 1) * P], dbc[:, :],
                                                          start=True, stop=True), [low, k.free])
                    for j in range(2):
                        d = 2 * m + j
                        ta = act.step(G, lambda e: e.activation(delta[:, d, :], k.t[:, j * T:(j + 1) * T], ACT.Abs,
                                                                bias=dt_b[:, d:d + 1]), [t, last_scan[0]])
                    for j in range(2):
                        d = 2 * m + j
                        tv = dve.step(G, lambda e: e.tensor_scalar(work[:, d, :], k.t[:, j * T:(j + 1) * T],
                                                                   dt_b[:, d:d + 1], 0.0, ALU.add, ALU.max), [t, ta, u_ready])
                    k.free = tv
                    ring.append(k)
                ring.append(k2)
                yield
                t = act.step(G, lambda e: e.activation(delta[:, :, :], delta[:, :, :], ACT.Exp, scale=-1.0), [ta])
                t = act.step(G, lambda e: e.activation(delta[:, :, :], delta[:, :, :], ACT.Ln, bias=one[:, 0:1]), [t, const])
                delta_ready = pool.step(G, lambda e: e.tensor_tensor(delta[:, :, :], delta[:, :, :], work[:, :, :], ALU.add), [t, tv])
                for d in range(DT):
                    t = dve.step(G, lambda e: e.tensor_scalar(work[:, d, :], u[:, d, :], skip_w[:, d:d + 1], None, ALU.mult),
                                 [delta_ready])
                du_ready = pool.step(G, lambda e: e.tensor_tensor(du[:, :, :], delta[:, :, :], u[:, :, :], ALU.mult), [delta_ready, t])
                yield

                while scanning or len(ring) < 5:
                    yield
                scanning.append(b)
                y_banks = [ring.pop(0), ring.pop(0)]
                decay, dbu, scanned, multiplied, summed_y, bank_of = {}, {}, {}, {}, {}, {}
                flat = lambda x: x[:, :, :].rearrange("p d t -> p (d t)")

                def spread(n):
                    k = bank_of[n] = ring.pop(0)
                    for half, row in ((0, n), (1, NS + n)):
                        t = pe.step(G, lambda e: e.matmul(k.t[:, half * T:(half + 1) * T], sel(row), bc3[:, :],
                                                          start=True, stop=True), [bc_ready, consts_ready, k.free])
                    spread_done[n] = t

                def inputs(n):
                    k = bank_of[n]
                    b_copied = act.step(G, lambda e: e.activation(b_all[n % 2][:, :], k.t[:, 0:T], ACT.Copy),
                                        [spread_done[n], dbu.get(n - 2)])
                    dbu[n] = pool.step(G, lambda e: e.tensor_tensor(
                        hs[n % 3][:, :, :], du[:, :, :], b_all[n % 2][:, :].unsqueeze(1).broadcast_to([P, DT, T]), ALU.mult),
                        [b_copied, du_ready, summed_y.get(n - 3, last_y[0])])
                    for d in range(DT):
                        decay[n] = act.step(G, lambda e: e.activation(dA[n % 2][:, d, 1:], delta[:, d, 1:], ACT.Exp,
                                                                      scale=A[:, d, n:n + 1]),
                                            [delta_ready, A_neg, edge, scanned.get(n - 2, last_scan[0])])

                def sum_state(n):
                    for m in range(2):
                        summed_y[n] = pe.step(G, lambda e: e.matmul(
                            y_banks[m].t[:, :], ident[:, :], hs[n % 3][:, 2 * m:2 * m + 2, :].rearrange("p d t -> p (d t)"),
                            start=n == 0, stop=n == NS - 1), [multiplied[n], y_banks[m].free])

                spread_done = {}
                spread(0)
                yield
                inputs(0)
                spread(1)
                yield
                for n in range(NS):
                    k = bank_of[n]
                    if n + 1 < NS:
                        inputs(n + 1)
                    h = hs[n % 3]
                    scanned[n] = dve.step(G, lambda e: e.tensor_tensor_scan(flat(h), flat(dA[n % 2]), flat(h), 0.0,
                                                                            ALU.mult, ALU.add), [decay[n], dbu[n]])
                    multiplied[n] = dve.step(G, lambda e: e.tensor_tensor(
                        h[:, :, :], h[:, :, :], k.t[:, T:2 * T].unsqueeze(1).broadcast_to([P, DT, T]), ALU.mult),
                        [scanned[n]])
                    k.free = multiplied[n]
                    ring.append(k)
                    if n + 2 < NS:
                        spread(n + 2)
                    if n:
                        sum_state(n - 1)
                    yield
                sum_state(NS - 1)
                yield
                scanning.pop()
                last_scan[0], last_y[0] = multiplied[NS - 1], summed_y[NS - 1]
                for m in range(2):
                    t = dve.step(G, lambda e: e.tensor_tensor(work[:, 2 * m:2 * m + 2, :], work[:, 2 * m:2 * m + 2, :],
                                                              halves(y_banks[m]), ALU.add), [summed_y[NS - 1]])
                for k in y_banks:
                    k.free = t
                    ring.append(k)
                t = pool.step(G, lambda e: e.tensor_tensor(work[:, :, :], work[:, :, :], gate[:, :, :], ALU.mult), [t, gate_ready])
                yield
                yield
                k = ring.pop(0)
                for tt in range(TT):
                    for d in range(DT):
                        t2 = pe.step(G, lambda e: e.matmul(k.t[:, tt * D:(tt + 1) * D], work[:, d, tt * P:(tt + 1) * P],
                                                           out_w[:, d, :], start=d == 0, stop=d == DT - 1), [t, k.free])
                yield
                while y_free() is None:
                    yield
                yield from layer_norm(s, k, x[:, :, :], [t2, loaded], x1, x1T, y_free())
                s.out = s.normed

            conv_read, last_scan, last_y = [], [None], [None]
            s.run, s.load = mamba, load
            return s

        def first_attention(name):
            s = Stream(name)
            s.masks_read = None
            s.stats = stats_of(name)
            ctxT = sb("ctxT" + name, [P, FT, T])
            x_sum = sb("x_sum" + name, [P, TT, D])
            s.x_sum_read = []
            proj = sb("proj" + name, [P, FT, T])
            attT = proj
            parts = sb("parts" + name, [P, 3, FT, T], BF16)
            store = sb("store" + name, [P, H * T])
            q_packed, k_packed = (store[0:96, i * H * T // 2:(i + 1) * H * T // 2].bitcast(BF16)
                                  .rearrange("p (h t) -> p h t", t=T) for i in range(2))
            V = sb("V" + name, [P, TT, D])
            Vpad = sb("Vpad" + name, [P, TT, H, P])
            nmax = sb("nmax" + name, [P, TT, H])
            sums = sb("sums" + name, [P, TT, H])
            nlse = sb("nlse" + name, [P, TT, H])
            lseT = sb("lseT" + name, [H, T])
            probs = [sb(f"probs{name}{i}", [P, TT, T]) for i in range(3)]
            probs_read = {}
            dma_store = Dma(sp, "qk_store" + name, new_sem, 1)
            dma_load = {w: Dma(sp, w + "_load" + name, new_sem, 1) for w in "qk"}
            s.stores = [dma_store]
            flag = sb("flag" + name, [P, TT, H])
            v_cols = sb("v_cols" + name, [H, D])
            mask = sb("mask" + name, [P, TT, T], I32)
            maskT = sb("maskT" + name, [P, TT, T], I32)
            hide = sb("hide" + name, [P, TT, T], BF16)
            keepT = sb("keepT" + name, [P, TT, T], BF16)
            negT = sb("negT" + name, [P, TT, T])
            any_kept = sb("any_kept" + name, [P, T])
            pad_read = [None]
            s.x2 = sb("x2" + name, [P, TT, D])
            s.x2T = sb("x2T" + name, [P, FT, T])
            zeroed = pool.step("const", lambda e: e.memset(Vpad[:, :, :, :], 0.0))
            dma_ctx = Dma(sp, "ctx" + name, new_sem, 1)

            def load(b, after):
                return dma_ctx.send([(ctxT[:, :, :], a["ctxT"][b].rearrange("(t p) d -> p t d", p=P)),
                                     (mask[:, :, :], a["mask"][b].rearrange("(t p) d -> p t d", p=P)),
                                     (maskT[:, :, :], a["maskT"][b].rearrange("(t p) d -> p t d", p=P))], after)

            def project(G, w, src, ready, free=()):
                k = ring.pop(0)
                for f in range(FT):
                    for c in range(FT):
                        t = pe.step(G, lambda e: e.matmul(k.t[:, f * T:(f + 1) * T], w[:, c, f * P:(f + 1) * P], src[:, c, :],
                                                          start=c == 0, stop=c == FT - 1), ready + [k.free])
                return k, t

            def project_tokens(G, w, src, ready):
                k = ring.pop(0)
                for tt in range(TT):
                    for c in range(FT):
                        t = pe.step(G, lambda e: e.matmul(k.t[:, tt * D:(tt + 1) * D], src[:, c, tt * P:(tt + 1) * P],
                                                          w[:, c, :], start=c == 0, stop=c == FT - 1), ready + [k.free])
                return k, t

            def pack(G, what, b, w, bias, scale, src, ready, order, packed, packed_free, slot):
                k, t = project(G, w, src, ready)
                for f in range(FT):
                    t = dve.step(G, lambda e: e.tensor_scalar(proj[:, f, :], k.t[:, f * T:(f + 1) * T], bias[:, f:f + 1],
                                                              scale, ALU.add, ALU.mult), [t] + ready + parts_read)
                k.free = t
                ring.append(k)
                t = pool.step(G, lambda e: e.tensor_copy(parts[:, 0, :, :], proj[:, :, :]), [t] + parts_read)
                t = pool.step(G, lambda e: e.tensor_tensor(proj[:, :, :], proj[:, :, :], parts[:, 0, :, :], ALU.subtract), [t])
                t = pool.step(G, lambda e: e.tensor_copy(parts[:, 1, :, :], proj[:, :, :]), [t])
                t = pool.step(G, lambda e: e.tensor_tensor(parts[:, 2, :, :], proj[:, :, :], parts[:, 1, :, :], ALU.subtract), [t])
                yield
                stored = dma_store.send(
                    [(scratch_q[b, slot, s].rearrange("(k p) t -> p k t", k=FT), parts[:, s, :, :]) for s in range(3)], [t])
                parts_read[:] = [stored]
                loaded = dma_load[what].send(
                    [(packed[r * HD:(r + 1) * HD, :, :], scratch_q[b, slot, s].rearrange("(c e) t -> e c t", e=HD))
                     for r, s in enumerate(order)], [stored] + packed_free)
                packed_ready[what] = loaded
                yield
                yield

            parts_read, packed_ready = [], {}
            softmaxed = [None]

            def turn_lse(G, heads, t):
                yield
                yield
                k = ring.pop(0)
                for q in range(TT):
                    t2 = pe.step(G, lambda e: e.transpose(k.t[0:heads, q * P:(q + 1) * P], nlse[:, q, 0:heads], ident[:, :]),
                                 [t, k.free])
                yield
                t2 = dve.step(G, lambda e: e.tensor_copy(lseT[0:heads, :], k.t[0:heads, 0:T]), [t2])
                k.free = t2
                ring.append(k)
                return t2

            def split_lse(G, heads, t):
                t = dve.step(G, lambda e: e.tensor_copy(lse3[0:heads, :], lseT[0:heads, :]), [t, const])
                t = dve.step(G, lambda e: e.tensor_tensor(lseT[0:heads, :], lseT[0:heads, :], lse3[0:heads, :], ALU.subtract), [t])
                t = dve.step(G, lambda e: e.tensor_copy(lse_mid[0:heads, :], lseT[0:heads, :]), [t])
                dve.step(G, lambda e: e.tensor_copy(lse3[32:32 + heads, :], lse_mid[0:heads, :]), [t])
                return dve.step(G, lambda e: e.tensor_tensor(lse3[64:64 + heads, :], lseT[0:heads, :], lse_mid[0:heads, :],
                                                             ALU.subtract))

            def tokens_of(G, w, bias_row, src, ready, x_old, t_x):
                biased = pool.step(G, lambda e: e.tensor_tensor(
                    x_sum[:, :, :], x_old[:, :, :], bias_row[:, :].unsqueeze(1).broadcast_to([P, TT, D]), ALU.add),
                    [t_x] + ready + s.x_sum_read)
                k, t = project_tokens(G, w, src, ready)
                return k, t, biased

            def xattn0(b, ctx_ready, x_ready, xT_ready, x, xT, y, yT, y_free):
                G = "x0" + s.name
                t = dve.step(G, lambda e: e.tensor_scalar(hide[:, :, :], mask[:, :, :], 0.0, HIDE, ALU.is_equal, ALU.mult), [ctx_ready])
                hide_ready = t
                keep_ready = dve.step(G, lambda e: e.tensor_scalar(keepT[:, :, :], maskT[:, :, :], 0.0, None, ALU.not_equal), [ctx_ready])
                k = ring.pop(0)
                for c in range(TT):
                    t = pe.step(G, lambda e: e.matmul(k.t[:, 0:T], onesb[:, :], keepT[:, c, :], start=c == 0, stop=c == TT - 1),
                                [keep_ready, const, k.free])
                t = dve.step(G, lambda e: e.tensor_scalar(any_kept[:, :], k.t[:, 0:T], 0.0, NEG, ALU.is_gt, ALU.mult), [t])
                k.free = t
                ring.append(k)
                for c in range(TT):
                    neg_ready = dve.step(G, lambda e: e.scalar_tensor_tensor(
                        negT[:, c, :], maskT[:, c, :], 0.0, any_kept[:, :], ALU.is_equal, ALU.mult), [t])
                s.masks_read = neg_ready
                yield
                yield from pack(G, "k", b, xw["0k"], xw["0bk"], 1.0, ctxT, [ctx_ready, w_xattn], PARTS_K, k_packed,
                                [softmaxed[0]], 0)
                yield from pack(G, "q", b, xw["0q"], xw["0bq"], HD ** -0.5, xT, [xT_ready, w_xattn], PARTS_Q, q_packed,
                                [softmaxed[0]], 1)
                k, t = project_tokens(G, xw["0v"], ctxT, [ctx_ready, w_xattn])
                t = dve.step(G, lambda e: e.tensor_tensor(V[:, :, :], halves(k), xw["0bv"][:, :].unsqueeze(1).broadcast_to([P, TT, D]),
                                                          ALU.add), [t, w_xattn])
                k.free = v_ready = s.ctx_read = t
                ring.append(k)
                for c in range(TT):
                    for f in range(FT):
                        half = Vpad[:, c, 8 * f:8 * f + 8, :].rearrange("p h n -> p (h n)")
                        for j in range(8):
                            pad_ready = pool.step(G, lambda e: e.tensor_copy(
                                Vpad[:, c, 8 * f + j, j * HD:(j + 1) * HD], V[:, c, f * P + j * HD:f * P + (j + 1) * HD]),
                                [v_ready, zeroed, pad_read[0]])
                k = ring.pop(0)
                for c in range(TT):
                    t = pe.step(G, lambda e: e.matmul(k.t[0:H, 0:D], ones16[:, :], V[:, c, :], start=c == 0, stop=c == TT - 1),
                                [v_ready, k.free, const])
                cols_ready = dve.step(G, lambda e: e.tensor_tensor(v_cols[:, :], k.t[0:H, 0:D], head_block[:, :], ALU.mult), [t])
                k.free = cols_ready
                ring.append(k)
                yield
                for h in range(H):
                    k = ring.pop(0)
                    for q in range(TT):
                        dst = k.t[:, q * T:(q + 1) * T]
                        pe.step(G, lambda e: e.matmul(dst, q_packed[:, h, q * P:(q + 1) * P], k_packed[:, h, :], start=True, stop=False),
                                [packed_ready["q"], packed_ready["k"], k.free])
                        t = pe.step(G, lambda e: e.matmul(dst, identb[:, :], hide[:, q, :], start=False, stop=True), [hide_ready])
                    t = dve.step(G, lambda e: e.tensor_reduce(nmax[:, :, h], halves(k), AX.X, ALU.max, negate=True), [t])
                    for q in range(TT):
                        t2 = act.step(G, lambda e: e.activation(k.t[:, q * T:(q + 1) * T], k.t[:, q * T:(q + 1) * T], ACT.Exp,
                                                                bias=nmax[:, q, h:h + 1], accum_out=sums[:, q, h:h + 1]), [t])
                    k.free = t2
                    ring.append(k)
                    yield
                ln = act.step(G, lambda e: e.activation(sums[:, :, :], sums[:, :, :], ACT.Ln), [t2])
                t = dve.step(G, lambda e: e.scalar_tensor_tensor(flag[:, :, :], nmax[:, :, :], -HIDE / 2, nmax[:, :, :],
                                                                 ALU.is_lt, ALU.mult), [t2])
                t = dve.step(G, lambda e: e.tensor_tensor(nlse[:, :, :], flag[:, :, :], sums[:, :, :], ALU.subtract), [ln, t])
                t = yield from turn_lse(G, H, t)
                lse_ready = t
                yield
                acc = ring.pop(0)
                scored = {}

                def score(h):
                    k = ring.pop(0)
                    for c in range(TT):
                        t = pe.step(G, lambda e: e.matmul(k.t[:, c * T:(c + 1) * T], k_packed[:, h, c * P:(c + 1) * P],
                                                          q_packed[:, h, :], start=True, stop=True), [k.free])
                    softmaxed[0] = t
                    scored[h] = dve.step(G, lambda e: e.tensor_tensor(probs[h % 3][:, :, :], halves(k), keepT[:, :, :], ALU.mult),
                                         [t, probs_read.get(h % 3)])
                    k.free = scored[h]
                    ring.append(k)

                score(0)
                score(1)
                yield
                for f in range(FT):
                    dst = acc.t[:, f * T:(f + 1) * T]
                    for c in range(TT):
                        pe.step(G, lambda e: e.matmul(dst, V[:, c, f * P:(f + 1) * P], negT[:, c, :], start=c == 0, stop=False),
                                [acc.free, neg_ready, v_ready])
                    pe.step(G, lambda e: e.matmul(dst, v_cols[:, f * P:(f + 1) * P], lseT[:, :], start=False, stop=False),
                            [lse_ready, cols_ready])
                    for h in range(8 * f, 8 * f + 8):
                        if h + 2 < H:
                            score(h + 2)
                        for c in range(TT):
                            t = pe.step(G, lambda e: e.matmul(dst, Vpad[:, c, h, :], probs[h % 3][:, c, :], start=False,
                                                              stop=h == 8 * f + 7 and c == TT - 1), [scored[h], pad_ready])
                        probs_read[h % 3] = t
                        yield
                pad_read[0] = t
                t = act.step(G, lambda e: e.activation(attT[:, :, :], halves(acc), ACT.Copy), [t])
                acc.free = t
                ring.append(acc)
                k, t, biased = tokens_of(G, xw["0o"], xw["0bo"], attT, [t, w_xattn], x, x_ready)
                s.x1_read = biased
                yield from layer_norm(s, k, x_sum[:, :, :], [t, biased], y, yT, y_free)
                s.x_sum_read[:] = [s.normed[0]]
            s.run, s.load, s.store = xattn0, load, store
            return s

        route_read = [None]

        def route(buffers, G, n, xT, gate_w, bias, ready):
            logits, top, top_i, top_f, wts, comb, comb2, padded = buffers
            k = ring.pop(0)
            for tt in range(TT):
                for c in range(FT):
                    t = route_read[0] = pe.step(G, lambda e: e.matmul(
                        k.t[:, tt * 8:tt * 8 + n], xT[:, c, tt * P:(tt + 1) * P], gate_w[:, c, :],
                        start=c == 0, stop=c == FT - 1), ready + [k.free])
            src = k.t[:, 0:16].rearrange("p (t n) -> p t n", t=TT)[:, :, 0:n]
            if bias is None:
                t = dve.step(G, lambda e: e.tensor_copy(logits[:, :, 0:n], src), [t, padded])
            else:
                t = dve.step(G, lambda e: e.tensor_tensor(
                    logits[:, :, 0:n], src, bias[:, :].unsqueeze(1).broadcast_to([P, TT, n]), ALU.add), [t, padded])
            k.free = t
            ring.append(k)
            for tt in range(TT):
                t = dve.step(G, lambda e: e.max(top[:, tt, :], logits[:, tt, :]), [t])
            for tt in range(TT):
                t = dve.step(G, lambda e: e.max_index(top_i[:, tt, :], top[:, tt, :], logits[:, tt, :]), [t])
            t = dve.step(G, lambda e: e.tensor_copy(top_f[:, :, :], top_i[:, :, 0:2]), [t])
            t2 = dve.step(G, lambda e: e.tensor_tensor(wts[:, :, 0:1], top[:, :, 1:2], top[:, :, 0:1], ALU.subtract))
            t2 = act.step(G, lambda e: e.activation(wts[:, :, 1:2], wts[:, :, 0:1], ACT.Exp), [t2])
            t2 = dve.step(G, lambda e: e.tensor_scalar(wts[:, :, 2:3], wts[:, :, 1:2], 1.0, None, ALU.add), [t2])
            t2 = dve.step(G, lambda e: e.reciprocal(wts[:, :, 2:3], wts[:, :, 2:3]), [t2])
            t2 = dve.step(G, lambda e: e.tensor_tensor(wts[:, :, 3:4], wts[:, :, 1:2], wts[:, :, 2:3], ALU.mult), [t2])
            for tt in range(TT):
                dve.step(G, lambda e: e.tensor_scalar(comb[:, tt, :], iota[:, :], top_f[:, tt, 0:1], wts[:, tt, 2:3],
                                                      ALU.is_equal, ALU.mult), [t, t2])
                t3 = dve.step(G, lambda e: e.tensor_scalar(comb2[:, tt, :], iota[:, :], top_f[:, tt, 1:2], wts[:, tt, 3:4],
                                                           ALU.is_equal, ALU.mult), [])
            return dve.step(G, lambda e: e.tensor_tensor(comb[:, :, :], comb[:, :, :], comb2[:, :, :], ALU.add), [t3])

        def late_stages(name):
            s = Stream(name)
            s.ctx_read = None
            s.stats = stats_of(name)
            s.routing = routing_of(name)
            ctxT = sb("ctxT" + name, [P, FT, T])
            x_sum = sb("x_sum" + name, [P, TT, D])
            s.x_sum_read = []
            proj = sb("proj" + name, [P, FT, T])
            attT = proj
            parts = sb("parts" + name, [P, 3, FT, T], BF16)
            store = sb("store" + name, [P, H * T])
            q_packed, k_packed = (store[0:96, i * H * T // 2:(i + 1) * H * T // 2].bitcast(BF16)
                                  .rearrange("p (h t) -> p h t", t=T) for i in range(2))
            V = sb("V" + name, [P, TT, D])
            Vpad = sb("Vpad" + name, [P, TT, H, P])
            nmax = sb("nmax" + name, [P, TT, H])
            sums = sb("sums" + name, [P, TT, H])
            nlse = sb("nlse" + name, [P, TT, H])
            lseT = sb("lseT" + name, [H, T])
            probs = [sb(f"probs{name}{i}", [P, TT, T]) for i in range(3)]
            probs_read = {}
            dma_store = Dma(sp, "qk_store" + name, new_sem, 1)
            dma_load = {w: Dma(sp, w + "_load" + name, new_sem, 1) for w in "qk"}
            s.stores = [dma_store]
            xs = [sb(f"xs{name}{i}", [P, TT, D]) for i in range(2)]
            xsT = [sb(f"xsT{name}{i}", [P, FT, T]) for i in range(2)]
            Vb = sb("Vb" + name, [P, 2 * H, HD])
            lse3 = sb("lse3" + name, [96, T], BF16)
            lse_mid = sb("lse_mid" + name, [H, T], BF16)
            const = pool.step("const", lambda e: e.memset(lse3[:, :], 0.0))
            raw = {w: Vpad[0:96, c, :, :].rearrange("p h n -> p (h n)").bitcast(BF16).rearrange("p (h t) -> p h t", t=T)
                   for c, w in enumerate("qk")}
            blkT = Vpad[0:HD, :, :, :].rearrange("p c h n -> p (c h n)").rearrange("p (h t) -> p h t", t=T)
            K4 = sb("K4" + name, [P, GKV, T])
            VL = sb("VL" + name, [P, TT, GKV * LAT])
            combT = sb("combT" + name, [8, T])
            hid = [store[:, i * FT * T:(i + 1) * FT * T].rearrange("p (k t) -> p k t", t=T) for i in range(E0 + 1)]
            vb_read, blk_read = [None], []
            dma_x2 = Dma(sp, "x2" + name, new_sem, 1)
            dma_ctx = Dma(sp, "ctx" + name, new_sem, 1)
            dma_v_store, dma_v_load, dma_o_store, dma_o_load, dma_x5 = (
                Dma(sp, n + name, new_sem, 1) for n in ("v_store", "v_load", "o_store", "o_load", "x5_store"))
            s.stores += [dma_v_store, dma_o_store, dma_x5]

            def project(G, w, src, ready, free=()):
                k = ring.pop(0)
                for f in range(FT):
                    for c in range(FT):
                        t = pe.step(G, lambda e: e.matmul(k.t[:, f * T:(f + 1) * T], w[:, c, f * P:(f + 1) * P], src[:, c, :],
                                                          start=c == 0, stop=c == FT - 1), ready + [k.free])
                return k, t

            def project_tokens(G, w, src, ready):
                k = ring.pop(0)
                for tt in range(TT):
                    for c in range(FT):
                        t = pe.step(G, lambda e: e.matmul(k.t[:, tt * D:(tt + 1) * D], src[:, c, tt * P:(tt + 1) * P],
                                                          w[:, c, :], start=c == 0, stop=c == FT - 1), ready + [k.free])
                return k, t

            def pack(G, what, b, w, bias, scale, src, ready, order, packed, packed_free, slot):
                k, t = project(G, w, src, ready)
                for f in range(FT):
                    t = dve.step(G, lambda e: e.tensor_scalar(proj[:, f, :], k.t[:, f * T:(f + 1) * T], bias[:, f:f + 1],
                                                              scale, ALU.add, ALU.mult), [t] + ready + parts_read)
                k.free = t
                ring.append(k)
                t = pool.step(G, lambda e: e.tensor_copy(parts[:, 0, :, :], proj[:, :, :]), [t] + parts_read)
                t = pool.step(G, lambda e: e.tensor_tensor(proj[:, :, :], proj[:, :, :], parts[:, 0, :, :], ALU.subtract), [t])
                t = pool.step(G, lambda e: e.tensor_copy(parts[:, 1, :, :], proj[:, :, :]), [t])
                t = pool.step(G, lambda e: e.tensor_tensor(parts[:, 2, :, :], proj[:, :, :], parts[:, 1, :, :], ALU.subtract), [t])
                yield
                stored = dma_store.send(
                    [(scratch_q[b, slot, s].rearrange("(k p) t -> p k t", k=FT), parts[:, s, :, :]) for s in range(3)], [t])
                parts_read[:] = [stored]
                loaded = dma_load[what].send(
                    [(packed[r * HD:(r + 1) * HD, :, :], scratch_q[b, slot, s].rearrange("(c e) t -> e c t", e=HD))
                     for r, s in enumerate(order)], [stored] + packed_free)
                packed_ready[what] = loaded
                yield
                yield

            parts_read, packed_ready = [], {}
            softmaxed = [None]

            def turn_lse(G, heads, t):
                yield
                yield
                k = ring.pop(0)
                for q in range(TT):
                    t2 = pe.step(G, lambda e: e.transpose(k.t[0:heads, q * P:(q + 1) * P], nlse[:, q, 0:heads], ident[:, :]),
                                 [t, k.free])
                yield
                t2 = dve.step(G, lambda e: e.tensor_copy(lseT[0:heads, :], k.t[0:heads, 0:T]), [t2])
                k.free = t2
                ring.append(k)
                return t2

            def split_lse(G, heads, t):
                t = dve.step(G, lambda e: e.tensor_copy(lse3[0:heads, :], lseT[0:heads, :]), [t, const])
                t = dve.step(G, lambda e: e.tensor_tensor(lseT[0:heads, :], lseT[0:heads, :], lse3[0:heads, :], ALU.subtract), [t])
                t = dve.step(G, lambda e: e.tensor_copy(lse_mid[0:heads, :], lseT[0:heads, :]), [t])
                dve.step(G, lambda e: e.tensor_copy(lse3[32:32 + heads, :], lse_mid[0:heads, :]), [t])
                return dve.step(G, lambda e: e.tensor_tensor(lse3[64:64 + heads, :], lseT[0:heads, :], lse_mid[0:heads, :],
                                                             ALU.subtract))

            def tokens_of(G, w, bias_row, src, ready, x_old, t_x):
                biased = pool.step(G, lambda e: e.tensor_tensor(
                    x_sum[:, :, :], x_old[:, :, :], bias_row[:, :].unsqueeze(1).broadcast_to([P, TT, D]), ALU.add),
                    [t_x] + ready + s.x_sum_read)
                k, t = project_tokens(G, w, src, ready)
                return k, t, biased

            def ffn0(b, x_ready, xT_ready, x, xT, y, yT, y_free):
                G = "f0" + s.name
                E = E0 + 1
                comb = s.routing[5]
                routed = route(s.routing, G, E0, xT, gate0, gbias, [xT_ready, w_route])
                routed = dve.step(G, lambda e: e.memset(comb[:, :, E0:E], 1.0), [routed])
                yield
                k = ring.pop(0)
                for tt in range(TT):
                    t = pe.step(G, lambda e: e.transpose(k.t[0:E, tt * P:(tt + 1) * P], comb[:, tt, :], ident[:, :]),
                                [routed, k.free])
                turned = dve.step(G, lambda e: e.tensor_copy(combT[:, :], k.t[0:E, 0:T]), [t])
                k.free = turned
                ring.append(k)
                hidden = {}

                def up(j):
                    k = ring.pop(0)
                    for f in range(FT):
                        for c in range(FT):
                            t = pe.step(G, lambda e: e.matmul(k.t[:, f * T:(f + 1) * T], w1_0[:, j, c, f * P:(f + 1) * P],
                                                              xT[:, c, :], start=c == 0, stop=c == FT - 1),
                                        [xT_ready, w_ffn0[j], k.free])
                    for f in range(FT):
                        hidden[j] = act.step(G, lambda e: e.activation(hid[j][:, f, :], k.t[:, f * T:(f + 1) * T], ACT.Gelu,
                                                                       bias=b1_0[:, j, f:f + 1]),
                                             [t, softmaxed[0]])
                    k.free = hidden[j]
                    ring.append(k)

                for j in range(E):
                    up(j)
                k = ring.pop(0)
                for tt in range(TT):
                    t = pe.step(G, lambda e: e.matmul(k.t[:, tt * D:(tt + 1) * D], combT[:, tt * P:(tt + 1) * P], b2_0[:, :],
                                                      start=True, stop=True), [turned, w_route, k.free])
                t = dve.step(G, lambda e: e.tensor_tensor(x_sum[:, :, :], halves(k), x[:, :, :], ALU.add), [t, x_ready] + s.x_sum_read)
                k.free = t
                ring.append(k)
                yield
                for j in range(E):
                    k = ring.pop(0)
                    for tt in range(TT):
                        for f in range(FT):
                            t2 = pe.step(G, lambda e: e.matmul(k.t[:, tt * D:(tt + 1) * D], hid[j][:, f, tt * P:(tt + 1) * P],
                                                               w2_0[:, j, f, :], start=f == 0, stop=f == FT - 1),
                                         [hidden[j], k.free])
                    if j < E - 1:
                        for tt in range(TT):
                            t = dve.step(G, lambda e: e.scalar_tensor_tensor(
                                x_sum[:, tt, :], k.t[:, tt * D:(tt + 1) * D], comb[:, tt, j:j + 1], x_sum[:, tt, :],
                                ALU.mult, ALU.add), [t2, t])
                        k.free = t
                        ring.append(k)
                    yield
                yield from layer_norm(s, k, x_sum[:, :, :], [t2, t], y, yT, y_free)
                s.x_sum_read[:] = [s.normed[0]]

            def gqa(b, x_ready, xT_ready, x, xT, y, yT):
                G = "g1" + s.name
                k, t = project(G, Wqk, xT, [xT_ready, fold_done])
                q_ready = act.step(G, lambda e: e.activation(proj[:, :, :], halves(k), ACT.Copy, scale=GHD ** -0.5), [t] + parts_read)
                k.free = q_ready
                ring.append(k)
                k = ring.pop(0)
                for g in range(GKV):
                    for c in range(FT):
                        t = pe.step(G, lambda e: e.matmul(k.t[:, g * T:(g + 1) * T],
                                                          kdown4[:, c, g, :, :].rearrange("p r l -> p (r l)"), xT[:, c, :],
                                                          start=c == 0, stop=c == FT - 1), [xT_ready, kdown4_done, k.free])
                k_ready = act.step(G, lambda e: e.activation(K4[:, :, :], halves(k), ACT.Copy), [t])
                k.free = k_ready
                ring.append(k)
                k = ring.pop(0)
                W = GKV * LAT
                for tt in range(TT):
                    for c in range(FT):
                        t = pe.step(G, lambda e: e.matmul(k.t[:, tt * W:(tt + 1) * W], xT[:, c, tt * P:(tt + 1) * P], vdown[:, c, :],
                                                          start=c == 0, stop=c == FT - 1), [k.free])
                v_ready = act.step(G, lambda e: e.activation(
                    VL[:, :, :], k.t[:, 0:TT * W].rearrange("p (t n) -> p t n", t=TT), ACT.Copy), [t])
                k.free = v_ready
                ring.append(k)
                yield
                for h in range(GH):
                    r, g = 32 * (h % 4), h // 4
                    k = ring.pop(0)
                    for q, at, n in ((0, 0, P), (1, P, T)):
                        pe.step(G, lambda e: e.matmul(k.t[:, at:at + n], proj[r:r + LAT, g, q * P:(q + 1) * P], K4[r:r + LAT, g, 0:n],
                                                      start=True, stop=False), [q_ready, k_ready, k.free])
                        t = pe.step(G, lambda e: e.matmul(k.t[:, at + n - P:at + n], identb[:, :], causal[:, :], start=False, stop=True))
                    for q, at, n in ((0, 0, P), (1, P, T)):
                        t2 = dve.step(G, lambda e: e.tensor_reduce(nmax[:, q, h:h + 1], k.t[:, at:at + n], AX.X, ALU.max, negate=True), [t])
                    for q, at, n in ((0, 0, P), (1, P, T)):
                        t3 = act.step(G, lambda e: e.activation(k.t[:, at:at + n], k.t[:, at:at + n], ACT.Exp, bias=nmax[:, q, h:h + 1],
                                                                accum_out=sums[:, q, h:h + 1]), [t2])
                    k.free = t3
                    ring.append(k)
                    if h % 2:
                        yield
                ln = act.step(G, lambda e: e.activation(sums[:, :, 0:GH], sums[:, :, 0:GH], ACT.Ln), [t3])
                t = dve.step(G, lambda e: e.tensor_tensor(nlse[:, :, 0:GH], nmax[:, :, 0:GH], sums[:, :, 0:GH], ALU.subtract), [ln])
                t = yield from turn_lse(G, GH, t)
                lse_ready = split_lse(G, GH, t)
                yield
                acc = ring.pop(0)
                ready = {}

                def score(h):
                    r, g = 32 * (h % 4), h // 4
                    k = ring.pop(0)
                    for c, at, q0 in ((0, 0, 0), (1, T, P)):
                        n = T - q0
                        pe.step(G, lambda e: e.matmul(k.t[:, at:at + n], K4[r:r + LAT, g, c * P:(c + 1) * P], proj[r:r + LAT, g, q0:T],
                                                      start=True, stop=False), [k.free])
                        pe.step(G, lambda e: e.matmul(k.t[:, at:at + P], identb[:, :], causalT[:, :], start=False, stop=False))
                        t = pe.step(G, lambda e: e.matmul(k.t[:, at:at + n], sel(h), lse3[:, q0:T], start=False, stop=True), [lse_ready])
                    flat = probs[h % 3][:, :, :].rearrange("p c t -> p (c t)")
                    ready[h] = act.step(G, lambda e: e.activation(flat[:, 0:T + P], k.t[:, 0:T + P], ACT.Exp), [t, probs_read.get(h % 3)])
                    k.free = ready[h]
                    ring.append(k)

                score(0)
                score(1)
                yield
                for h in range(GH):
                    r, g = 32 * (h % 4), h // 4
                    if h + 2 < GH:
                        score(h + 2)
                    flat = probs[h % 3][:, :, :].rearrange("p c t -> p (c t)")
                    pe.step(G, lambda e: e.matmul(acc.t[r:r + LAT, g * T:(g + 1) * T], VL[:, 0, g * LAT:(g + 1) * LAT], flat[:, 0:T],
                                                  start=True, stop=False), [ready[h], v_ready, acc.free])
                    t = pe.step(G, lambda e: e.matmul(acc.t[r:r + LAT, g * T + P:(g + 1) * T], VL[:, 1, g * LAT:(g + 1) * LAT],
                                                      flat[:, T:T + P], start=False, stop=True))
                    probs_read[h % 3] = t
                    yield
                t = act.step(G, lambda e: e.activation(attT[:, :, :], halves(acc), ACT.Copy), [t])
                acc.free = t
                ring.append(acc)
                k, t = project_tokens(G, Wvo, attT, [t])
                yield from layer_norm(s, k, x[:, :, :], [t, x_ready], y, yT, [])

            def xattn1(b, ctx_ready, x_ready, xT_ready, x, xT, y, yT):
                G = "x1" + s.name
                BT = T // H
                HT = BT // 2
                k, t = project_tokens(G, xw["1v"], ctxT, [w_xattn, ctx_ready])
                t = dve.step(G, lambda e: e.tensor_tensor(V[:, :, :], halves(k), xw["1bv"][:, :].unsqueeze(1).broadcast_to([P, TT, D]),
                                                          ALU.add), [t, w_xattn])
                k.free = t
                ring.append(k)
                stored = dma_v_store.send([(scratch_v[b].rearrange("(t p) d -> p t d", p=P), V[:, :, :])], [t])
                v_ready = dma_v_load.send(
                    [(Vb[c * HT:(c + 1) * HT, :, :],
                      scratch_v[b].rearrange("(j t) (c e) -> c t j e", t=HT, e=HD)[c]) for c in range(H)], [stored, vb_read[0]])
                yield
                yield from pack(G, "k", b, xw["1k"], xw["1bk"], 1.0, ctxT, [w_xattn, ctx_ready], PARTS_K, raw["k"], blk_read, 2)
                s.ctx_read = parts_read[0]
                yield from pack(G, "q", b, xw["1q"], xw["1bq"], HD ** -0.5, xT, [xT_ready, w_xattn], PARTS_Q, raw["q"],
                                blk_read, 3)
                for what, packed in (("k", k_packed), ("q", q_packed)):
                    for tile in range(2):
                        ordered = dve.step(G, lambda e: e.tensor_copy(
                            packed[:, :, tile * P:(tile + 1) * P].rearrange("p h (c t) -> p h c t", t=HT),
                            raw[what][:, :, :].rearrange("p c (h i t) -> p h i c t", h=H, i=2)[:, :, tile]),
                            [packed_ready[what], softmaxed[0]])
                yield

                for h in range(H):
                    k = ring.pop(0)
                    for q, at, n in ((0, 0, P), (1, P, T)):
                        pe.step(G, lambda e: e.matmul(k.t[:, at:at + n], q_packed[:, h, q * P:(q + 1) * P], k_packed[:, h, 0:n],
                                                      start=True, stop=False), [ordered, k.free])
                        t = pe.step(G, lambda e: e.matmul(k.t[:, at + n - P:at + n], identb[:, :], bcausal[:, :], start=False, stop=True))
                    for q, at, n in ((0, 0, P), (1, P, T)):
                        t2 = dve.step(G, lambda e: e.tensor_reduce(nmax[:, q, h:h + 1], k.t[:, at:at + n], AX.X, ALU.max, negate=True), [t])
                    for q, at, n in ((0, 0, P), (1, P, T)):
                        t3 = act.step(G, lambda e: e.activation(k.t[:, at:at + n], k.t[:, at:at + n], ACT.Exp, bias=nmax[:, q, h:h + 1],
                                                                accum_out=sums[:, q, h:h + 1]), [t2])
                    k.free = t3
                    ring.append(k)
                    yield
                ln = act.step(G, lambda e: e.activation(sums[:, :, :], sums[:, :, :], ACT.Ln), [t3])
                t = dve.step(G, lambda e: e.tensor_tensor(nlse[:, :, :], nmax[:, :, :], sums[:, :, :], ALU.subtract), [ln])
                t = yield from turn_lse(G, H, t)
                lse_ready = split_lse(G, H, t)
                yield
                ready = {}

                def score(h):
                    k = ring.pop(0)
                    for c, at, q0 in ((0, 0, 0), (1, T, P)):
                        n = T - q0
                        pe.step(G, lambda e: e.matmul(k.t[:, at:at + n], k_packed[:, h, c * P:(c + 1) * P], q_packed[:, h, q0:T],
                                                      start=True, stop=False), [k.free])
                        pe.step(G, lambda e: e.matmul(k.t[:, at:at + P], identb[:, :], bcausalT[:, :], start=False, stop=False))
                        t = pe.step(G, lambda e: e.matmul(k.t[:, at:at + n], sel(h), lse3[:, q0:T], start=False, stop=True), [lse_ready])
                    softmaxed[0] = t
                    flat = probs[h % 3][:, :, :].rearrange("p c t -> p (c t)")
                    ready[h] = act.step(G, lambda e: e.activation(flat[:, 0:T + P], k.t[:, 0:T + P], ACT.Exp), [t, probs_read.get(h % 3)])
                    k.free = ready[h]
                    ring.append(k)

                score(0)
                score(1)
                yield
                for h in range(H):
                    if h + 2 < H:
                        score(h + 2)
                    if h % 2 == 0:
                        acc = ring.pop(0)
                    at = (h % 2) * T
                    flat = probs[h % 3][:, :, :].rearrange("p c t -> p (c t)")
                    pe.step(G, lambda e: e.matmul(acc.t[0:HD, at:at + T], Vb[:, 2 * h, :], flat[:, 0:T], start=True, stop=False),
                            [ready[h], v_ready, acc.free])
                    t = pe.step(G, lambda e: e.matmul(acc.t[0:HD, at + P:at + T], Vb[:, 2 * h + 1, :], flat[:, T:T + P],
                                                      start=False, stop=True))
                    probs_read[h % 3] = t
                    if h % 2:
                        t = act.step(G, lambda e: e.activation(
                            blkT[:, :, (h - 1) * BT:(h + 1) * BT].rearrange("p c (i t) -> p c i t", t=HT),
                            acc.t[0:HD, :].rearrange("p (i c t) -> p c i t", c=H, t=HT), ACT.Copy), [t, ordered])
                        acc.free = t
                        ring.append(acc)
                    yield
                vb_read[0] = probs_read[(H - 1) % 3]
                stored = dma_o_store.send([(scratch_o[b].rearrange("(c e) t -> e c t", e=HD), blkT[:, :, :])], [t])
                blk_read[:] = [stored]
                t = dma_o_load.send([(attT[:, :, :], scratch_o[b].rearrange("(k p) t -> p k t", k=FT))], [stored])
                yield
                k, t, biased = tokens_of(G, xw["1o"], xw["1bo"], attT, [t, w_xattn], x, x_ready)
                yield from layer_norm(s, k, x_sum[:, :, :], [t, biased], y, yT, [])
                s.x_sum_read[:] = [s.normed[0]]

            def run(b, after):
                ready = dma_x2.send([(xs[0][:, :, :], scratch_x2[b].rearrange("(t p) d -> p t d", p=P)),
                                     (xsT[0][:, :, :], scratch_x2T[b].rearrange("(k p) t -> p k t", p=P))],
                                    after + list(s.normed or ()))
                ctx_ready = dma_ctx.send([(ctxT[:, :, :], a["ctxT"][b].rearrange("(t p) d -> p t d", p=P))], [s.ctx_read])
                yield from ffn0(b, ready, ready, xs[0], xsT[0], xs[1], xsT[1], [x5_stored[0]])
                yield from gqa(b, *s.normed, xs[1], xsT[1], xs[0], xsT[0])
                yield from xattn1(b, ctx_ready, *s.normed, xs[0], xsT[0], xs[1], xsT[1])
                x5_stored[0] = dma_x5.send([(scratch_x[b].rearrange("(t p) d -> p t d", p=P), xs[1][:, :, :]),
                                            (scratch_xT[b].rearrange("(k p) t -> p k t", p=P), xsT[1][:, :, :])],
                                           list(s.normed))
                s.stored = x5_stored[0]
                yield

            x5_stored = [None]
            s.store, s.run = store, run
            return s

        mambas = [mamba_stream("A"), mamba_stream("B")]
        first = first_attention("C")
        x_loaded = {0: mambas[0].load(0, [])}
        w_mamba = dma_w["mamba"].send([l1, l2, l3, l4, l5, l6, l7, l8, l9])
        consts_raw = first.store[:, 0:5 * P + 32]
        consts_loaded = dma_w["fold"].send([(consts_raw, a["consts"])])
        x_loaded[1] = mambas[1].load(1, [])
        ctx_loaded = first.load(0, [])
        w_xattn = dma_w["x0"].send(xloads)
        consts_ready = dve.step("const", lambda e: e.tensor_copy(consts[:, :], consts_raw), [consts_loaded])
        for t, value in ((one, 1.0), (ones16, 1.0), (onesb, 1.0)):
            const = pool.step("const", lambda e: e.memset(t[:, :], value))
        A_exp = act.step("const", lambda e: e.activation(A[:, :, :], A[:, :, :], ACT.Exp), [w_mamba])
        A_neg = pool.step("const", lambda e: e.tensor_scalar(A[:, :, :], A[:, :, :], -1.0, None, ALU.mult), [A_exp])

        dma_x2 = Dma(sp, "x2_store", new_sem, 2)
        x1_read = {}
        x2_stored, x2_out = {}, [None]

        def mamba_of(i):
            for b in range(i, BATCH, 2):
                yield from mambas[i].run(b, x_loaded[b], lambda: x1_read.get(b - 2) if b >= 2 else [])
                m_out[b] = mambas[i].out
                if b + 2 < BATCH:
                    x_loaded[b + 2] = mambas[i].load(b + 2, list(mambas[i].out))
                yield

        def attention_0():
            ctx_ready = ctx_loaded
            for b in range(BATCH):
                while b not in m_out:
                    yield
                m = mambas[b % 2]
                yield from first.run(b, ctx_ready, *m_out[b], m.x1, m.x1T, first.x2, first.x2T, [x2_out[0]])
                x1_read[b] = [first.x1_read]
                x2_stored[b] = x2_out[0] = dma_x2.send(
                    [(rows_of(scratch_x2[b]), first.x2[:, :, :]), (rows_of(scratch_x2T[b]), first.x2T[:, :, :])],
                    list(first.normed))
                if b + 1 < BATCH:
                    ctx_ready = first.load(b + 1, [first.masks_read, first.ctx_read])
                yield

        m_out = {}
        interleave([(mamba_of(0), 0, 1), (mamba_of(1), MAMBA_LAG, 1), (attention_0(), 0, 2)])

        phase_1_done = next_phase([dma_x2] + first.stores)
        E = E0 + 1
        w1_0 = sb("w1_0", [P, E, FT, D])
        w2_0 = sb("w2_0", [P, E, FT, D])
        b1_0, f3 = weight("b1_0", [P, E, FT], a["b1_0"])
        b2_0, f4 = weight("b2_0", [E, D], a["b2_0"])
        gate0, f5 = weight("gate0", [P, FT, E0], k_rows(a["gate0T"], FT))
        gbias, f6 = weight("gbias", [P, E0], a["gbias"].partition_broadcast(P))
        xloads = attention_weights("1")
        kdown, g1 = weight("kdown", [P, FT, GKV * LAT], k_rows(a["wk_down"], FT))
        vdown, g2 = weight("vdown", [P, FT, GKV * LAT], k_rows(a["wv_down"], FT))
        kup, g3 = weight("kup", [P, LAT], a["wk_upT"])
        vup, g4 = weight("vup", [P, LAT], a["wv_upT"])
        kdown4 = sb("kdown4", [P, FT, GKV, 4, LAT])
        Wqk = sb("Wqk", [P, FT, GH * LAT])
        Wvo = sb("Wvo", [P, FT, D])
        pool.wait(phase_1_done)
        sp.wait(phase_1_done)
        for e in (pe, dve, act):
            e.wait(phase_1_done)
        late = [late_stages("D"), late_stages("E")]
        w_route = dma_w["route"].send([f3, f4, f5, f6])
        runs = [late[0].run, late[1].run]
        w_gqa = dma_w["gqa"].send([g1, g2, g3, g4])
        w_ffn0 = [Dma(sp, f"expert0_{j}", new_sem, 1).send(
            [(w1_0[:, j, :, :], k_rows(a["w1_0"][j], FT)), (w2_0[:, j, :, :], k_rows(a["w2_0"][j], FT))]) for j in range(E)]
        w_xattn = dma_w["x1"].send(xloads)
        for g in range(GKV):
            for r in range(4):
                kdown4_done = pool.step("const", lambda e: e.tensor_copy(
                    kdown4[:, :, g, r, :], kdown[:, :, g * LAT:(g + 1) * LAT]), [w_gqa])
        folded, fold_dma = [w_gqa], [Dma(sp, f"fold{i}", new_sem, 1) for i in range(2)]
        fold_read = {}
        for h in range(GH):
            wq_wo = late[1].store[:, (h % 2) * 2 * D:(h % 2 + 1) * 2 * D]
            loaded = fold_dma[h % 2].send([(wq_wo[:, 0:D], a["wqT"][h * GHD:(h + 1) * GHD, :]),
                                           (wq_wo[:, D:2 * D], a["wo"][h * GHD:(h + 1) * GHD, :])], [fold_read.get(h % 2)])
            k = ring.pop(0)
            for c in range(FT):
                t = pe.step("fold", lambda e: e.matmul(k.t[:, c * LAT:(c + 1) * LAT], wq_wo[:, c * P:(c + 1) * P],
                                                       kup[:, :], start=True, stop=True), [loaded, k.free, w_gqa])
            r = 32 * (h % 4)
            t = pe.step("fold", lambda e: e.matmul(k.t[r:r + LAT, D:2 * D], vup[:, :], wq_wo[:, D:2 * D],
                                                   start=True, stop=True))
            fold_read[h % 2] = t
            dve.step("fold", lambda e: e.tensor_copy(
                Wqk[:, :, h * LAT:(h + 1) * LAT], k.t[:, 0:FT * LAT].rearrange("p (c l) -> p c l", c=FT)), [t])
            k.free = fold_done = dve.step("fold", lambda e: e.tensor_copy(Wvo[r:r + LAT, h // 4, :], k.t[r:r + LAT, D:2 * D]))
            ring.append(k)

        stored_5 = {}

        def late_of(i):
            for b in range(i, BATCH, 2):
                yield from late[i].run(b, [x2_stored[b]])
                stored_5[b] = late[i].stored

        interleave([(late_of(0), 0, 1), (late_of(1), LATE_LAG, 1)])

        phase_2_done = next_phase(late[0].stores + late[1].stores)
        for e in (pe, dve, act, pool, sp):
            e.wait(phase_2_done)
        G = "f1"
        FH = HID1 // P
        x5 = [sb(f"x5_{i}", [P, TT, D]) for i in range(2)]
        x5T = [sb(f"x5T_{i}", [P, FT, T]) for i in range(2)]
        y6 = [sb(f"y6_{i}", [P, TT, D]) for i in range(2)]
        hid1 = [Split(sb, f"hid1_{i}", [P, FH, T]) for i in range(2)]
        gate1, gate1_load = weight("gate1", [P, FT, E1], k_rows(a["Wg"], FT), alloc=sb)
        w1_1 = Split(sb, "w1_1", [P, E1, FT, HID1])
        w2_1 = Split(sb, "w2_1", [P, E1, FH, D])
        w1_raw = sb("w1_raw", [P, 2, FT, HID1])
        w2_raw = sb("w2_raw", [P, 2, FH, D])
        xT_split = [Split(sb, f"x5T_split{i}", [P, FT, T]) for i in range(2)]
        s = Stream("F")
        s.stats, s.routing = stats_of("F"), [routing_of("F0"), routing_of("F1")]
        x_sum = sb("x_sumF", [P, TT, D])
        dma_out = Dma(sp, "out", new_sem, 2)
        dma_x5 = Dma(sp, "x5", new_sem, 2)

        def load_x5(b, after):
            return dma_x5.send([(x5[b % 2][:, :, :], scratch_x[b].rearrange("(t p) d -> p t d", p=P)),
                                (x5T[b % 2][:, :, :], scratch_xT[b].rearrange("(k p) t -> p k t", p=P))], after)

        x5_loaded = [load_x5(0, [])]
        gate_loaded = Dma(sp, "gate1", new_sem, 1).send([gate1_load])
        dma_expert = [Dma(sp, f"expert{j}", new_sem, 1) for j in range(2)]
        w_loaded, split_of = {}, {}

        def load_expert(j):
            w_loaded[j] = dma_expert[j % 2].send([(w1_raw[:, j % 2, :, :], k_rows(a["W1"][j], FT)), (w2_raw[:, j % 2, :, :], k_rows(a["W2"][j], FH))],
            [split_of.get(j - 2)])

        load_expert(0)
        load_expert(1)
        x5_loaded.append(load_x5(1, []))
        hidden, hid_free, y_sent, up_read = {}, {}, {}, {}

        def w_split(j):
            if j not in split_of:
                w1_1.divide(act, pool, G, (slice(None), j), w1_raw[:, j % 2, :, :], [w_loaded[j]])
                split_of[j] = w2_1.divide(dve, pool, G, (slice(None), j), w2_raw[:, j % 2, :, :], [w_loaded[j]])
                if j + 2 < E1:
                    load_expert(j + 2)
            return split_of[j]

        prepared = {}

        def prepare(b):
            loaded = x5_loaded[b]
            ready = xT_split[b % 2].divide(dve, pool, G, (slice(None),) * 3, x5T[b % 2][:, :, :], [loaded, up_read.get(b - 2)])
            routed = route(s.routing[b % 2], G, E1, x5T[b % 2], gate1, None, [loaded, gate_loaded])
            prepared[b] = routed, ready, [ready, route_read[0]]

        def up(b, j):
            xT, ready = xT_split[b % 2], prepared[b][1]
            for m in range(FH // 2):
                k = ring.pop(0)
                for i in range(2):
                    f = 2 * m + i
                    for c in range(FT):
                        t = split_matmul(G, k.t[:, i * T:(i + 1) * T], w1_1, (slice(None), j, c, slice(f * P, (f + 1) * P)),
                                         xT, (slice(None), c, slice(None)), c == 0, c == FT - 1,
                                         [ready, w_split(j), k.free])
                h, at = hid1[j % 2], slice(2 * m, 2 * m + 2)
                upper = act.step(G, lambda e: e.activation(h.hi[:, at, :], halves(k), ACT.Relu),
                                 [t, hid_free.get(j % 2)])
                hidden[j] = dve.step(G, lambda e: e.scalar_tensor_tensor(
                    h.lo[:, at, :], halves(k), 0.0, h.hi[:, at, :].bitcast(FP32), ALU.max, ALU.subtract), [upper])
                k.free = hidden[j]
                ring.append(k)

        prepare(0)
        up(0, 0)
        for b in range(BATCH):
            x, xT, y, loaded, comb = x5[b % 2], xT_split[b % 2], y6[b % 2], x5_loaded[b], s.routing[b % 2][5]
            routed, ready, x5T_read = prepared[b]

            t = None
            for j in range(E1):
                if j == E1 // 2 and b + 1 < BATCH:
                    prepare(b + 1)
                if j + 1 < E1:
                    up(b, j + 1)
                elif b + 1 < BATCH:
                    up(b + 1, 0)
                k = ring.pop(0)
                for tt in range(TT):
                    for f in range(FH):
                        t2 = split_matmul(G, k.t[:, tt * D:(tt + 1) * D], hid1[j % 2], (slice(None), f, slice(tt * P, (tt + 1) * P)),
                                          w2_1, (slice(None), j, f, slice(None)), f == 0, f == FH - 1,
                                          [hidden[j], k.free])
                hid_free[j % 2] = t2
                src = x if j == 0 else x_sum
                for tt in range(TT):
                    t = dve.step(G, lambda e: e.scalar_tensor_tensor(
                        x_sum[:, tt, :], k.t[:, tt * D:(tt + 1) * D], comb[:, tt, j:j + 1], src[:, tt, :],
                        ALU.mult, ALU.add), [t2, t, routed, loaded])
                k.free = t
                ring.append(k)
            if b + 2 < BATCH:
                x5_loaded.append(load_x5(b + 2, [t] + x5T_read))
            up_read[b] = t2
            st, mv, rstd = s.stats
            for tt in range(TT):
                t = dve.step(G, lambda e: e.bn_stats(st[:, tt, :], x_sum[:, tt, :]), [t])
            for tt in range(TT):
                t = dve.step(G, lambda e: e.bn_aggr(mv[:, tt, :], st[:, tt, :]), [t])
            t2 = dve.step(G, lambda e: e.tensor_scalar(rstd[:, :], mv[:, :, 1], EPS, None, ALU.add), [t])
            t2 = pool.step(G, lambda e: e.tensor_tensor(rstd[:, :], rstd[:, :], root[:, :], ALU.pow), [t2])
            for tt in range(TT):
                t = dve.step(G, lambda e: e.tensor_scalar(y[:, tt, :], x_sum[:, tt, :], mv[:, tt, 0:1], rstd[:, tt:tt + 1],
                                                          ALU.subtract, ALU.mult), [t2, t, y_sent.get(b % 2)])
            y_sent[b % 2] = dma_out.send([(out[b].rearrange("(t p) d -> p t d", p=P), y[:, :, :])], [t])
        sp.wait(dma_out.all_sent())
        phase[0].close()


def order_ct(n_tokens):
    return (16 * np.arange(n_tokens)[None, :] + np.arange(16)[:, None]).reshape(-1)


def constants():
    below = lambda rows, cols: np.where(cols[None, :] > rows[:, None], HIDE, 0.0).astype(np.float32)
    n = np.arange(P)
    block = order_ct(8)
    sel = np.zeros((P, 32), np.float32)
    sel[:96] = np.tile(np.eye(32), (3, 1))
    head_block = np.zeros((H, D), np.float32)
    for h in range(H):
        head_block[h, h * HD:(h + 1) * HD] = 1
    return {
        "ident": np.eye(P, dtype=np.float32), "head_block": head_block,
        "iota": np.tile(np.arange(8, dtype=np.float32), (P, 1)),
        "consts": np.concatenate([np.eye(P, dtype=np.float32), below(n, n), below(n, n).T,
                                  below(block, block), below(block, block).T, sel], 1),
    }


def kernel(**inputs):
    import numpy as _np
    import concourse.bacc as _bacc
    from concourse import mybir as _mybir
    from concourse.bass_utils import run_bass_kernel_spmd as _run

    i = {k: _np.asarray(v) for k, v in inputs.items()}
    m, c, e, r = "L0_attn_", "L0_xattn_", "L0_ffn_", "L1_attn_"
    xp = i[m + "xproj_w"].T
    host = {
        "x": i["x"], "xT": i["x"].transpose(0, 2, 1), "ctxT": i["ctx_1024"].transpose(0, 2, 1),
        "mask": i["mask_BxSxS2_if1"], "maskT": i["mask_BxSxS2_if1"].transpose(0, 2, 1),
        "in_wT": i[m + "in_w"].T, "conv_w": i[m + "conv_w"][:, 0, :], "conv_b": i[m + "conv_b"],
        "xprojT": _np.concatenate([xp[:, RANK:], xp[:, :RANK]], 1), "dt_wT": i[m + "dt_w"].T, "dt_b": i[m + "dt_b"],
        "A_log": i[m + "A_log"], "D": i[m + "D"], "out_wT": i[m + "out_w"].T,
        "w1_0": _np.concatenate([i[e + "rw1"], i[e + "sw1"][None]]), "b1_0": _np.concatenate([i[e + "rb1"], i[e + "sb1"][None]]),
        "w2_0": _np.concatenate([i[e + "rw2"], i[e + "sw2"][None]]), "b2_0": _np.concatenate([i[e + "rb2"], i[e + "sb2"][None]]),
        "gate0T": i[e + "gate_w"].T, "gbias": i[e + "expert_bias"],
        "wqT": i[r + "wq"].T, "wk_down": i[r + "wk_down"], "wv_down": i[r + "wv_down"],
        "wk_upT": i[r + "wk_up"].T, "wv_upT": i[r + "wv_up"].T, "wo": i[r + "wo"],
        "Wg": i["L1_ffn_Wg"], "W1": i["L1_ffn_W1"], "W2": i["L1_ffn_W2"],
    }
    for layer, last in (("0", "o"), ("1", "p")):
        for part in "qkvo":
            n = last if part == "o" else part
            host[f"W{part}{layer}T"] = i[f"L{layer}_xattn_W{n}"].T
            host[f"b{part}{layer}"] = i[f"L{layer}_xattn_b{n}"]
    cols = lambda v: v.reshape(*v.shape[:-1], -1, P)
    for name in ("conv_b", "dt_b", "D", "bq0", "bk0", "bq1", "bk1"):
        host[name] = cols(host[name]).T
    host["b1_0"] = cols(host["b1_0"]).transpose(2, 0, 1)
    host.update(constants())
    nc = _bacc.Bacc("TRN2", target_bir_lowering=False, num_devices=1)
    arrays, aps = {}, {}
    for name, v in host.items():
        v = _np.ascontiguousarray(v)
        arrays["in_" + name] = v
        aps[name] = nc.dram_tensor("in_" + name, v.shape, _mybir.dt.from_np(v.dtype), kind="ExternalInput").ap()
    out = nc.dram_tensor("out_0", (BATCH, T, D), FP32, kind="ExternalOutput").ap()
    scratch_q = nc.dram_tensor("scratch_q", (BATCH, 4, 3, D, T), BF16, kind="Internal").ap()
    scratch_o = nc.dram_tensor("scratch_o", (BATCH, D, T), FP32, kind="Internal").ap()
    scratch_v = nc.dram_tensor("scratch_v", (BATCH, T, D), FP32, kind="Internal").ap()
    scratch_x = nc.dram_tensor("scratch_x", (BATCH, T, D), FP32, kind="Internal").ap()
    scratch_xT = nc.dram_tensor("scratch_xT", (BATCH, D, T), FP32, kind="Internal").ap()
    scratch_x2 = nc.dram_tensor("scratch_x2", (BATCH, T, D), FP32, kind="Internal").ap()
    scratch_x2T = nc.dram_tensor("scratch_x2T", (BATCH, D, T), FP32, kind="Internal").ap()
    program(nc, aps, out, scratch_q, scratch_o, scratch_v, scratch_x2, scratch_x2T, scratch_x, scratch_xT)
    got = _run(nc, [arrays], core_ids=[0])
    return got.results[0]["out_0"]
```

```python
from contextlib import ExitStack

import numpy as np
import concourse.bass as bass
from concourse import mybir

FP32 = mybir.dt.float32
BF16 = mybir.dt.bfloat16
F32R = mybir.dt.float32r
I32 = mybir.dt.int32
U32 = mybir.dt.uint32
ALU = mybir.AluOpType
ACT = mybir.ActivationFunctionType
AX = mybir.AxisListType

P = 128
BATCH, T, D = 16, 256, 256
TT = T // P
FT = D // P
DI = 512
DT = DI // P
NS = 16
RANK = 16
TAPS = 4
H, HD = 16, 16
GH, GKV, LAT, GHD = 8, 2, 32, 128
E0, E1, HID1 = 7, 8, 512
EPS = 1e-5
NEG = -1e9
HIDE = -1e30
LOWEST = -3e38
AHEAD_1 = (0, 0, 0, 8)
AHEAD_2 = (0, 0, 0, 4)
PE_STEP = 0.25
YIELD_LAG = 1.0
LSE_LAG = 4
SPLIT_LAG = 3
PACK_LAG = 12
REORDER_LAG = 3
O_LAG = 8
ROUTE_LAG = 9
NORM_LAG = 7
SCAN_LAG = 2
FOLD_LAG = 25
KEYS_LAG = 14
PARTS_Q = (0, 0, 1, 1, 0, 2)
PARTS_K = (0, 1, 0, 1, 2, 0)


class Engine:

    def __init__(self, eng, name, new_sem):
        self.eng, self.name, self.new_sem = eng, name, new_sem
        self.sems, self.count, self.seen = {}, {}, {}
        self.issued = 0

    def wait(self, after):
        for t in after:
            if t is None:
                continue
            sem, value, key = t
            if self.seen.get(key, 0) < value:
                self.eng.wait_ge(sem, value)
                self.seen[key] = value

    def step(self, stage, issue, after=()):
        self.wait(after)
        key = f"{self.name}_{stage}"
        if key not in self.sems:
            self.sems[key] = self.new_sem(key)
            self.count[key] = 0
        issue(self.eng).then_inc(self.sems[key], 1)
        self.count[key] += 1
        self.issued += 1
        return self.sems[key], self.count[key], key

    def all_steps(self):
        return [(self.sems[k], self.count[k], k) for k in self.sems]


class Dma:

    def __init__(self, engine, name, new_sem, turns):
        self.engine, self.name = engine, name
        self.sems = [new_sem(f"dma_{name}{i}") for i in range(turns)]
        self.count = [0] * turns
        self.at = 0

    def send(self, pairs, after=()):
        self.engine.wait(after)
        i = self.at % len(self.sems)
        self.at += 1
        for out, in_ in pairs:
            self.engine.eng.dma_start(out, in_).then_inc(self.sems[i], 16)
            self.count[i] += 16
        return self.sems[i], self.count[i], f"{self.name}{i}"

    def all_sent(self):
        return [(s, self.count[i], f"{self.name}{i}") for i, s in enumerate(self.sems) if self.count[i]]


class Split:

    def __init__(self, alloc, name, shape):
        self.hi, self.lo = alloc(name + "_hi", shape, F32R), alloc(name + "_lo", shape, F32R)

    def divide(self, first, second, stage, at, x, ready):
        hi, lo = self.hi[at], self.lo[at]
        if first.name == "act":
            t = first.step(stage, lambda e: e.activation(hi, x, ACT.Copy), ready)
        else:
            t = first.step(stage, lambda e: e.tensor_copy(hi, x), ready)
        return second.step(stage, lambda e: e.tensor_tensor(lo, x, hi.bitcast(FP32), ALU.subtract), [t])


END = object()


def by_clock(streams, ahead, pe):
    clock = 0.0
    start = [(-ahead[i], i) for i in range(len(streams))]
    while start:
        start.sort()
        at, i = start.pop(0)
        clock = max(clock, at + ahead[i])
        issued = pe.issued
        lag = next(streams[i], END)
        clock += (pe.issued - issued) * PE_STEP
        if lag is not END:
            start.append((clock + (lag or YIELD_LAG) - ahead[i], i))


class Stream:

    def __init__(self, name):
        self.name = name
        self.normed = self.out = self.stored = None


class Bank:

    def __init__(self, tensor):
        self.t, self.free = tensor, None


def program(nc, a, out, scratch_q, scratch_o, scratch_v, scratch_x2, scratch_x2T, scratch_x, scratch_xT):
    ctx = ExitStack()
    phase = [ExitStack()]
    with ctx:
        def keep(name, shape, dt=FP32):
            return ctx.enter_context(nc.sbuf_tensor(name, shape, dt))

        def sb(name, shape, dt=FP32):
            return phase[0].enter_context(nc.sbuf_tensor(name, shape, dt))

        def new_sem(name):
            return ctx.enter_context(nc.semaphore(name))

        pe = Engine(nc.tensor, "pe", new_sem)
        dve = Engine(nc.vector, "dve", new_sem)
        act = Engine(nc.scalar, "act", new_sem)
        pool = Engine(nc.gpsimd, "pool", new_sem)
        sp = Engine(nc.sync, "sp", new_sem)
        ring = [Bank(ctx.enter_context(nc.psum_tensor(f"bank{i}", [P, 512], FP32))) for i in range(8)]

        def split_matmul(stage, out, w, w_at, x, x_at, start, stop, ready):
            parts = ((w.lo, x.hi), (w.hi, x.lo), (w.hi, x.hi))
            for i, (wp, xp) in enumerate(parts):
                t = pe.step(stage, lambda e: e.matmul(out, wp[w_at], xp[x_at],
                                                      start=start and i == 0, stop=stop and i == 2), ready)
            return t

        def next_phase(stores):
            done = [t for e in (pe, dve, act, pool) for t in e.all_steps()]
            done += [t for d in stores for t in d.all_sent()]
            phase[0].close()
            phase[0] = ExitStack()
            return done

        def weight(name, shape, view, dt=FP32, alloc=sb):
            t = alloc("w_" + name, shape, dt)
            return t, (t[tuple(slice(None) for _ in shape)], view)

        k_rows = lambda ap, k: ap.rearrange("(k p) n -> p k n", k=k)
        rows_of = lambda ap: ap.rearrange("(t p) d -> p t d", p=P)
        stats_of = lambda s: (sb("stats" + s, [P, TT, 6]), sb("mv" + s, [P, TT, 2]), sb("rstd" + s, [P, TT]))

        def routing_of(s):
            r = [sb(n + s, [P, TT, w], dt) for n, w, dt in (
                ("logits", 8, FP32), ("top", 8, FP32), ("top_i", 8, U32), ("top_f", 2, FP32), ("wts", 4, FP32),
                ("comb", 8, FP32), ("comb2", 8, FP32))]
            return r + [pool.step("const", lambda e: e.memset(r[0][:, :, :], LOWEST))]

        root = keep("root", [P, TT])
        iota = keep("iota", [P, 8])
        ident = keep("ident", [P, P])
        consts = keep("consts", [P, 5 * P + 32], BF16)
        identb, causal, causalT, bcausal, bcausalT = (consts[:, i * P:(i + 1) * P] for i in range(5))
        sel1 = consts[0:96, 5 * P:]

        def sel(row):
            return sel1[:, row:row + 1].broadcast_to([96, P])

        dma_w = {n: Dma(sp, "w_" + n, new_sem, 1) for n in ("const", "mamba", "x0", "route", "x1", "gqa", "fold")}
        ident_ready = dma_w["const"].send([(ident[:, :], a["ident"]), (iota[:, :], a["iota"])])
        const = pool.step("const", lambda e: e.memset(root[:, :], -0.5))

        in_w, l1 = weight("in_w", [P, FT, 2 * DI], k_rows(a["in_wT"], FT))
        conv_w, l2 = weight("conv_w", [P, DT, TAPS], k_rows(a["conv_w"], DT))
        conv_b, l3 = weight("conv_b", [P, DT], a["conv_b"])
        xproj, l4 = weight("xproj", [P, DT, 2 * NS + RANK], k_rows(a["xprojT"], DT))
        dt_w, l5 = weight("dt_w", [RANK, DI], a["dt_wT"])
        dt_b, l6 = weight("dt_b", [P, DT], a["dt_b"])
        A, l7 = weight("A_log", [P, DT, NS], k_rows(a["A_log"], DT))
        skip_w, l8 = weight("D", [P, DT], a["D"])
        out_w, l9 = weight("out_w", [P, DT, D], k_rows(a["out_wT"], DT))

        def attention_weights(layer):
            loads = []
            for m in "qkvo":
                xw[layer + m], l = weight(f"x{layer}{m}", [P, FT, D], k_rows(a[f"W{m}{layer}T"], FT))
                loads.append(l)
                if m in "qk":
                    xw[layer + "b" + m], l = weight(f"x{layer}b{m}", [P, FT], a[f"b{m}{layer}"])
                else:
                    xw[layer + "b" + m], l = weight(f"x{layer}b{m}", [P, D], a[f"b{m}{layer}"].partition_broadcast(P))
                loads.append(l)
            return loads

        xw = {}
        xloads = attention_weights("0")
        head_block, l = weight("head_block", [H, D], a["head_block"])
        xloads.append(l)
        ones16 = sb("ones16", [P, H])
        onesb = sb("onesb", [P, P], BF16)
        one = sb("one", [P, 1])

        def halves(bank):
            return bank.t[:, :].rearrange("p (k n) -> p k n", k=2)

        def layer_norm(s, bank, x_old, ready, y, yT, y_free):
            st, mv, rstd = s.stats
            G = "ln" + s.name
            yield
            summed = dve.step(G, lambda e: e.tensor_tensor(y[:, :, :], halves(bank), x_old, ALU.add), ready + y_free)
            bank.free = summed
            ring.append(bank)
            for t in range(TT):
                k = dve.step(G, lambda e: e.bn_stats(st[:, t, :], y[:, t, :]), [summed])
            for t in range(TT):
                k = dve.step(G, lambda e: e.bn_aggr(mv[:, t, :], st[:, t, :]), [k])
            k2 = dve.step(G, lambda e: e.tensor_scalar(rstd[:, :], mv[:, :, 1], EPS, None, ALU.add), [k])
            k2 = pool.step(G, lambda e: e.tensor_tensor(rstd[:, :], rstd[:, :], root[:, :], ALU.pow), [k2, const])
            for t in range(TT):
                normed = dve.step(G, lambda e: e.tensor_scalar(
                    y[:, t, :], y[:, t, :], mv[:, t, 0:1], rstd[:, t:t + 1], ALU.subtract, ALU.mult), [k2, k])
            yield NORM_LAG
            turned = ring.pop(0)
            for c in range(FT):
                for t in range(TT):
                    k = pe.step(G, lambda e: e.transpose(
                        turned.t[:, c * T + t * P:c * T + (t + 1) * P], y[:, t, c * P:(c + 1) * P], ident[:, :]),
                        [normed, turned.free, ident_ready])
            turned.free = act.step(G, lambda e: e.activation(yT[:, :, :], halves(turned), ACT.Copy), [k] + y_free)
            ring.append(turned)
            s.normed = (normed, turned.free)
            yield 2

        scanning = []

        def mamba_stream(name):
            s = Stream(name)
            s.stats = stats_of(name)
            s.x_in = x_in = sb("x_in" + name, [P, TT, D])
            s.xT_in = xT_in = sb("xT_in" + name, [P, FT, T])
            s.x1 = x1 = sb("x1" + name, [P, TT, D])
            s.x1T = x1T = sb("x1T" + name, [P, FT, T])
            dma_x = Dma(sp, "x" + name, new_sem, 1)

            def load(b, after):
                return dma_x.send([(x_in[:, :, :], a["x"][b].rearrange("(t p) d -> p t d", p=P)),
                                   (xT_in[:, :, :], a["xT"][b].rearrange("(t p) d -> p t d", p=P))], after)

            xx_pad = sb("xx_pad" + name, [P, DT, T + TAPS - 1])
            u = sb("u" + name, [P, DT, T])
            gate = sb("gate" + name, [P, DT, T])
            delta = sb("delta" + name, [P, DT, T])
            du = u
            work = sb("work" + name, [P, DT, T])
            dbc = sb("dbc" + name, [RANK, T])
            bc3 = sb("bc3" + name, [96, T], BF16)
            bc_mid = sb("bc_mid" + name, [32, T], BF16)
            dA = [sb(f"dA{name}{i}", [P, DT, T]) for i in range(2)]
            hs = s.hs = [sb(f"hs{name}{i}", [P, DT, T]) for i in range(3)]
            b_all = [sb(f"b_all{name}{i}", [P, T]) for i in range(2)]
            bc_rest = b_all[0][0:32, :]
            for t in (xx_pad, dA[0], dA[1]):
                edge = pool.step("const", lambda e: e.memset(t[:, :, 0:TAPS - 1], 0.0))

            def mamba(b, loaded, y_free):
                x, xT, G = x_in, xT_in, "mamba" + s.name

                for m in range(DT):
                    k = ring.pop(0)
                    for j in range(2):
                        for c in range(FT):
                            n0 = (2 * m + j) * P
                            t = pe.step(G, lambda e: e.matmul(k.t[:, j * T:(j + 1) * T], in_w[:, c, n0:n0 + P], xT[:, c, :],
                                                              start=c == 0, stop=c == FT - 1), [loaded, w_mamba, k.free])
                    if m < 2:
                        t = in_pad = act.step(G, lambda e: e.activation(
                            xx_pad[:, 2 * m:2 * m + 2, TAPS - 1:], halves(k), ACT.Copy), [t, edge] + conv_read)
                    else:
                        t = res_in = act.step(G, lambda e: e.activation(
                            gate[:, 2 * m - 4:2 * m - 2, :], halves(k), ACT.Copy), [t])
                    k.free = t
                    ring.append(k)
                    yield
                for d in range(DT):
                    t = dve.step(G, lambda e: e.tensor_scalar(work[:, d, :], xx_pad[:, d, 0:T], conv_w[:, d, 0:1],
                                                              conv_b[:, d:d + 1], ALU.mult, ALU.add), [in_pad])
                for tap in range(1, TAPS):
                    for d in range(DT):
                        t = dve.step(G, lambda e: e.scalar_tensor_tensor(
                            work[:, d, :], xx_pad[:, d, tap:tap + T], conv_w[:, d, tap:tap + 1], work[:, d, :],
                            ALU.mult, ALU.add), [t])
                    yield
                conv_read[:] = [t]
                yield 2
                gate_ready = act.step(G, lambda e: e.activation(gate[:, :, :], gate[:, :, :], ACT.Silu), [res_in])
                u_ready = act.step(G, lambda e: e.activation(u[:, :, :], work[:, :, :], ACT.Silu), [t, last_scan[0]])
                yield 6
                k = ring.pop(0)
                for d in range(DT):
                    t = pe.step(G, lambda e: e.matmul(k.t[0:2 * NS + RANK, 0:T], xproj[:, d, :], u[:, d, :],
                                                      start=d == 0, stop=d == DT - 1), [u_ready, k.free])
                yield
                low = act.step(G, lambda e: e.activation(dbc[:, :], k.t[2 * NS:, 0:T][0:RANK], ACT.Copy), [t])
                t = dve.step(G, lambda e: e.tensor_copy(bc3[0:32, :], k.t[0:32, 0:T]), [low])
                t = dve.step(G, lambda e: e.tensor_tensor(bc_rest, k.t[0:32, 0:T], bc3[0:32, :], ALU.subtract), [t])
                k.free = t
                t = dve.step(G, lambda e: e.tensor_copy(bc_mid[:, :], bc_rest), [t])
                dve.step(G, lambda e: e.tensor_copy(bc3[32:64, :], bc_mid[:, :]), [t])
                bc_ready = dve.step(G, lambda e: e.tensor_tensor(bc3[64:96, :], bc_rest, bc_mid[:, :], ALU.subtract))
                k2 = k
                yield 2
                for m in range(2):
                    k = ring.pop(0)
                    for j in range(2):
                        d = 2 * m + j
                        t = pe.step(G, lambda e: e.matmul(k.t[:, j * T:(j + 1) * T], dt_w[:, d * P:(d + 1) * P], dbc[:, :],
                                                          start=True, stop=True), [low, k.free])
                    for j in range(2):
                        d = 2 * m + j
                        ta = act.step(G, lambda e: e.activation(delta[:, d, :], k.t[:, j * T:(j + 1) * T], ACT.Abs,
                                                                bias=dt_b[:, d:d + 1]), [t, last_scan[0]])
                    for j in range(2):
                        d = 2 * m + j
                        tv = dve.step(G, lambda e: e.tensor_scalar(work[:, d, :], k.t[:, j * T:(j + 1) * T],
                                                                   dt_b[:, d:d + 1], 0.0, ALU.add, ALU.max), [t, ta, u_ready])
                    k.free = tv
                    ring.append(k)
                ring.append(k2)
                yield
                t = act.step(G, lambda e: e.activation(delta[:, :, :], delta[:, :, :], ACT.Exp, scale=-1.0), [ta])
                t = act.step(G, lambda e: e.activation(delta[:, :, :], delta[:, :, :], ACT.Ln, bias=one[:, 0:1]), [t, const])
                delta_ready = pool.step(G, lambda e: e.tensor_tensor(delta[:, :, :], delta[:, :, :], work[:, :, :], ALU.add), [t, tv])
                for d in range(DT):
                    t = dve.step(G, lambda e: e.tensor_scalar(work[:, d, :], u[:, d, :], skip_w[:, d:d + 1], None, ALU.mult),
                                 [delta_ready])
                du_ready = pool.step(G, lambda e: e.tensor_tensor(du[:, :, :], delta[:, :, :], u[:, :, :], ALU.mult), [delta_ready, t])
                yield

                while scanning or len(ring) < 5:
                    yield 3
                scanning.append(b)
                y_banks = [ring.pop(0), ring.pop(0)]
                decay, dbu, scanned, multiplied, summed_y, bank_of = {}, {}, {}, {}, {}, {}
                flat = lambda x: x[:, :, :].rearrange("p d t -> p (d t)")

                def spread(n):
                    k = bank_of[n] = ring.pop(0)
                    for half, row in ((0, n), (1, NS + n)):
                        t = pe.step(G, lambda e: e.matmul(k.t[:, half * T:(half + 1) * T], sel(row), bc3[:, :],
                                                          start=True, stop=True), [bc_ready, consts_ready, k.free])
                    spread_done[n] = t

                def inputs(n):
                    k = bank_of[n]
                    b_copied = act.step(G, lambda e: e.activation(b_all[n % 2][:, :], k.t[:, 0:T], ACT.Copy),
                                        [spread_done[n], dbu.get(n - 2)])
                    dbu[n] = pool.step(G, lambda e: e.tensor_tensor(
                        hs[n % 3][:, :, :], du[:, :, :], b_all[n % 2][:, :].unsqueeze(1).broadcast_to([P, DT, T]), ALU.mult),
                        [b_copied, du_ready, summed_y.get(n - 3, last_y[0])])
                    for d in range(DT):
                        decay[n] = act.step(G, lambda e: e.activation(dA[n % 2][:, d, 1:], delta[:, d, 1:], ACT.Exp,
                                                                      scale=A[:, d, n:n + 1]),
                                            [delta_ready, A_neg, edge, scanned.get(n - 2, last_scan[0])])

                def sum_state(n):
                    for m in range(2):
                        summed_y[n] = pe.step(G, lambda e: e.matmul(
                            y_banks[m].t[:, :], ident[:, :], hs[n % 3][:, 2 * m:2 * m + 2, :].rearrange("p d t -> p (d t)"),
                            start=n == 0, stop=n == NS - 1), [multiplied[n], y_banks[m].free])

                spread_done = {}
                spread(0)
                yield
                inputs(0)
                spread(1)
                yield
                for n in range(NS):
                    k = bank_of[n]
                    if n + 1 < NS:
                        inputs(n + 1)
                    h = hs[n % 3]
                    scanned[n] = dve.step(G, lambda e: e.tensor_tensor_scan(flat(h), flat(dA[n % 2]), flat(h), 0.0,
                                                                            ALU.mult, ALU.add), [decay[n], dbu[n]])
                    multiplied[n] = dve.step(G, lambda e: e.tensor_tensor(
                        h[:, :, :], h[:, :, :], k.t[:, T:2 * T].unsqueeze(1).broadcast_to([P, DT, T]), ALU.mult),
                        [scanned[n]])
                    k.free = multiplied[n]
                    ring.append(k)
                    if n + 2 < NS:
                        spread(n + 2)
                    if n:
                        sum_state(n - 1)
                    yield SCAN_LAG
                sum_state(NS - 1)
                yield
                scanning.pop()
                last_scan[0], last_y[0] = multiplied[NS - 1], summed_y[NS - 1]
                for m in range(2):
                    t = dve.step(G, lambda e: e.tensor_tensor(work[:, 2 * m:2 * m + 2, :], work[:, 2 * m:2 * m + 2, :],
                                                              halves(y_banks[m]), ALU.add), [summed_y[NS - 1]])
                for k in y_banks:
                    k.free = t
                    ring.append(k)
                t = pool.step(G, lambda e: e.tensor_tensor(work[:, :, :], work[:, :, :], gate[:, :, :], ALU.mult), [t, gate_ready])
                yield
                yield
                k = ring.pop(0)
                for tt in range(TT):
                    for d in range(DT):
                        t2 = pe.step(G, lambda e: e.matmul(k.t[:, tt * D:(tt + 1) * D], work[:, d, tt * P:(tt + 1) * P],
                                                           out_w[:, d, :], start=d == 0, stop=d == DT - 1), [t, k.free])
                yield
                while y_free() is None:
                    yield 5
                yield from layer_norm(s, k, x[:, :, :], [t2, loaded], x1, x1T, y_free())
                s.out = s.normed

            conv_read, last_scan, last_y = [], [None], [None]
            s.run, s.load = mamba, load
            return s

        def project(G, w, src, ready):
            k = ring.pop(0)
            for f in range(FT):
                for c in range(FT):
                    t = pe.step(G, lambda e: e.matmul(k.t[:, f * T:(f + 1) * T], w[:, c, f * P:(f + 1) * P], src[:, c, :],
                                                      start=c == 0, stop=c == FT - 1), ready + [k.free])
            return k, t

        def project_tokens(G, w, src, ready):
            k = ring.pop(0)
            for tt in range(TT):
                for c in range(FT):
                    t = pe.step(G, lambda e: e.matmul(k.t[:, tt * D:(tt + 1) * D], src[:, c, tt * P:(tt + 1) * P],
                                                      w[:, c, :], start=c == 0, stop=c == FT - 1), ready + [k.free])
            return k, t

        class Softmax:

            def __init__(self, name, split=True):
                self.split = split
                self.nmax = sb("nmax" + name, [P, TT, H])
                self.sums = sb("sums" + name, [P, TT, H])
                self.nlse = sb("nlse" + name, [P, TT, H])
                self.lseT = sb("lseT" + name, [H, T])
                self.probs = [sb(f"probs{name}{i}", [P, TT, T]) for i in range(3)]
                self.probs_read = {}
                if split:
                    self.lse3 = sb("lse3" + name, [96, T], BF16)
                    self.lse_mid = sb("lse_mid" + name, [H, T], BF16)
                    self.zeroed = pool.step("const", lambda e: e.memset(self.lse3[:, :], 0.0))

            def finish(self, G, heads, t, also=None):
                nmax, sums, nlse, lseT = self.nmax, self.sums, self.nlse, self.lseT
                ln = act.step(G, lambda e: e.activation(sums[:, :, 0:heads], sums[:, :, 0:heads], ACT.Ln), [t])
                t = dve.step(G, lambda e: e.tensor_tensor(nlse[:, :, 0:heads], nmax[:, :, 0:heads], sums[:, :, 0:heads],
                                                          ALU.subtract), [ln, also])
                yield LSE_LAG
                k = ring.pop(0)
                for q in range(TT):
                    t2 = pe.step(G, lambda e: e.transpose(k.t[0:heads, q * P:(q + 1) * P], nlse[:, q, 0:heads], ident[:, :]),
                                 [t, k.free])
                t = dve.step(G, lambda e: e.tensor_copy(lseT[0:heads, :], k.t[0:heads, 0:T]), [t2])
                k.free = t
                ring.append(k)
                if not self.split:
                    return t
                lse3, lse_mid = self.lse3, self.lse_mid
                t = dve.step(G, lambda e: e.tensor_copy(lse3[0:heads, :], lseT[0:heads, :]), [t, self.zeroed])
                t = dve.step(G, lambda e: e.tensor_tensor(lseT[0:heads, :], lseT[0:heads, :], lse3[0:heads, :], ALU.subtract), [t])
                t = dve.step(G, lambda e: e.tensor_copy(lse_mid[0:heads, :], lseT[0:heads, :]), [t])
                dve.step(G, lambda e: e.tensor_copy(lse3[32:32 + heads, :], lse_mid[0:heads, :]), [t])
                t = dve.step(G, lambda e: e.tensor_tensor(lse3[64:64 + heads, :], lseT[0:heads, :], lse_mid[0:heads, :],
                                                          ALU.subtract))
                yield SPLIT_LAG
                return t

        class Packer:

            def __init__(self, name, slot, raw="raw"):
                self.proj = sb("proj" + name, [P, FT, T])
                self.parts = sb("parts" + name, [P, 3, FT, T], BF16)
                self.raw = sb("raw" + name, [96, H, T], BF16) if raw else None
                self.store, self.load = Dma(sp, "store" + name, new_sem, 1), Dma(sp, "load" + name, new_sem, 1)
                self.slot, self.stored, self.raw_read = slot, None, None

            def pack(self, G, b, w, bias, scale, src, ready, order, dst=None, free=()):
                dst, free = (self.raw, [self.raw_read]) if dst is None else (dst, free)
                proj, parts = self.proj, self.parts
                k, t = project(G, w, src, ready)
                self.projected = t
                for f in range(FT):
                    t = dve.step(G, lambda e: e.tensor_scalar(proj[:, f, :], k.t[:, f * T:(f + 1) * T], bias[:, f:f + 1],
                                                              scale, ALU.add, ALU.mult), [t, self.stored] + ready)
                k.free = t
                ring.append(k)
                t = act.step(G, lambda e: e.activation(parts[:, 0, :, :], proj[:, :, :], ACT.Copy), [t, self.stored])
                t = pool.step(G, lambda e: e.tensor_tensor(proj[:, :, :], proj[:, :, :], parts[:, 0, :, :], ALU.subtract), [t])
                yield SPLIT_LAG
                t = act.step(G, lambda e: e.activation(parts[:, 1, :, :], proj[:, :, :], ACT.Copy), [t])
                t = pool.step(G, lambda e: e.tensor_tensor(parts[:, 2, :, :], proj[:, :, :], parts[:, 1, :, :], ALU.subtract), [t])
                self.stored = self.store.send(
                    [(scratch_q[b, self.slot, s].rearrange("(k p) t -> p k t", k=FT), parts[:, s, :, :]) for s in range(3)], [t])
                loaded = self.load.send(
                    [(dst[r * HD:(r + 1) * HD, :, :], scratch_q[b, self.slot, s].rearrange("(c e) t -> e c t", e=HD))
                     for r, s in enumerate(order)], [self.stored] + list(free))
                yield PACK_LAG
                return loaded

            def reorder(self, G, packed, ready):
                for tile in range(2):
                    self.raw_read = dve.step(G, lambda e: e.tensor_copy(
                        packed[:, :, tile * P:(tile + 1) * P].rearrange("p h (c t) -> p h c t", t=T // H // 2),
                        self.raw[:, :, :].rearrange("p c (h i t) -> p h i c t", h=H, i=2)[:, :, tile]), ready)
                return self.raw_read

        def keys_stream_0():
            s = Stream("K0")
            packer = Packer("K0", 0, None)
            ctxT = sb("ctxT_0", [P, FT, T])
            mask = sb("mask", [P, TT, T], I32)
            maskT = sb("maskT", [P, TT, T], I32)
            any_kept = packer.proj[:, 0, :]
            V = sb("V0", [P, TT, D])
            hide = [sb(f"hide{i}", [P, TT, T], BF16) for i in range(2)]
            keepT = [sb(f"keepT{i}", [P, TT, T], BF16) for i in range(2)]
            negT = sb("negT", [P, TT, T])
            v_neg = [sb(f"v_neg{i}", [P, FT, T]) for i in range(2)]
            k_packed = [sb(f"k_packed0{i}", [96, H, T], BF16) for i in range(2)]
            Vpad = [sb(f"Vpad{i}", [P, TT, H, 2 * HD]) for i in range(2)]
            v_cols = [sb(f"v_cols{i}", [H, D]) for i in range(2)]
            dma_ctx = Dma(sp, "ctx0", new_sem, 1)
            zeroed = [pool.step("const", lambda e: e.memset(v[:, :, :, :], 0.0)) for v in Vpad][1]
            loaded_read = []

            def load(b):
                return dma_ctx.send([(ctxT[:, :, :], rows_of(a["ctxT"][b])), (mask[:, :, :], rows_of(a["mask"][b])),
                                     (maskT[:, :, :], rows_of(a["maskT"][b]))], loaded_read)

            def run(b, ctx_ready, free):
                G, i = "k0", b % 2
                hide_ready = dve.step(G, lambda e: e.tensor_scalar(hide[i][:, :, :], mask[:, :, :], 0.0, HIDE,
                                                                   ALU.is_equal, ALU.mult), [ctx_ready] + free)
                keep_ready = dve.step(G, lambda e: e.tensor_scalar(keepT[i][:, :, :], maskT[:, :, :], 0.0, None,
                                                                   ALU.not_equal), [ctx_ready] + free)
                k = ring.pop(0)
                for c in range(TT):
                    t = pe.step(G, lambda e: e.matmul(k.t[:, 0:T], onesb[:, :], keepT[i][:, c, :], start=c == 0, stop=c == TT - 1),
                                [keep_ready, const, k.free])
                t = dve.step(G, lambda e: e.tensor_scalar(any_kept, k.t[:, 0:T], 0.0, NEG, ALU.is_gt, ALU.mult), [t, packer.stored])
                k.free = t
                ring.append(k)
                for c in range(TT):
                    neg_ready = dve.step(G, lambda e: e.scalar_tensor_tensor(
                        negT[:, c, :], maskT[:, c, :], 0.0, any_kept, ALU.is_equal, ALU.mult), [t, neg_read[0]])
                yield 3
                k, t = project_tokens(G, xw["0v"], ctxT, [ctx_ready, w_xattn])
                v_read = t
                v_ready = dve.step(G, lambda e: e.tensor_tensor(
                    V[:, :, :], halves(k), xw["0bv"][:, :].unsqueeze(1).broadcast_to([P, TT, D]), ALU.add),
                    [t, w_xattn, neg_read[0]])
                k.free = v_ready
                ring.append(k)
                for c in range(TT):
                    for odd in range(2):
                        at = slice(odd * HD, (odd + 1) * HD)
                        pad_ready = pool.step(G, lambda e: e.tensor_copy(
                            Vpad[i][:, c, :, :].rearrange("p (g o) n -> p g o n", o=2)[:, :, odd, at],
                            V[:, c, :].rearrange("p (g o n) -> p g o n", o=2, n=HD)[:, :, odd, :]),
                            [v_ready, zeroed] + free)
                yield 2
                k = ring.pop(0)
                for c in range(TT):
                    t = pe.step(G, lambda e: e.matmul(k.t[0:H, 0:D], ones16[:, :], V[:, c, :], start=c == 0, stop=c == TT - 1),
                                [v_ready, k.free, const])
                cols_ready = dve.step(G, lambda e: e.tensor_tensor(v_cols[i][:, :], k.t[0:H, 0:D], head_block[:, :], ALU.mult),
                                      [t] + free)
                k.free = cols_ready
                ring.append(k)
                k = ring.pop(0)
                for f in range(FT):
                    for c in range(TT):
                        t = pe.step(G, lambda e: e.matmul(k.t[:, f * T:(f + 1) * T], V[:, c, f * P:(f + 1) * P], negT[:, c, :],
                                                          start=c == 0, stop=c == TT - 1), [neg_ready, k.free])
                neg_read[0] = t
                v_neg_ready = act.step(G, lambda e: e.activation(v_neg[i][:, :, :], halves(k), ACT.Copy), [t] + free)
                k.free = v_neg_ready
                ring.append(k)
                yield
                packed = yield from packer.pack(G, b, xw["0k"], xw["0bk"], 1.0, ctxT, [ctx_ready, w_xattn], PARTS_K,
                                                k_packed[i], free)
                loaded_read[:] = [neg_ready, v_read, packer.projected]
                s.ready[b] = (hide[i], keepT[i], v_neg[i], k_packed[i], Vpad[i], v_cols[i],
                              hide_ready, v_neg_ready, packed, pad_ready, cols_ready)
                yield

            neg_read = [None]
            s.ready = {}
            s.stores = [packer.store]
            s.load, s.run = load, run
            return s

        def cross_stream_0(keys):
            s = Stream("C")
            s.stats = stats_of("C")
            soft = Softmax("C", split=False)
            nmax, sums, probs, probs_read = soft.nmax, soft.sums, soft.probs, soft.probs_read
            packer = Packer("C", 1, None)
            q_packed = sb("q_packed0", [96, H, T], BF16)
            attT = packer.proj
            s.x2, s.x2T = sb("x2", [P, TT, D]), sb("x2T", [P, FT, T])

            def run(b, x_ready, xT_ready, x, xT, y, yT, y_free):
                G = "x0"
                biased = pool.step(G, lambda e: e.tensor_tensor(
                    y[:, :, :], x[:, :, :], xw["0bo"][:, :].unsqueeze(1).broadcast_to([P, TT, D]), ALU.add),
                    [x_ready, w_xattn] + y_free)
                packing = packer.pack(G, b, xw["0q"], xw["0bq"], HD ** -0.5, xT, [xT_ready, w_xattn], PARTS_Q, q_packed,
                                      [softmaxed[0]])
                lag = next(packing)
                s.x1_read[b] = [biased, packer.projected]
                yield lag
                q_ready = yield from packing
                while b not in keys.ready:
                    yield 5
                (hide, keepT, v_neg, k_packed, Vpad, v_cols,
                 hide_ready, v_neg_ready, k_ready, pad_ready, cols_ready) = keys.ready[b]
                for h in range(H):
                    k = ring.pop(0)
                    for q in range(TT):
                        dst = k.t[:, q * T:(q + 1) * T]
                        pe.step(G, lambda e: e.matmul(dst, q_packed[:, h, q * P:(q + 1) * P], k_packed[:, h, :], start=True, stop=False),
                                [q_ready, k_ready, k.free])
                        t = pe.step(G, lambda e: e.matmul(dst, identb[:, :], hide[:, q, :], start=False, stop=True), [hide_ready])
                    t = dve.step(G, lambda e: e.tensor_reduce(nmax[:, :, h], halves(k), AX.X, ALU.max, negate=True), [t])
                    for q in range(TT):
                        t2 = act.step(G, lambda e: e.activation(k.t[:, q * T:(q + 1) * T], k.t[:, q * T:(q + 1) * T], ACT.Exp,
                                                                bias=nmax[:, q, h:h + 1], accum_out=sums[:, q, h:h + 1]), [t])
                    k.free = t2
                    ring.append(k)
                    yield
                t = dve.step(G, lambda e: e.scalar_tensor_tensor(nmax[:, :, :], nmax[:, :, :], -HIDE / 2, nmax[:, :, :],
                                                                 ALU.is_lt, ALU.mult), [t2])
                lse_ready = yield from soft.finish(G, H, t2, t)
                acc = ring.pop(0)
                scored = {}

                def score(h):
                    k = ring.pop(0)
                    for c in range(TT):
                        t = pe.step(G, lambda e: e.matmul(k.t[:, c * T:(c + 1) * T], k_packed[:, h, c * P:(c + 1) * P],
                                                          q_packed[:, h, :], start=True, stop=True), [k.free])
                    softmaxed[0] = t
                    scored[h] = dve.step(G, lambda e: e.tensor_tensor(probs[h % 3][:, :, :], halves(k), keepT[:, :, :], ALU.mult),
                                         [t, probs_read.get(h % 3)])
                    k.free = scored[h]
                    ring.append(k)

                score(0)
                score(1)
                yield
                for f in range(FT):
                    pe.step(G, lambda e: e.matmul(acc.t[:, f * T:(f + 1) * T], v_cols[:, f * P:(f + 1) * P], soft.lseT[:, :],
                                                  start=True, stop=False), [lse_ready, cols_ready, acc.free])
                    for h in range(8 * f, 8 * f + 8):
                        if h + 2 < H:
                            score(h + 2)
                        row = (h % 8) // 2 * 2 * HD
                        for c in range(TT):
                            t = pe.step(G, lambda e: e.matmul(acc.t[row:row + 2 * HD, f * T:(f + 1) * T], Vpad[:, c, h, :],
                                                              probs[h % 3][:, c, :], start=False, stop=h % 2 == 1 and c == TT - 1),
                                        [scored[h], pad_ready])
                        probs_read[h % 3] = t
                        yield
                t = dve.step(G, lambda e: e.tensor_tensor(attT[:, :, :], halves(acc), v_neg[:, :, :], ALU.add), [t, v_neg_ready])
                acc.free = t
                ring.append(acc)
                s.keys_read[b] = [softmaxed[0], t]
                yield 1
                k, t = project_tokens(G, xw["0o"], attT, [t, w_xattn])
                yield from layer_norm(s, k, y[:, :, :], [t, biased], y, yT, y_free)

            softmaxed = [None]
            s.x1_read, s.keys_read = {}, {}
            s.stores = [packer.store]
            s.run = run
            return s

        route_read = [None]

        def route(buffers, G, n, xT, gate_w, bias, ready):
            logits, top, top_i, top_f, wts, comb, comb2, padded = buffers
            k = ring.pop(0)
            for tt in range(TT):
                for c in range(FT):
                    t = route_read[0] = pe.step(G, lambda e: e.matmul(
                        k.t[:, tt * 8:tt * 8 + n], xT[:, c, tt * P:(tt + 1) * P], gate_w[:, c, :],
                        start=c == 0, stop=c == FT - 1), ready + [k.free])
            src = k.t[:, 0:16].rearrange("p (t n) -> p t n", t=TT)[:, :, 0:n]
            if bias is None:
                t = dve.step(G, lambda e: e.tensor_copy(logits[:, :, 0:n], src), [t, padded])
            else:
                t = dve.step(G, lambda e: e.tensor_tensor(
                    logits[:, :, 0:n], src, bias[:, :].unsqueeze(1).broadcast_to([P, TT, n]), ALU.add), [t, padded])
            k.free = t
            ring.append(k)
            for tt in range(TT):
                t = dve.step(G, lambda e: e.max(top[:, tt, :], logits[:, tt, :]), [t])
            for tt in range(TT):
                t = dve.step(G, lambda e: e.max_index(top_i[:, tt, :], top[:, tt, :], logits[:, tt, :]), [t])
            t = dve.step(G, lambda e: e.tensor_copy(top_f[:, :, :], top_i[:, :, 0:2]), [t])
            t2 = dve.step(G, lambda e: e.tensor_tensor(wts[:, :, 0:1], top[:, :, 1:2], top[:, :, 0:1], ALU.subtract))
            t2 = act.step(G, lambda e: e.activation(wts[:, :, 1:2], wts[:, :, 0:1], ACT.Exp), [t2])
            t2 = dve.step(G, lambda e: e.tensor_scalar(wts[:, :, 2:3], wts[:, :, 1:2], 1.0, None, ALU.add), [t2])
            t2 = dve.step(G, lambda e: e.reciprocal(wts[:, :, 2:3], wts[:, :, 2:3]), [t2])
            t2 = dve.step(G, lambda e: e.tensor_tensor(wts[:, :, 3:4], wts[:, :, 1:2], wts[:, :, 2:3], ALU.mult), [t2])
            for tt in range(TT):
                dve.step(G, lambda e: e.tensor_scalar(comb[:, tt, :], iota[:, :], top_f[:, tt, 0:1], wts[:, tt, 2:3],
                                                      ALU.is_equal, ALU.mult), [t, t2])
                t3 = dve.step(G, lambda e: e.tensor_scalar(comb2[:, tt, :], iota[:, :], top_f[:, tt, 1:2], wts[:, tt, 3:4],
                                                           ALU.is_equal, ALU.mult), [])
            return dve.step(G, lambda e: e.tensor_tensor(comb[:, :, :], comb[:, :, :], comb2[:, :, :], ALU.add), [t3])

        def ffn0_stream():
            s = Stream("M")
            s.stats, s.routing = stats_of("M"), routing_of("M")
            x_sum = sb("x_sumM", [P, TT, D])
            combT = sb("combT", [8, T])
            hid = [sb(f"hid{i}", [P, FT, T]) for i in range(E0 + 1)]
            x_sum_read, hid_read = [None], [None]

            def run(b, ready, x, xT, y, yT, y_free):
                G = "f0"
                E = E0 + 1
                comb = s.routing[5]
                routed = route(s.routing, G, E0, xT, gate0, gbias, [ready, w_route])
                routed = dve.step(G, lambda e: e.memset(comb[:, :, E0:E], 1.0), [routed])
                yield ROUTE_LAG
                k = ring.pop(0)
                for tt in range(TT):
                    t = pe.step(G, lambda e: e.transpose(k.t[0:E, tt * P:(tt + 1) * P], comb[:, tt, :], ident[:, :]),
                                [routed, k.free])
                turned = dve.step(G, lambda e: e.tensor_copy(combT[:, :], k.t[0:E, 0:T]), [t])
                k.free = turned
                ring.append(k)
                hidden = {}

                def up(j):
                    k = ring.pop(0)
                    for f in range(FT):
                        for c in range(FT):
                            t = pe.step(G, lambda e: e.matmul(k.t[:, f * T:(f + 1) * T], w1_0[:, j, c, f * P:(f + 1) * P],
                                                              xT[:, c, :], start=c == 0, stop=c == FT - 1),
                                        [ready, w_ffn0[j], k.free])
                    for f in range(FT):
                        hidden[j] = act.step(G, lambda e: e.activation(hid[j][:, f, :], k.t[:, f * T:(f + 1) * T], ACT.Gelu,
                                                                       bias=b1_0[:, j, f:f + 1]),
                                             [t, hid_read[0]])
                    k.free = hidden[j]
                    ring.append(k)

                for j in range(E):
                    up(j)
                k = ring.pop(0)
                for tt in range(TT):
                    t = pe.step(G, lambda e: e.matmul(k.t[:, tt * D:(tt + 1) * D], combT[:, tt * P:(tt + 1) * P], b2_0[:, :],
                                                      start=True, stop=True), [turned, w_route, k.free])
                t = dve.step(G, lambda e: e.tensor_tensor(x_sum[:, :, :], halves(k), x[:, :, :], ALU.add), [t, ready] + x_sum_read)
                k.free = t
                ring.append(k)
                yield
                for j in range(E):
                    k = ring.pop(0)
                    for tt in range(TT):
                        for f in range(FT):
                            t2 = pe.step(G, lambda e: e.matmul(k.t[:, tt * D:(tt + 1) * D], hid[j][:, f, tt * P:(tt + 1) * P],
                                                               w2_0[:, j, f, :], start=f == 0, stop=f == FT - 1),
                                         [hidden[j], k.free])
                    if j < E - 1:
                        for tt in range(TT):
                            t = dve.step(G, lambda e: e.scalar_tensor_tensor(
                                x_sum[:, tt, :], k.t[:, tt * D:(tt + 1) * D], comb[:, tt, j:j + 1], x_sum[:, tt, :],
                                ALU.mult, ALU.add), [t2, t])
                        k.free = t
                        ring.append(k)
                    yield
                yield from layer_norm(s, k, x_sum[:, :, :], [t2, t], y, yT, y_free)
                x_sum_read[0] = s.normed[0]
                hid_read[0] = t2
                s.read = [s.normed[0], t2, turned]

            s.run = run
            return s

        def gqa_stream():
            s = Stream("G")
            s.stats = stats_of("G")
            soft = Softmax("G")
            nmax, sums, lse3, probs, probs_read = soft.nmax, soft.sums, soft.lse3, soft.probs, soft.probs_read
            proj = sb("projG", [P, FT, T])
            attT = sb("attTG", [P, FT, T])
            K4 = sb("K4", [P, GKV, T])
            VL = sb("VL", [P, TT, GKV * LAT])

            def run(b, x_ready, xT_ready, x, xT, y, yT, y_free):
                G = "g1"
                k, t = project(G, Wqk, xT, [xT_ready, fold_done[0]])
                q_ready = act.step(G, lambda e: e.activation(proj[:, :, :], halves(k), ACT.Copy, scale=GHD ** -0.5), [t])
                k.free = q_ready
                ring.append(k)
                k = ring.pop(0)
                for g in range(GKV):
                    for c in range(FT):
                        t = pe.step(G, lambda e: e.matmul(k.t[:, g * T:(g + 1) * T],
                                                          kdown4[:, c, g, :, :].rearrange("p r l -> p (r l)"), xT[:, c, :],
                                                          start=c == 0, stop=c == FT - 1), [xT_ready, kdown4_done, k.free])
                k_ready = act.step(G, lambda e: e.activation(K4[:, :, :], halves(k), ACT.Copy), [t])
                k.free = k_ready
                ring.append(k)
                k = ring.pop(0)
                W = GKV * LAT
                for tt in range(TT):
                    for c in range(FT):
                        t = pe.step(G, lambda e: e.matmul(k.t[:, tt * W:(tt + 1) * W], xT[:, c, tt * P:(tt + 1) * P], vdown[:, c, :],
                                                          start=c == 0, stop=c == FT - 1), [k.free])
                v_ready = act.step(G, lambda e: e.activation(
                    VL[:, :, :], k.t[:, 0:TT * W].rearrange("p (t n) -> p t n", t=TT), ACT.Copy), [t])
                k.free = v_ready
                ring.append(k)
                yield
                for h in range(GH):
                    r, g = 32 * (h % 4), h // 4
                    k = ring.pop(0)
                    for q, at, n in ((0, 0, P), (1, P, T)):
                        pe.step(G, lambda e: e.matmul(k.t[:, at:at + n], proj[r:r + LAT, g, q * P:(q + 1) * P], K4[r:r + LAT, g, 0:n],
                                                      start=True, stop=False), [q_ready, k_ready, k.free])
                        t = pe.step(G, lambda e: e.matmul(k.t[:, at + n - P:at + n], identb[:, :], causal[:, :], start=False, stop=True))
                    for q, at, n in ((0, 0, P), (1, P, T)):
                        t2 = dve.step(G, lambda e: e.tensor_reduce(nmax[:, q, h:h + 1], k.t[:, at:at + n], AX.X, ALU.max, negate=True), [t])
                    for q, at, n in ((0, 0, P), (1, P, T)):
                        t3 = act.step(G, lambda e: e.activation(k.t[:, at:at + n], k.t[:, at:at + n], ACT.Exp, bias=nmax[:, q, h:h + 1],
                                                                accum_out=sums[:, q, h:h + 1]), [t2])
                    k.free = t3
                    ring.append(k)
                    if h % 2:
                        yield
                lse_ready = yield from soft.finish(G, GH, t3)
                acc = ring.pop(0)
                ready = {}

                def score(h):
                    r, g = 32 * (h % 4), h // 4
                    k = ring.pop(0)
                    for c, at, q0 in ((0, 0, 0), (1, T, P)):
                        n = T - q0
                        pe.step(G, lambda e: e.matmul(k.t[:, at:at + n], K4[r:r + LAT, g, c * P:(c + 1) * P], proj[r:r + LAT, g, q0:T],
                                                      start=True, stop=False), [k.free])
                        pe.step(G, lambda e: e.matmul(k.t[:, at:at + P], identb[:, :], causalT[:, :], start=False, stop=False))
                        t = pe.step(G, lambda e: e.matmul(k.t[:, at:at + n], sel(h), lse3[:, q0:T], start=False, stop=True), [lse_ready])
                    flat = probs[h % 3][:, :, :].rearrange("p c t -> p (c t)")
                    ready[h] = act.step(G, lambda e: e.activation(flat[:, 0:T + P], k.t[:, 0:T + P], ACT.Exp), [t, probs_read.get(h % 3)])
                    k.free = ready[h]
                    ring.append(k)

                score(0)
                score(1)
                yield
                for h in range(GH):
                    r, g = 32 * (h % 4), h // 4
                    if h + 2 < GH:
                        score(h + 2)
                    flat = probs[h % 3][:, :, :].rearrange("p c t -> p (c t)")
                    pe.step(G, lambda e: e.matmul(acc.t[r:r + LAT, g * T:(g + 1) * T], VL[:, 0, g * LAT:(g + 1) * LAT], flat[:, 0:T],
                                                  start=True, stop=False), [ready[h], v_ready, acc.free])
                    t = pe.step(G, lambda e: e.matmul(acc.t[r:r + LAT, g * T + P:(g + 1) * T], VL[:, 1, g * LAT:(g + 1) * LAT],
                                                      flat[:, T:T + P], start=False, stop=True))
                    probs_read[h % 3] = t
                    yield
                t = act.step(G, lambda e: e.activation(attT[:, :, :], halves(acc), ACT.Copy), [t])
                acc.free = t
                ring.append(acc)
                k, t = project_tokens(G, Wvo, attT, [t])
                yield from layer_norm(s, k, x[:, :, :], [t, x_ready], y, yT, y_free)
                s.read = list(s.normed)

            s.run = run
            return s

        def keys_stream():
            s = Stream("K")
            packer = Packer("K", 2)
            ctxT = [sb(f"ctxT{i}", [P, FT, T]) for i in range(2)]
            V = sb("V", [P, TT, D])
            s.k_packed = [sb(f"k_packed{i}", [96, H, T], BF16) for i in range(2)]
            s.Vb = [sb(f"Vb{i}", [P, 2 * H, HD]) for i in range(2)]
            dma_ctx = Dma(sp, "ctxK", new_sem, 2)
            dma_v_store, dma_v_load = Dma(sp, "v_store", new_sem, 1), Dma(sp, "v_load", new_sem, 2)
            s.stores = [packer.store, dma_v_store]
            ctx_read, ctx_loaded, v_stored = {}, {}, [None]
            HT = T // H // 2

            def load(b):
                ctx_loaded[b] = dma_ctx.send([(ctxT[b % 2][:, :, :], rows_of(a["ctxT"][b]))], ctx_read.get(b - 2, []))

            def run(b, free):
                G = "kv"
                Vb = s.Vb[b % 2]
                ready = [w_xattn, ctx_loaded[b]]
                k, t = project_tokens(G, xw["1v"], ctxT[b % 2], ready)
                read = [t]
                t = dve.step(G, lambda e: e.tensor_tensor(V[:, :, :], halves(k), xw["1bv"][:, :].unsqueeze(1).broadcast_to([P, TT, D]),
                                                          ALU.add), [t, w_xattn, v_stored[0]])
                k.free = t
                ring.append(k)
                stored = v_stored[0] = dma_v_store.send([(scratch_v[b].rearrange("(t p) d -> p t d", p=P), V[:, :, :])], [t])
                v_ready = dma_v_load.send(
                    [(Vb[c * HT:(c + 1) * HT, :, :],
                      scratch_v[b].rearrange("(j t) (c e) -> c t j e", t=HT, e=HD)[c]) for c in range(H)], [stored] + free)
                yield 5
                loaded = yield from packer.pack(G, b, xw["1k"], xw["1bk"], 1.0, ctxT[b % 2], ready, PARTS_K)
                ctx_read[b] = read + [packer.stored]
                if b + 2 < BATCH:
                    load(b + 2)
                s.ready[b] = [packer.reorder(G, s.k_packed[b % 2], [loaded] + free), v_ready]
                yield

            s.ready = {}
            s.load, s.run = load, run
            return s

        def cross_stream(keys):
            s = Stream("X")
            s.stats = stats_of("X")
            soft = Softmax("X")
            nmax, sums, lse3, probs, probs_read = soft.nmax, soft.sums, soft.lse3, soft.probs, soft.probs_read
            packer = Packer("X", 3)
            q_packed = sb("q_packedX", [96, H, T], BF16)
            s.blk = sb("blkT", [P, H, T])
            blkT = s.blk[0:HD, :, :]
            attT = sb("attTX", [P, FT, T])
            x_sum = sb("x_sumX", [P, TT, D])
            dma_o_store, dma_o_load = Dma(sp, "o_store", new_sem, 1), Dma(sp, "o_load", new_sem, 1)
            s.stores = [packer.store, dma_o_store]
            BT = T // H
            HT = BT // 2

            def run(b, x_ready, xT_ready, x, xT, y, yT, y_free):
                G = "x1"
                x_read = []
                loaded = yield from packer.pack(G, b, xw["1q"], xw["1bq"], HD ** -0.5, xT, [xT_ready, w_xattn], PARTS_Q)
                x_read.append(packer.stored)
                ordered = packer.reorder(G, q_packed, [loaded, softmaxed[0]])
                while b not in keys.ready:
                    yield 5
                k_ready, v_ready = keys.ready[b]
                k_packed, Vb = keys.k_packed[b % 2], keys.Vb[b % 2]
                yield REORDER_LAG

                for h in range(H):
                    k = ring.pop(0)
                    for q, at, n in ((0, 0, P), (1, P, T)):
                        pe.step(G, lambda e: e.matmul(k.t[:, at:at + n], q_packed[:, h, q * P:(q + 1) * P], k_packed[:, h, 0:n],
                                                      start=True, stop=False), [ordered, k_ready, k.free])
                        t = pe.step(G, lambda e: e.matmul(k.t[:, at + n - P:at + n], identb[:, :], bcausal[:, :], start=False, stop=True))
                    for q, at, n in ((0, 0, P), (1, P, T)):
                        t2 = dve.step(G, lambda e: e.tensor_reduce(nmax[:, q, h:h + 1], k.t[:, at:at + n], AX.X, ALU.max, negate=True), [t])
                    for q, at, n in ((0, 0, P), (1, P, T)):
                        t3 = act.step(G, lambda e: e.activation(k.t[:, at:at + n], k.t[:, at:at + n], ACT.Exp, bias=nmax[:, q, h:h + 1],
                                                                accum_out=sums[:, q, h:h + 1]), [t2])
                    k.free = t3
                    ring.append(k)
                    yield
                lse_ready = yield from soft.finish(G, H, t3)
                ready = {}

                def score(h):
                    k = ring.pop(0)
                    for c, at, q0 in ((0, 0, 0), (1, T, P)):
                        n = T - q0
                        pe.step(G, lambda e: e.matmul(k.t[:, at:at + n], k_packed[:, h, c * P:(c + 1) * P], q_packed[:, h, q0:T],
                                                      start=True, stop=False), [k.free])
                        pe.step(G, lambda e: e.matmul(k.t[:, at:at + P], identb[:, :], bcausalT[:, :], start=False, stop=False))
                        t = pe.step(G, lambda e: e.matmul(k.t[:, at:at + n], sel(h), lse3[:, q0:T], start=False, stop=True), [lse_ready])
                    softmaxed[0] = t
                    flat = probs[h % 3][:, :, :].rearrange("p c t -> p (c t)")
                    ready[h] = act.step(G, lambda e: e.activation(flat[:, 0:T + P], k.t[:, 0:T + P], ACT.Exp), [t, probs_read.get(h % 3)])
                    k.free = ready[h]
                    ring.append(k)

                score(0)
                score(1)
                yield
                for h in range(H):
                    if h + 2 < H:
                        score(h + 2)
                    if h % 2 == 0:
                        acc = ring.pop(0)
                    at = (h % 2) * T
                    flat = probs[h % 3][:, :, :].rearrange("p c t -> p (c t)")
                    pe.step(G, lambda e: e.matmul(acc.t[0:HD, at:at + T], Vb[:, 2 * h, :], flat[:, 0:T], start=True, stop=False),
                            [ready[h], v_ready, acc.free])
                    t = pe.step(G, lambda e: e.matmul(acc.t[0:HD, at + P:at + T], Vb[:, 2 * h + 1, :], flat[:, T:T + P],
                                                      start=False, stop=True))
                    probs_read[h % 3] = t
                    if h % 2:
                        t = act.step(G, lambda e: e.activation(
                            s.blk[0:HD, :, (h - 1) * BT:(h + 1) * BT].rearrange("p c (i t) -> p c i t", t=HT),
                            acc.t[0:HD, :].rearrange("p (i c t) -> p c i t", c=H, t=HT), ACT.Copy), [t, o_stored[0]])
                        acc.free = t
                        ring.append(acc)
                    yield
                s.keys_read[b] = [probs_read[(H - 1) % 3]]
                stored = o_stored[0] = dma_o_store.send([(scratch_o[b].rearrange("(c e) t -> e c t", e=HD), blkT)], [t])
                t = dma_o_load.send([(attT[:, :, :], scratch_o[b].rearrange("(k p) t -> p k t", k=FT))], [stored, att_read[0]])
                biased = pool.step(G, lambda e: e.tensor_tensor(
                    x_sum[:, :, :], x[:, :, :], xw["1bo"][:, :].unsqueeze(1).broadcast_to([P, TT, D]), ALU.add),
                    [x_ready, w_xattn, x_sum_read[0]])
                yield O_LAG
                k, t = project_tokens(G, xw["1o"], attT, [t, w_xattn])
                att_read[0] = t
                s.read = [biased] + x_read
                yield from layer_norm(s, k, x_sum[:, :, :], [t, biased], y, yT, y_free)
                x_sum_read[0] = s.normed[0]

            softmaxed, x_sum_read, o_stored, att_read = [None], [None], [None], [None]
            s.keys_read = {}
            s.run = run
            return s

        mambas = [mamba_stream("A"), mamba_stream("B")]
        keys0 = keys_stream_0()
        first = cross_stream_0(keys0)
        x_loaded = {0: mambas[0].load(0, [])}
        w_mamba = dma_w["mamba"].send([l1, l2, l3, l4, l5, l6, l7, l8, l9])
        consts_raw = mambas[1].hs[0][:, :, :].rearrange("p d t -> p (d t)")[:, 0:5 * P + 32]
        consts_loaded = dma_w["fold"].send([(consts_raw, a["consts"])])
        x_loaded[1] = mambas[1].load(1, [])
        ctx_loaded = {0: keys0.load(0)}
        w_xattn = dma_w["x0"].send(xloads)
        consts_ready = dve.step("const", lambda e: e.tensor_copy(consts[:, :], consts_raw), [consts_loaded])
        for t, value in ((one, 1.0), (ones16, 1.0), (onesb, 1.0)):
            const = pool.step("const", lambda e: e.memset(t[:, :], value))
        A_exp = act.step("const", lambda e: e.activation(A[:, :, :], A[:, :, :], ACT.Exp), [w_mamba])
        A_neg = pool.step("const", lambda e: e.tensor_scalar(A[:, :, :], A[:, :, :], -1.0, None, ALU.mult), [A_exp])

        dma_x2 = Dma(sp, "x2_store", new_sem, 2)
        x2_stored, x2_out = {}, [None]

        def mamba_of(i):
            for b in range(i, BATCH, 2):
                yield from mambas[i].run(b, x_loaded[b], lambda: first.x1_read.get(b - 2) if b >= 2 else [])
                m_out[b] = mambas[i].out
                if b + 2 < BATCH:
                    x_loaded[b + 2] = mambas[i].load(b + 2, list(mambas[i].out))
                yield

        def keys_0():
            for b in range(BATCH):
                while b - 2 not in first.keys_read and b >= 2:
                    yield 5
                yield from keys0.run(b, ctx_loaded[b], first.keys_read.get(b - 2, []))
                if b + 1 < BATCH:
                    ctx_loaded[b + 1] = keys0.load(b + 1)

        def attention_0():
            for b in range(BATCH):
                while b not in m_out:
                    yield 5
                m = mambas[b % 2]
                yield from first.run(b, *m_out[b], m.x1, m.x1T, first.x2, first.x2T, [x2_out[0]])
                x2_stored[b] = x2_out[0] = dma_x2.send(
                    [(rows_of(scratch_x2[b]), first.x2[:, :, :]), (rows_of(scratch_x2T[b]), first.x2T[:, :, :])],
                    list(first.normed))
                yield

        m_out = {}
        by_clock([mamba_of(0), mamba_of(1), keys_0(), attention_0()], AHEAD_1, pe)

        phase_1_done = next_phase([dma_x2] + first.stores + keys0.stores)
        E = E0 + 1
        w1_0 = sb("w1_0", [P, E, FT, D])
        w2_0 = sb("w2_0", [P, E, FT, D])
        b1_0, f3 = weight("b1_0", [P, E, FT], a["b1_0"])
        b2_0, f4 = weight("b2_0", [E, D], a["b2_0"])
        gate0, f5 = weight("gate0", [P, FT, E0], k_rows(a["gate0T"], FT))
        gbias, f6 = weight("gbias", [P, E0], a["gbias"].partition_broadcast(P))
        xloads = attention_weights("1")
        kdown, g1 = weight("kdown", [P, FT, GKV * LAT], k_rows(a["wk_down"], FT))
        vdown, g2 = weight("vdown", [P, FT, GKV * LAT], k_rows(a["wv_down"], FT))
        kup, g3 = weight("kup", [P, LAT], a["wk_upT"])
        vup, g4 = weight("vup", [P, LAT], a["wv_upT"])
        kdown4 = sb("kdown4", [P, FT, GKV, 4, LAT])
        Wqk = sb("Wqk", [P, FT, GH * LAT])
        Wvo = sb("Wvo", [P, FT, D])
        pool.wait(phase_1_done)
        sp.wait(phase_1_done)
        for e in (pe, dve, act):
            e.wait(phase_1_done)
        x2 = [(sb(f"x2_{i}", [P, TT, D]), sb(f"x2T_{i}", [P, FT, T])) for i in range(2)]
        x3 = [(sb(f"x3_{i}", [P, TT, D]), sb(f"x3T_{i}", [P, FT, T])) for i in range(2)]
        x4 = [(sb(f"x4_{i}", [P, TT, D]), sb(f"x4T_{i}", [P, FT, T])) for i in range(2)]
        x5 = [(sb(f"y5_{i}", [P, TT, D]), sb(f"y5T_{i}", [P, FT, T])) for i in range(2)]
        ffn, gqa, keys = ffn0_stream(), gqa_stream(), keys_stream()
        cross = cross_stream(keys)
        dma_x2_load, dma_x5_store = Dma(sp, "x2_load", new_sem, 2), Dma(sp, "x5_store", new_sem, 2)
        w_route = dma_w["route"].send([f3, f4, f5, f6])
        x2_loaded, x3_ready, x4_ready, stored_5 = {}, {}, {}, {}
        x2_read, x3_read, x4_read = {}, {}, {}

        def load_x2(b):
            x, xT = x2[b % 2]
            x2_loaded[b] = dma_x2_load.send([(x[:, :, :], rows_of(scratch_x2[b])), (xT[:, :, :], rows_of(scratch_x2T[b]))],
                                            [x2_stored[b]] + x2_read.get(b - 2, []))

        load_x2(0)
        keys.load(0)
        w_gqa = dma_w["gqa"].send([g1, g2, g3, g4])
        w_ffn0 = [Dma(sp, f"expert0_{j}", new_sem, 1).send(
            [(w1_0[:, j, :, :], k_rows(a["w1_0"][j], FT)), (w2_0[:, j, :, :], k_rows(a["w2_0"][j], FT))]) for j in range(E)]
        w_xattn = dma_w["x1"].send(xloads)
        fold_in = cross.blk[:, :, :].rearrange("p h t -> p (h t)").rearrange("p (h n) -> p h n", h=GH)
        fold_loaded = dma_w["fold"].send([(fold_in[:, :, 0:D], a["wqT"].rearrange("(h p) n -> p h n", p=GHD)),
                                          (fold_in[:, :, D:2 * D], a["wo"].rearrange("(h p) n -> p h n", p=GHD))])
        fold_done = [None]

        for g in range(GKV):
            for r in range(4):
                kdown4_done = pool.step("const", lambda e: e.tensor_copy(
                    kdown4[:, :, g, r, :], kdown[:, :, g * LAT:(g + 1) * LAT]), [w_gqa])
        def fold():
            yield FOLD_LAG
            for h in range(GH):
                wq_wo = fold_in[:, h, :]
                k = ring.pop(0)
                for c in range(FT):
                    t = pe.step("fold", lambda e: e.matmul(k.t[:, c * LAT:(c + 1) * LAT], wq_wo[:, c * P:(c + 1) * P],
                                                           kup[:, :], start=True, stop=True), [fold_loaded, k.free, w_gqa])
                r = 32 * (h % 4)
                t = pe.step("fold", lambda e: e.matmul(k.t[r:r + LAT, D:2 * D], vup[:, :], wq_wo[:, D:2 * D],
                                                       start=True, stop=True))
                dve.step("fold", lambda e: e.tensor_copy(
                    Wqk[:, :, h * LAT:(h + 1) * LAT], k.t[:, 0:FT * LAT].rearrange("p (c l) -> p c l", c=FT)), [t])
                k.free = fold_done[0] = dve.step("fold", lambda e: e.tensor_copy(Wvo[r:r + LAT, h // 4, :], k.t[r:r + LAT, D:2 * D]))
                ring.append(k)
                yield 2

        def ffn_of_all():
            for b in range(BATCH):
                while b - 2 not in x3_read and b >= 2:
                    yield 5
                yield from ffn.run(b, x2_loaded[b], *x2[b % 2], *x3[b % 2], x3_read.get(b - 2, []))
                x3_ready[b], x2_read[b] = ffn.normed, ffn.read
                if b + 2 < BATCH:
                    load_x2(b + 2)
                yield

        def gqa_of_all():
            yield from fold()
            for b in range(BATCH):
                while b not in x3_ready or (b - 2 not in x4_read and b >= 2):
                    yield 5
                yield from gqa.run(b, *x3_ready[b], *x3[b % 2], *x4[b % 2], x4_read.get(b - 2, []))
                x4_ready[b], x3_read[b] = gqa.normed, gqa.read
                yield

        def keys_of_all():
            yield KEYS_LAG
            for b in range(BATCH):
                while b - 2 not in cross.keys_read and b >= 2:
                    yield 5
                yield from keys.run(b, cross.keys_read.get(b - 2, []))

        def cross_of_all():
            for b in range(BATCH):
                while b not in x4_ready:
                    yield 5
                yield from cross.run(b, *x4_ready[b], *x4[b % 2], *x5[b % 2], [stored_5.get(b - 2)])
                x4_read[b] = cross.read
                y, yT = x5[b % 2]
                stored_5[b] = dma_x5_store.send([(rows_of(scratch_x[b]), y[:, :, :]), (rows_of(scratch_xT[b]), yT[:, :, :])],
                                                list(cross.normed))
                yield

        load_x2(1)
        keys.load(1)
        by_clock([ffn_of_all(), gqa_of_all(), keys_of_all(), cross_of_all()], AHEAD_2, pe)

        phase_2_done = next_phase(keys.stores + cross.stores + [dma_x5_store])
        for e in (pe, dve, act, pool, sp):
            e.wait(phase_2_done)
        G = "f1"
        FH = HID1 // P
        x5 = [sb(f"x5_{i}", [P, TT, D]) for i in range(2)]
        x5T = [sb(f"x5T_{i}", [P, FT, T]) for i in range(2)]
        y6 = [sb(f"y6_{i}", [P, TT, D]) for i in range(2)]
        hid1 = [Split(sb, f"hid1_{i}", [P, FH, T]) for i in range(2)]
        gate1, gate1_load = weight("gate1", [P, FT, E1], k_rows(a["Wg"], FT), alloc=sb)
        w1_1 = Split(sb, "w1_1", [P, E1, FT, HID1])
        w2_1 = Split(sb, "w2_1", [P, E1, FH, D])
        w1_raw = sb("w1_raw", [P, 2, FT, HID1])
        w2_raw = sb("w2_raw", [P, 2, FH, D])
        xT_split = [Split(sb, f"x5T_split{i}", [P, FT, T]) for i in range(2)]
        s = Stream("F")
        s.stats, s.routing = stats_of("F"), [routing_of("F0"), routing_of("F1")]
        x_sum = sb("x_sumF", [P, TT, D])
        dma_out = Dma(sp, "out", new_sem, 2)
        dma_x5 = Dma(sp, "x5", new_sem, 2)

        def load_x5(b, after):
            return dma_x5.send([(x5[b % 2][:, :, :], scratch_x[b].rearrange("(t p) d -> p t d", p=P)),
                                (x5T[b % 2][:, :, :], scratch_xT[b].rearrange("(k p) t -> p k t", p=P))], after)

        x5_loaded = [load_x5(0, [])]
        gate_loaded = Dma(sp, "gate1", new_sem, 1).send([gate1_load])
        dma_expert = [Dma(sp, f"expert{j}", new_sem, 1) for j in range(2)]
        w_loaded, split_of = {}, {}

        def load_expert(j):
            w_loaded[j] = dma_expert[j % 2].send([(w1_raw[:, j % 2, :, :], k_rows(a["W1"][j], FT)), (w2_raw[:, j % 2, :, :], k_rows(a["W2"][j], FH))],
            [split_of.get(j - 2)])

        load_expert(0)
        load_expert(1)
        x5_loaded.append(load_x5(1, []))
        hidden, hid_free, y_sent, up_read = {}, {}, {}, {}

        def w_split(j):
            if j not in split_of:
                w1_1.divide(act, pool, G, (slice(None), j), w1_raw[:, j % 2, :, :], [w_loaded[j]])
                split_of[j] = w2_1.divide(dve, pool, G, (slice(None), j), w2_raw[:, j % 2, :, :], [w_loaded[j]])
                if j + 2 < E1:
                    load_expert(j + 2)
            return split_of[j]

        prepared = {}

        def prepare(b):
            loaded = x5_loaded[b]
            ready = xT_split[b % 2].divide(dve, pool, G, (slice(None),) * 3, x5T[b % 2][:, :, :], [loaded, up_read.get(b - 2)])
            routed = route(s.routing[b % 2], G, E1, x5T[b % 2], gate1, None, [loaded, gate_loaded])
            prepared[b] = routed, ready, [ready, route_read[0]]

        def up(b, j):
            xT, ready = xT_split[b % 2], prepared[b][1]
            for m in range(FH // 2):
                k = ring.pop(0)
                for i in range(2):
                    f = 2 * m + i
                    for c in range(FT):
                        t = split_matmul(G, k.t[:, i * T:(i + 1) * T], w1_1, (slice(None), j, c, slice(f * P, (f + 1) * P)),
                                         xT, (slice(None), c, slice(None)), c == 0, c == FT - 1,
                                         [ready, w_split(j), k.free])
                h, at = hid1[j % 2], slice(2 * m, 2 * m + 2)
                upper = act.step(G, lambda e: e.activation(h.hi[:, at, :], halves(k), ACT.Relu),
                                 [t, hid_free.get(j % 2)])
                hidden[j] = dve.step(G, lambda e: e.scalar_tensor_tensor(
                    h.lo[:, at, :], halves(k), 0.0, h.hi[:, at, :].bitcast(FP32), ALU.max, ALU.subtract), [upper])
                k.free = hidden[j]
                ring.append(k)

        prepare(0)
        up(0, 0)
        for b in range(BATCH):
            x, xT, y, loaded, comb = x5[b % 2], xT_split[b % 2], y6[b % 2], x5_loaded[b], s.routing[b % 2][5]
            routed, ready, x5T_read = prepared[b]

            t = None
            for j in range(E1):
                if j == E1 // 2 and b + 1 < BATCH:
                    prepare(b + 1)
                if j + 1 < E1:
                    up(b, j + 1)
                elif b + 1 < BATCH:
                    up(b + 1, 0)
                k = ring.pop(0)
                for tt in range(TT):
                    for f in range(FH):
                        t2 = split_matmul(G, k.t[:, tt * D:(tt + 1) * D], hid1[j % 2], (slice(None), f, slice(tt * P, (tt + 1) * P)),
                                          w2_1, (slice(None), j, f, slice(None)), f == 0, f == FH - 1,
                                          [hidden[j], k.free])
                hid_free[j % 2] = t2
                src = x if j == 0 else x_sum
                for tt in range(TT):
                    t = dve.step(G, lambda e: e.scalar_tensor_tensor(
                        x_sum[:, tt, :], k.t[:, tt * D:(tt + 1) * D], comb[:, tt, j:j + 1], src[:, tt, :],
                        ALU.mult, ALU.add), [t2, t, routed, loaded])
                k.free = t
                ring.append(k)
            if b + 2 < BATCH:
                x5_loaded.append(load_x5(b + 2, [t] + x5T_read))
            up_read[b] = t2
            st, mv, rstd = s.stats
            for tt in range(TT):
                t = dve.step(G, lambda e: e.bn_stats(st[:, tt, :], x_sum[:, tt, :]), [t])
            for tt in range(TT):
                t = dve.step(G, lambda e: e.bn_aggr(mv[:, tt, :], st[:, tt, :]), [t])
            t2 = dve.step(G, lambda e: e.tensor_scalar(rstd[:, :], mv[:, :, 1], EPS, None, ALU.add), [t])
            t2 = pool.step(G, lambda e: e.tensor_tensor(rstd[:, :], rstd[:, :], root[:, :], ALU.pow), [t2])
            for tt in range(TT):
                t = dve.step(G, lambda e: e.tensor_scalar(y[:, tt, :], x_sum[:, tt, :], mv[:, tt, 0:1], rstd[:, tt:tt + 1],
                                                          ALU.subtract, ALU.mult), [t2, t, y_sent.get(b % 2)])
            y_sent[b % 2] = dma_out.send([(out[b].rearrange("(t p) d -> p t d", p=P), y[:, :, :])], [t])
        sp.wait(dma_out.all_sent())
        phase[0].close()


def order_ct(n_tokens):
    return (16 * np.arange(n_tokens)[None, :] + np.arange(16)[:, None]).reshape(-1)


def constants():
    below = lambda rows, cols: np.where(cols[None, :] > rows[:, None], HIDE, 0.0).astype(np.float32)
    n = np.arange(P)
    block = order_ct(8)
    sel = np.zeros((P, 32), np.float32)
    sel[:96] = np.tile(np.eye(32), (3, 1))
    head_block = np.zeros((H, D), np.float32)
    for h in range(H):
        head_block[h, h * HD:(h + 1) * HD] = 1
    return {
        "ident": np.eye(P, dtype=np.float32), "head_block": head_block,
        "iota": np.tile(np.arange(8, dtype=np.float32), (P, 1)),
        "consts": np.concatenate([np.eye(P, dtype=np.float32), below(n, n), below(n, n).T,
                                  below(block, block), below(block, block).T, sel], 1),
    }


def kernel(**inputs):
    import numpy as _np
    import concourse.bacc as _bacc
    from concourse import mybir as _mybir
    from concourse.bass_utils import run_bass_kernel_spmd as _run

    i = {k: _np.asarray(v) for k, v in inputs.items()}
    m, c, e, r = "L0_attn_", "L0_xattn_", "L0_ffn_", "L1_attn_"
    xp = i[m + "xproj_w"].T
    host = {
        "x": i["x"], "xT": i["x"].transpose(0, 2, 1), "ctxT": i["ctx_1024"].transpose(0, 2, 1),
        "mask": i["mask_BxSxS2_if1"], "maskT": i["mask_BxSxS2_if1"].transpose(0, 2, 1),
        "in_wT": i[m + "in_w"].T, "conv_w": i[m + "conv_w"][:, 0, :], "conv_b": i[m + "conv_b"],
        "xprojT": _np.concatenate([xp[:, RANK:], xp[:, :RANK]], 1), "dt_wT": i[m + "dt_w"].T, "dt_b": i[m + "dt_b"],
        "A_log": i[m + "A_log"], "D": i[m + "D"], "out_wT": i[m + "out_w"].T,
        "w1_0": _np.concatenate([i[e + "rw1"], i[e + "sw1"][None]]), "b1_0": _np.concatenate([i[e + "rb1"], i[e + "sb1"][None]]),
        "w2_0": _np.concatenate([i[e + "rw2"], i[e + "sw2"][None]]), "b2_0": _np.concatenate([i[e + "rb2"], i[e + "sb2"][None]]),
        "gate0T": i[e + "gate_w"].T, "gbias": i[e + "expert_bias"],
        "wqT": i[r + "wq"].T, "wk_down": i[r + "wk_down"], "wv_down": i[r + "wv_down"],
        "wk_upT": i[r + "wk_up"].T, "wv_upT": i[r + "wv_up"].T, "wo": i[r + "wo"],
        "Wg": i["L1_ffn_Wg"], "W1": i["L1_ffn_W1"], "W2": i["L1_ffn_W2"],
    }
    for layer, last in (("0", "o"), ("1", "p")):
        for part in "qkvo":
            n = last if part == "o" else part
            host[f"W{part}{layer}T"] = i[f"L{layer}_xattn_W{n}"].T
            host[f"b{part}{layer}"] = i[f"L{layer}_xattn_b{n}"]
    cols = lambda v: v.reshape(*v.shape[:-1], -1, P)
    for name in ("conv_b", "dt_b", "D", "bq0", "bk0", "bq1", "bk1"):
        host[name] = cols(host[name]).T
    host["b1_0"] = cols(host["b1_0"]).transpose(2, 0, 1)
    host.update(constants())
    nc = _bacc.Bacc("TRN2", target_bir_lowering=False, num_devices=1)
    arrays, aps = {}, {}
    for name, v in host.items():
        v = _np.ascontiguousarray(v)
        arrays["in_" + name] = v
        aps[name] = nc.dram_tensor("in_" + name, v.shape, _mybir.dt.from_np(v.dtype), kind="ExternalInput").ap()
    out = nc.dram_tensor("out_0", (BATCH, T, D), FP32, kind="ExternalOutput").ap()
    scratch_q = nc.dram_tensor("scratch_q", (BATCH, 4, 3, D, T), BF16, kind="Internal").ap()
    scratch_o = nc.dram_tensor("scratch_o", (BATCH, D, T), FP32, kind="Internal").ap()
    scratch_v = nc.dram_tensor("scratch_v", (BATCH, T, D), FP32, kind="Internal").ap()
    scratch_x = nc.dram_tensor("scratch_x", (BATCH, T, D), FP32, kind="Internal").ap()
    scratch_xT = nc.dram_tensor("scratch_xT", (BATCH, D, T), FP32, kind="Internal").ap()
    scratch_x2 = nc.dram_tensor("scratch_x2", (BATCH, T, D), FP32, kind="Internal").ap()
    scratch_x2T = nc.dram_tensor("scratch_x2T", (BATCH, D, T), FP32, kind="Internal").ap()
    program(nc, aps, out, scratch_q, scratch_o, scratch_v, scratch_x2, scratch_x2T, scratch_x, scratch_xT)
    got = _run(nc, [arrays], core_ids=[0])
    return got.results[0]["out_0"]
```
